# Optimizing a Trainium2 kernel written in Bass

```python
import numpy as np
import jax
import jax.numpy as jnp

def _softmax(x, axis=-1):
    return jax.nn.softmax(x, axis=axis)

def _gelu(x):
    return jax.nn.gelu(x, approximate=True)

def _silu(x):
    return jax.nn.silu(x)

def _sigmoid(x):
    return jax.nn.sigmoid(x)

def _layernorm(x, axis=-1, eps=1e-05):
    m = jnp.mean(x, axis=axis, keepdims=True)
    v = jnp.var(x, axis=axis, keepdims=True)
    return (x - m) / jnp.sqrt(v + eps)

def _scatter_add(tgt, idx, src, axis=0):
    return tgt.at[idx].add(src)

def _segment_sum(src, seg, n):
    return jax.ops.segment_sum(src, seg, n)
kernel_name = 'mk_gnn_ffn_d1_gnn_r32_bc5180'

def setup_inputs(seed: int=0):
    np.random.seed(seed)
    _w = jnp.asarray

    def _rec_inputs():
        import jax
        import jax.numpy as jnp
        _gk = jax.random.key(seed)
        x = -0.0003713 + 1 * jax.random.normal(jax.random.fold_in(_gk, 1), (3125, 256), jnp.float32)
        src = jax.random.randint(jax.random.fold_in(_gk, 2), (50000,), 0, 3125, jnp.int32)
        dst = jax.random.randint(jax.random.fold_in(_gk, 3), (50000,), 0, 3125, jnp.int32)
        _o = jnp.argsort(dst, stable=True)
        src = src[_o]
        dst = dst[_o]
        return (x, src, dst)
    x, src, dst = _rec_inputs()

    def _L0_gnn_setup():
        import jax, jax.numpy as jnp
        import numpy as np
        EPS = 1e-05
        key = jax.random.key(seed)
        k1, k2, k3 = jax.random.split(key, 3)
        N, E, D = (50000, 25000, 256)
        x = jax.random.normal(k1, (N, D), dtype=jnp.float32)
        edge_index = jax.random.randint(k2, (2, E), 0, N, dtype=jnp.int64)
        W = jax.random.normal(k3, (D, D), dtype=jnp.float32) * (1.0 / np.sqrt(D))
        bias = jnp.zeros((D,), dtype=jnp.float32)
        gamma = jnp.ones((D,), dtype=jnp.float32)
        beta = jnp.zeros((D,), dtype=jnp.float32)
        return {'x': x, 'edge_index': edge_index, 'W': W, 'bias': bias, 'gamma': gamma, 'beta': beta}
    _L0_gnn_all = _L0_gnn_setup()
    _L0_gnn_in = {k: v for k, v in _L0_gnn_all.items() if k in ('W', 'bias', 'gamma', 'beta')}
    del _L0_gnn_all

    def _L0_ffn_setup():
        import jax, jax.numpy as jnp
        import numpy as np
        E, D, H, TOP_K = (6, 256, 256, 2)
        ROUTER_H = D // 2
        key = jax.random.key(seed)
        ks = jax.random.split(key, 12)
        s = 1.0 / np.sqrt(D)
        sh = 1.0 / np.sqrt(H)
        sr = 1.0 / np.sqrt(ROUTER_H)
        return {'features': jax.random.normal(ks[0], (8, 128, D), dtype=jnp.float32), 'router_w1': jax.random.uniform(ks[1], (D, ROUTER_H), jnp.float32, -s, s), 'router_b1': jnp.zeros((ROUTER_H,), jnp.float32), 'router_w2': jax.random.uniform(ks[2], (ROUTER_H, E), jnp.float32, -sr, sr), 'router_b2': jnp.zeros((E,), jnp.float32), 'expert_w1': jax.random.uniform(ks[3], (E, D, H), jnp.float32, -s, s), 'expert_b1': jnp.zeros((E, H), jnp.float32), 'expert_w2': jax.random.uniform(ks[4], (E, H, H), jnp.float32, -sh, sh), 'expert_b2': jnp.zeros((E, H), jnp.float32), 'expert_w3': jax.random.uniform(ks[5], (E, H, D), jnp.float32, -sh, sh), 'expert_b3': jnp.zeros((E, D), jnp.float32)}
    _L0_ffn_all = _L0_ffn_setup()
    _L0_ffn_in = {k: v for k, v in _L0_ffn_all.items() if k in ('router_w1', 'router_b1', 'router_w2', 'router_b2', 'expert_w1', 'expert_b1', 'expert_w2', 'expert_b2', 'expert_w3', 'expert_b3')}
    del _L0_ffn_all
    return {'x': x, 'src': src, 'dst': dst, 'L0_gnn_W': _L0_gnn_in['W'], 'L0_gnn_bias': _L0_gnn_in['bias'], 'L0_gnn_gamma': _L0_gnn_in['gamma'], 'L0_gnn_beta': _L0_gnn_in['beta'], 'L0_ffn_router_w1': _L0_ffn_in['router_w1'], 'L0_ffn_router_b1': _L0_ffn_in['router_b1'], 'L0_ffn_router_w2': _L0_ffn_in['router_w2'], 'L0_ffn_router_b2': _L0_ffn_in['router_b2'], 'L0_ffn_expert_w1': _L0_ffn_in['expert_w1'], 'L0_ffn_expert_b1': _L0_ffn_in['expert_b1'], 'L0_ffn_expert_w2': _L0_ffn_in['expert_w2'], 'L0_ffn_expert_b2': _L0_ffn_in['expert_b2'], 'L0_ffn_expert_w3': _L0_ffn_in['expert_w3'], 'L0_ffn_expert_b3': _L0_ffn_in['expert_b3']}

def reference(x, src, dst, L0_gnn_W, L0_gnn_bias, L0_gnn_gamma, L0_gnn_beta, L0_ffn_router_w1, L0_ffn_router_b1, L0_ffn_router_w2, L0_ffn_router_b2, L0_ffn_expert_w1, L0_ffn_expert_b1, L0_ffn_expert_w2, L0_ffn_expert_b2, L0_ffn_expert_w3, L0_ffn_expert_b3):
    import jax
    import jax.numpy as jnp

    def _L0_gnn_ref(x, edge_index, W, bias, gamma, beta):
        import jax, jax.numpy as jnp
        import numpy as np
        EPS = 1e-05
        N = x.shape[0]
        loop = jnp.arange(N, dtype=edge_index.dtype)
        src = jnp.concatenate([edge_index[0], loop])
        dst = jnp.concatenate([edge_index[1], loop])
        deg = jax.ops.segment_sum(jnp.ones_like(dst, dtype=x.dtype), dst, num_segments=N)
        dinv = jnp.where(deg > 0, jax.lax.rsqrt(jnp.maximum(deg, 1.0)), 0.0)
        norm = dinv[src] * dinv[dst]
        h = x @ W
        msg = h[src] * norm[:, None]
        agg = jax.ops.segment_sum(msg, dst, num_segments=N) + bias
        mean = jnp.mean(agg, axis=0)
        var = jnp.mean(jnp.square(agg - mean), axis=0)
        y = (agg - mean) * jax.lax.rsqrt(var + EPS) * gamma + beta
        y = jax.nn.relu(y)
        return y + x

    def _L0_ffn_ref(features, router_w1, router_b1, router_w2, router_b2, expert_w1, expert_b1, expert_w2, expert_b2, expert_w3, expert_b3):
        import jax, jax.numpy as jnp
        import numpy as np
        E, D, H, TOP_K = (6, 256, 256, 2)
        ROUTER_H = D // 2
        rh = jax.nn.relu(features @ router_w1 + router_b1)
        expert_logits = jax.nn.softmax(rh @ router_w2 + router_b2, axis=-1)
        top_w, top_i = jax.lax.top_k(expert_logits, TOP_K)
        routing_weights = jax.nn.softmax(top_w, axis=-1)
        h1 = jax.nn.relu(jnp.einsum('bsd,edh->bseh', features, expert_w1) + expert_b1)
        h2 = jax.nn.relu(jnp.einsum('bseh,ehf->bsef', h1, expert_w2) + expert_b2)
        expert_out = jnp.einsum('bsef,efo->bseo', h2, expert_w3) + expert_b3
        sel = jnp.take_along_axis(expert_out, top_i[:, :, :, None], axis=2)
        combined = jnp.sum(sel * routing_weights[..., None], axis=2)
        return combined
    edge_index = jnp.stack([src, dst])
    x = x + _L0_gnn_ref(_layernorm(x, axis=-1), edge_index, L0_gnn_W, L0_gnn_bias, L0_gnn_gamma, L0_gnn_beta)
    x = x + _L0_ffn_ref(_layernorm(x, axis=-1)[None], L0_ffn_router_w1, L0_ffn_router_b1, L0_ffn_router_w2, L0_ffn_router_b2, L0_ffn_expert_w1, L0_ffn_expert_b1, L0_ffn_expert_w2, L0_ffn_expert_b2, L0_ffn_expert_w3, L0_ffn_expert_b3)[0]
    return x

_drawn_inputs = setup_inputs


def setup_inputs(seed=0):
    import zlib

    import numpy as np

    out = dict(_drawn_inputs(seed))
    spreads = {'L0_gnn_bias': (0.0, 0.8),
     'L0_gnn_gamma': (1.0, 0.2),
     'L0_gnn_beta': (0.0, 0.1),
     'L0_ffn_router_b1': (0.0, 0.462),
     'L0_ffn_router_b2': (0.0, 0.296),
     'L0_ffn_expert_b1': (0.0, 0.8),
     'L0_ffn_expert_b2': (0.0, 0.607),
     'L0_ffn_expert_b3': (0.0, 0.1)}
    factors = {}
    for name, (base, spread) in spreads.items():
        noise = np.random.default_rng([zlib.crc32(name.encode()), seed]).standard_normal(out[name].shape)
        drawn = base * np.exp(spread * noise) if base else spread * noise
        out[name] = jnp.asarray(drawn.astype(out[name].dtype))
    for name, factor in factors.items():
        out[name] = (out[name] * factor).astype(out[name].dtype)
    return out
```

```python
import concourse.bass as bass
from concourse import mybir
from contextlib import ExitStack

fp32 = mybir.dt.float32
fp16 = mybir.dt.float16
f32r = mybir.dt.float32r
i32 = mybir.dt.int32
ALU = mybir.AluOpType
ACT = mybir.ActivationFunctionType
AX = mybir.AxisListType

N, D, E = 3125, 256, 50000
P = 128
NT = -(-N // P)
FULL = N // P
LAST = N - FULL * P
DH = D // P
EP, EC = 125, 400
WIN = 16
KCH = 3
CAP = KCH * P
CNT = NT * WIN
GW = 32
GN = GW * WIN
NG = N // GN
TAILW = -(-(N - NG * GN) // WIN)
TAILN = TAILW * WIN
NPAD = NG * GN + TAILN
BK = 16
OHR = 4
HR = 16
NEXP, H, RH = 6, 256, 128
EPS = 1e-5
XSCALE = 256.0


def build(nc, x, src, dst, W, bias, gamma, beta, rw1, rb1, rw2, rb2, w1, b1, w2, b2, w3, b3, out):
    ctx, ctx1, ctx2 = ExitStack(), ExitStack(), ExitStack()
    with ctx:
        def sb(name, shape, dt, scope=ctx):
            return scope.enter_context(nc.sbuf_tensor(name, shape, dt))

        def ps(name, shape, scope=ctx, dt=fp32):
            return scope.enter_context(nc.psum_tensor(name, shape, dt))

        def sem(name):
            return ctx.enter_context(nc.semaphore(name))

        keys_d = nc.dram_tensor("keys_d", [(E + CAP) * 2], fp32, kind="Internal").ap()
        starts_d = nc.dram_tensor("starts_d", [NT * 8], i32, kind="Internal").ap()
        xs_d = nc.dram_tensor("xs_d", [NT * P, D], fp32, kind="Internal").ap()

        xx = sb("xx", [P, NT, D], fp32)
        agg = sb("agg", [P, NT * D], fp32)
        xn = agg[:, :].rearrange("p (t d) -> p t d", t=NT)
        stats = sb("stats", [P, DH, NG + 1, 6], fp32)
        identf = sb("identf", [P, P], fp32)
        eps1 = sb("eps1", [P, 1], fp32)

        C = sb("C", [P, 2, NT, GN], fp16, ctx1)
        xs = sb("xs", [P, 2, NT, D], fp16, ctx1)
        oh_src = sb("oh_src", [P, OHR, KCH, P], fp16, ctx1)
        oh_key = sb("oh_key", [P, OHR, KCH, CNT], fp16, ctx1)
        ekeys = sb("ekeys", [P, 2, BK, KCH, 2], fp32, ctx1)
        wkeys = sb("wkeys", [P, 2, BK, KCH], fp32, ctx1)
        dinvb = sb("dinvb", [P, NT * P], fp32, ctx1)
        zbuf = sb("zbuf", [P, DH, GN], fp32, ctx1)
        ubuf = sb("ubuf", [P, DH, GN], fp32, ctx1)
        wgcn = sb("wgcn", [P, DH, D], fp32, ctx1)
        biasT = sb("biasT", [P, DH], fp32, ctx1)
        iota_i = sb("iota_i", [P, GN], i32, ctx1)
        iota_h = sb("iota_h", [P, CNT], fp16, ctx1)
        win_i = sb("win_i", [P, NG * GW + TAILW], i32, ctx1)
        win_off = sb("win_off", [P, NG * GW + TAILW], fp32, ctx1)
        diff_i = sb("diff_i", [P, P], i32, ctx1)
        mask_i = sb("mask_i", [P, 9], i32, ctx1)
        ident16 = sb("ident16", [P, P], fp16, ctx1)
        below = sb("below", [P, 9], fp32, ctx1)
        upper = sb("upper", [NT, NT], fp32, ctx1)
        ones = sb("ones", [P, P], fp32, ctx1)
        srci = sb("srci", [EP, EC], i32, ctx1)
        dsti = sb("dsti", [EP, EC], i32, ctx1)
        nexti = sb("nexti", [EP, EC], i32, ctx1)
        ti = sb("ti", [EP, 4, EC], i32, ctx1)
        dstlo = sb("dstlo", [EP, EC], fp32, ctx1)
        dsthi = sb("dsthi", [EP, EC], fp32, ctx1)
        pack = sb("pack", [EP, EC, 2], fp32, ctx1)
        padk = sb("padk", [P, 6], fp32, ctx1)
        desc = sb("desc", [EP, EC], fp32, ctx1)
        descs = sb("descs", [EP, 1], fp32, ctx1)
        mv = sb("mv", [P, NT, 2], fp32, ctx1)
        st6 = sb("st6", [P, NT, 6], fp32, ctx1)
        rstd = sb("rstd", [P, NT], fp32, ctx1)
        deg = sb("deg", [P, NT], fp32, ctx1)
        dinv = sb("dinv", [P, NT], fp32, ctx1)
        dinvs = sb("dinvs", [P, NT], fp32, ctx1)
        cum = sb("cum", [NT, 9], fp32, ctx1)
        over = sb("over", [NT, 8], fp32, ctx1)
        overs = sb("overs", [NT, 1], fp32, ctx1)
        starti = sb("starti", [NT, 8], i32, ctx1)
        row = sb("row", [1, NT * 8], i32, ctx1)
        flag = sb("flag", [1, 1], i32, ctx1)
        degr = sb("degr", [P, NT], fp32, ctx1)
        dinvz = sb("dinvz", [P, NT], fp32, ctx1)
        dstf = sb("dstf", [EP, EC], fp32, ctx1)
        goff_i = sb("goff_i", [P, NG + 1], i32, ctx1)
        gkey = sb("gkey", [EP, 1], fp32, ctx1)
        gidx = sb("gidx", [EP, 1], i32, ctx1)
        diag4 = C[:, 1, :, :].rearrange("p a b -> p (a b)").bitcast(fp32)[:, 0:(NG + 1) * GN].rearrange("p (g n) -> p g n", n=GN)
        gen_oh = C[0:EP, 0, :, :].rearrange("p a b -> p (a b)").bitcast(fp32)[:, 0:GN]
        gen_xs = C[:, 1, :, :].rearrange("p a b -> p (a b)").bitcast(fp32)
        gen_rows = ubuf[0:EP, 0, 0:D]
        hist_lo = C[0:EP, 0, 0:4, :].rearrange("p a b -> p (a b)").rearrange("p (r n) -> p r n", n=P)
        hist_hi = C[0:EP, 1, :, :].rearrange("p a b -> p (a b)")[:, 0:EC * NT].rearrange("p (c n) -> p c n", n=NT)

        psC = [ps(f"psC{i}", [P, 512], ctx1) for i in range(4)]
        psZ = [ps(f"psZ{i}", [P, 512], ctx1) for i in range(2)]
        psY = [ps(f"psY{i}", [P, 512], ctx1) for i in range(2)]

        s_edge, s_x, s_wt, s_cst = sem("edges_loaded"), sem("x_loaded"), sem("weights_loaded"), sem("constants_ready")
        s_dve = sem("dve_step")
        s_packed, s_keys = sem("keys_packed"), sem("keys_in_dram")
        s_hoh, s_hmm = sem("degree_onehots_ready"), sem("degree_chunks_done")
        s_deg, s_cum, s_pref, s_flagmm = sem("deg_ready"), sem("cum_done"), sem("prefix_done"), sem("flag_done")
        s_cumsb, s_start, s_sd, s_row = sem("cum_in_sbuf"), sem("starts_ready"), sem("starts_in_dram"), sem("row_loaded")
        s_flag = sem("flag_ready")
        s_var, s_std, s_rstd, s_xn, s_sqd = sem("var_ready"), sem("std_ready"), sem("rstd_ready"), sem("xn_ready"), sem("sqrt_deg_ready")
        s_pool = sem("pool_step")
        s_dinv, s_xhi, s_xs = sem("dinv_ready"), sem("xs_hi_ready"), sem("xs_ready")
        s_diag, s_dbmm, s_dinvb = sem("diag_ready"), sem("dinv_row_done"), sem("dinv_row_ready")
        s_turn = sem("key_loads_turn")
        s_ek = [sem(f"edge_keys_loaded{i}") for i in range(2)]
        s_wk = sem("window_keys_ready")
        s_oh, s_cnt, s_cev = sem("onehots_ready"), sem("counts_done"), sem("counts_evicted")
        s_z, s_zev, s_y, s_yev, s_agg = sem("z_done"), sem("z_evicted"), sem("y_done"), sem("y_evicted"), sem("agg_ready")
        s_stat = sem("stats_ready")
        g_zero, g_xst, g_xsd = sem("gen_z_zeroed"), sem("gen_xs_staged"), sem("gen_xs_in_dram")
        g_row, g_oh, g_mm, g_add, g_y, g_u, g_idx, g_idx2 = (sem("gen_rows_gathered"), sem("gen_onehot_ready"), sem("gen_product_done"),
                                              sem("gen_z_added"), sem("gen_y_done"), sem("gen_u_ready"), sem("gen_index_ready"), sem("gen_key_ready"))

        g_turn = sem("gen_turn")
        windows = NG * GW + TAILW

        def parity(g):
            return g % 2 if isinstance(g, int) else bass.ds(g % 2, 1)

        def agg_at(g, m, cols):
            return agg[:, bass.ds(GN * g + m * NPAD, cols)]

        block = ctx1.enter_context(nc.Block())

        @block.sync
        def _(sp):
            sp.dma_start(srci[:], src.rearrange("(p c) -> p c", p=EP)).then_inc(s_edge, 16)
            sp.dma_start(dsti[:], dst.rearrange("(p c) -> p c", p=EP)).then_inc(s_edge, 16)
            sp.dma_start(nexti[0:EP - 1, :], dst[1:1 + (EP - 1) * EC].rearrange("(p c) -> p c", p=EP - 1)).then_inc(s_edge, 16)
            sp.dma_start(nexti[EP - 1:EP, 0:EC - 1], dst[1 + (EP - 1) * EC:E].rearrange("(p c) -> p c", p=1)).then_inc(s_edge, 16)
            sp.dma_start(nexti[EP - 1:EP, EC - 1:EC], dst[E - 1:E].rearrange("(p c) -> p c", p=1)).then_inc(s_edge, 16)
            sp.dma_start(wgcn[:], W.rearrange("(k p) n -> p k n", p=P)).then_inc(s_wt, 16)
            with nc.allow_non_contiguous_dma(reason="bias, one value per partition"):
                sp.dma_start(biasT[:], bias.rearrange("(k p) -> p k", p=P)).then_inc(s_wt, 16)
            sp.wait_ge(s_packed, 2)
            sp.dma_start(keys_d[0:2 * E].rearrange("(p c) -> p c", p=EP), pack[:].rearrange("p c k -> p (c k)")).then_inc(s_keys, 16)
            sp.dma_start(keys_d[2 * E:2 * (E + CAP)].rearrange("(p c) -> p c", p=P), padk[:]).then_inc(s_keys, 16)
            sp.wait_ge(s_start, 1)
            sp.dma_start(starts_d.rearrange("(p c) -> p c", p=NT), starti[:]).then_inc(s_sd, 16)
            sp.wait_ge(s_sd, 16)
            sp.dma_start(row[:], starts_d.rearrange("(p c) -> p c", p=1)).then_inc(s_row, 16)
            sp.wait_ge(s_keys, 32)
            sp.wait_ge(s_row, 16)

            def load_keys(first, count, slot):
                with sp.Fori(0, count) as w:
                    at = sp.value_load(row[0:1, bass.ds(first + w, 1)], min_val=0, max_val=E)
                    sp.dma_start(ekeys[:, slot, bass.ds(w, 1), :, :].rearrange("p w k c -> p (w k c)"),
                                 keys_d[bass.ds(2 * at, 2 * CAP)].rearrange("(p c) -> p c", p=P)).then_inc(s_ek[slot], 16)

            load_keys(0, BK, 0)
            load_keys(BK, BK, 1)
            with sp.Fori(1, NG) as g:
                for slot in range(2):
                    sp.wait_ge(s_oh, GW * (g - 1) + BK * (slot + 1))
                    sp.sem_inc(s_turn, 1)
                    load_keys(GW * g + BK * slot, BK, slot)
            sp.wait_ge(s_oh, GW * (NG - 1) + BK)
            load_keys(GW * NG, TAILW, 0)

        @block.gpsimd
        def _(gp):
            nc.gpsimd.iota(iota_i[:], pattern=[[1, GN]], base=0, channel_multiplier=0)
            nc.gpsimd.iota(diff_i[:], pattern=[[1, P]], base=0, channel_multiplier=-1)
            nc.gpsimd.iota(mask_i[:], pattern=[[WIN, 9]], base=0, channel_multiplier=-1)
            nc.gpsimd.iota(goff_i[:], pattern=[[-GN, NG + 1]], base=0, channel_multiplier=0)
            nc.gpsimd.iota(win_i[:], pattern=[[CNT, windows]], base=0, channel_multiplier=0).then_inc(s_cst, 1)
            gp.wait_ge(s_rstd, 1)
            for t in range(NT):
                nc.gpsimd.tensor_scalar(xn[:, t, :], xx[:, t, :], mv[:, t, 0:1], rstd[:, t:t + 1], ALU.subtract, ALU.mult).then_inc(s_pool, 1)
            for t in range(NT):
                gp.wait_ge(s_pool, t + 1)
                nc.gpsimd.tensor_tensor(xx[:, t, :], xx[:, t, :], xn[:, t, :], ALU.add).then_inc(s_xn, 1)

            gp.wait_ge(s_flag, 1)
            general = gp.value_load(flag[0:1, 0:1], min_val=0, max_val=2 * E)
            with gp.If(general > 0):
                gp.wait_ge(g_xst, 1)
                gp.dma_start(xs_d.rearrange("(t p) d -> p t d", p=P), gen_xs[:, :].rearrange("p (t d) -> p t d", t=NT)).then_inc(g_xsd, 16)
                gp.wait_ge(g_xsd, 16)
                with gp.Fori(0, NG + 1) as g:
                    with gp.Fori(0, EC) as c:
                        gp.wait_ge(g_add, (EC + 1) * g + c + 1)
                        nc.gpsimd.tensor_copy(gidx[:], srci[:, bass.ds(c, 1)]).then_inc(g_idx, 1)
                        gp.wait_ge(g_idx, EC * g + c + 1)
                        gp.sem_inc(g_turn, 1)
                        gp.indirect_dma_start(out=gen_rows, out_offset=None, in_=xs_d[:, :],
                                              in_offset=bass.IndirectOffsetOnAxis(ap=gidx[:, 0:1], axis=0)).then_inc(g_row, 16)

        @block.scalar
        def _(act):
            act.dma_start(xx[:, 0:FULL, :], x[0:FULL * P, :].rearrange("(t p) d -> p t d", p=P)).then_inc(s_x, 16)
            act.wait_ge(s_cst, 2)
            act.dma_start(xx[0:LAST, FULL, :], x[FULL * P:N, :]).then_inc(s_x, 16)
            act.wait_ge(s_var, 1)
            nc.scalar.activation(rstd[:], mv[:, :, 1], ACT.Sqrt, bias=eps1[:]).then_inc(s_std, 1)
            act.wait_ge(s_deg, 1)
            nc.scalar.activation(dinv[:], deg[:], ACT.Sqrt).then_inc(s_sqd, 1)
            for g in range(NG + 1):
                act.wait_ge(s_dbmm, g + 1)
                cols = GN if g < NG else P
                nc.scalar.activation(dinvb[:, GN * g:GN * g + cols], psZ[g % 2][:, 0:cols], ACT.Copy).then_inc(s_dinvb, 1)

            def evict_z(g, h, cols):
                act.wait_ge(s_z, 2 * g + h + 1)
                nc.scalar.activation(zbuf[:, h, 0:cols], psZ[h][:, 0:cols], ACT.Copy).then_inc(s_zev, 1)

            def add_bias(g, cols):
                for m in range(DH):
                    act.wait_ge(s_yev, 2 * g + m + 1)
                    at = agg_at(g, m, cols)
                    nc.scalar.activation(at, ubuf[:, m, 0:cols], ACT.Identity, bias=biasT[:, m:m + 1]).then_inc(s_agg, 1)

            def step(g, wins, sums, lagged, cols, zcols=GN):
                for w in range(wins):
                    act.wait_ge(s_cnt, GW * g + w + 1)
                    nc.scalar.activation(C[:, parity(g), :, WIN * w:WIN * w + WIN],
                                         psC[w % 4][:, 0:CNT].rearrange("p (s n) -> p s n", s=NT), ACT.Copy).then_inc(s_cev, 1)
                    if isinstance(g, int) and g == 0 and w < NT:
                        if w == 0:
                            act.wait_ge(s_dinv, 1)
                            act.wait_ge(s_pool, NT)
                        nc.scalar.activation(xs[:, 0, w, :], xn[:, w, :], ACT.Copy, scale=dinvs[:, w:w + 1]).then_inc(s_xhi, 1)
                    if w == 8 and lagged:
                        add_bias(g - 2, GN)
                    if sums and w == 17:
                        if lagged:
                            act.wait_ge(s_y, 2 * (g - 1))
                        evict_z(g - 1, 0, zcols)
                    if sums and w == 29:
                        evict_z(g - 1, 1, zcols)
                if wins < GW:
                    if lagged:
                        add_bias(g - 2, GN)
                        act.wait_ge(s_y, 2 * (g - 1))
                    evict_z(g - 1, 0, zcols)
                    evict_z(g - 1, 1, zcols)

            step(0, GW, False, False, GN)
            step(1, GW, True, False, GN)
            act.wait_ge(s_xs, NT)
            act.wait_ge(s_xn, NT)
            with act.Fori(2, NG) as g:
                step(g, GW, True, True, GN)
            step(NG, TAILW, True, True, GN)
            step(NG + 1, 0, True, True, GN, TAILN)
            add_bias(NG, TAILN)


        @block.vector
        def _(dve):
            chain = [0]

            def link(ins):
                chain[0] += 1
                ins.then_inc(s_dve, 1)
                dve.wait_ge(s_dve, chain[0])

            nc.vector.memset(eps1[:], EPS)
            nc.vector.memset(ones[:], 1.0)
            nc.vector.memset(padk[:], -float(CNT * (windows + 1)))
            nc.vector.memset(xx[:, FULL, :], 0.0).then_inc(s_cst, 1)
            dve.wait_ge(s_cst, 2)
            nc.vector.tensor_copy(iota_h[:], iota_i[:, 0:CNT])
            nc.vector.tensor_copy(win_off[:], win_i[:])
            nc.vector.tensor_scalar(ident16[:], diff_i[:], 0.0, None, ALU.is_equal)
            nc.vector.tensor_scalar(identf[:], diff_i[:], 0.0, None, ALU.is_equal)
            nc.vector.tensor_scalar(below[:], mask_i[:], 0.0, None, ALU.is_gt)
            nc.vector.tensor_scalar(upper[:], diff_i[0:NT, 0:NT], 0.0, None, ALU.is_gt)
            dve.wait_ge(s_edge, 80)
            nc.vector.tensor_scalar(ti[:, 0, :], srci[:], 7, 4, ALU.logical_shift_right, ALU.logical_shift_left)
            nc.vector.tensor_scalar(ti[:, 1, :], dsti[:], 4, None, ALU.logical_shift_right)
            nc.vector.tensor_scalar(ti[:, 2, :], dsti[:], WIN - 1, None, ALU.bitwise_and)
            link(nc.vector.tensor_scalar(ti[:, 3, :], srci[:], P - 1, None, ALU.bitwise_and))
            nc.vector.tensor_copy(pack[:, :, 0], ti[:, 3, :]).then_inc(s_packed, 1)
            link(nc.vector.scalar_tensor_tensor(dstf[:], ti[:, 1, :], float(CNT), ti[:, 0, :], ALU.mult, ALU.add))
            nc.vector.tensor_tensor(pack[:, :, 1], dstf[:], ti[:, 2, :], ALU.add).then_inc(s_packed, 1)
            dve.wait_ge(s_packed, 2)
            nc.vector.tensor_scalar(ti[:, 0, :], dsti[:], P - 1, None, ALU.bitwise_and)
            nc.vector.tensor_copy(dstf[:], dsti[:])
            link(nc.vector.tensor_scalar(ti[:, 1, :], dsti[:], 7, None, ALU.logical_shift_right))
            nc.vector.tensor_copy(dstlo[:], ti[:, 0, :])
            nc.vector.tensor_tensor(desc[:], dsti[:], nexti[:], ALU.is_gt)
            link(nc.vector.tensor_copy(dsthi[:], ti[:, 1, :]))
            link(nc.vector.reduce_sum(descs[:], desc[:], AX.X))
            link(nc.vector.tensor_tensor(hist_hi, iota_h[0:EP, 0:NT].unsqueeze(1).to_broadcast([EP, EC, NT]),
                                    dsthi[:].unsqueeze(2).to_broadcast([EP, EC, NT]), ALU.is_equal))
            dve.wait_ge(s_x, 32)
            for t in range(NT):
                last = nc.vector.bn_stats(st6[:, t, :], xx[:, t, :])
            link(last)
            for t in range(NT):
                last = nc.vector.bn_aggr(mv[:, t, :], st6[:, t, :])
            last.then_inc(s_var, 1)
            dve.wait_ge(s_std, 1)
            nc.vector.reciprocal(rstd[:], rstd[:]).then_inc(s_rstd, 1)

            def degree(i, first):
                for r in range(HR):
                    if not first:
                        dve.wait_ge(s_hmm, HR * (i - 1) + r + 1)
                    at = HR * i + r
                    nc.vector.tensor_scalar(hist_lo[:, r, :], iota_h[0:EP, 0:P], dstlo[:, bass.ds(at, 1)], None,
                                            ALU.is_equal).then_inc(s_hoh, 1)

            degree(0, True)
            with dve.Fori(1, EC // HR) as i:
                degree(i, False)
            dve.wait_ge(s_hmm, EC)
            link(nc.vector.tensor_copy(degr[:], psC[0][:, 0:NT]))
            nc.vector.tensor_scalar(deg[:], degr[:], 1.0, 1.0, ALU.add, ALU.max).then_inc(s_deg, 1)
            dve.wait_ge(s_cum, 1)
            link(nc.vector.tensor_copy(cum[:], psY[0][0:NT, 0:9]))
            nc.vector.tensor_tensor(over[:], cum[:, 1:9], cum[:, 0:8], ALU.subtract).then_inc(s_cumsb, 1)
            dve.wait_ge(s_pref, 1)
            nc.vector.tensor_scalar(starti[:], cum[:, 0:8], psY[1][0:NT, 0:1], None, ALU.add).then_inc(s_start, 1)
            dve.wait_ge(s_cumsb, 1)
            link(nc.vector.tensor_scalar(over[:], over[:], float(CAP), None, ALU.is_gt))
            nc.vector.reduce_sum(overs[:], over[:], AX.X).then_inc(s_cumsb, 1)
            dve.wait_ge(s_sqd, 1)
            link(nc.vector.reciprocal(dinv[:], dinv[:]))
            nc.vector.tensor_scalar(dinvz[:], dinv[:], 1.0 / XSCALE, None, ALU.mult)
            link(nc.vector.tensor_scalar(dinvs[:], dinv[:], XSCALE, None, ALU.mult))
            for g in range(NG + 1):
                k = 4 if g < NG else 1
                ins = nc.vector.tensor_tensor(diag4[:, g, 0:k * P].rearrange("p (k n) -> p k n", k=k),
                                              identf[:].unsqueeze(1).to_broadcast([P, k, P]),
                                              dinvz[:, 4 * g:4 * g + k].unsqueeze(2).to_broadcast([P, k, P]), ALU.mult)
                ins.then_inc(s_diag, 1)
            dve.wait_ge(s_diag, 1)
            nc.vector.memset(gkey[:], 0.0).then_inc(s_dinv, 1)
            dve.wait_ge(s_flagmm, 1)
            nc.vector.tensor_copy(flag[:], psY[0][0:1, 16:17]).then_inc(s_flag, 1)

            def neighbour_u(g, cols):
                for m in range(DH):
                    dve.wait_ge(s_y, 2 * g + m + 1)
                    nc.vector.tensor_tensor(ubuf[:, m, 0:cols], psY[m][:, 0:cols], dinvb[:, bass.ds(GN * g, cols)],
                                            ALU.mult).then_inc(s_yev, 1)

            def norm_stats(g, cols):
                for m in range(DH):
                    dve.wait_ge(s_agg, 2 * g + m + 1)
                    nc.vector.bn_stats(stats[:, m, bass.ds(g, 1), :].rearrange("p a b -> p (a b)"), agg_at(g, m, cols)).then_inc(s_stat, 1)

            def step(g, wins, lagged):
                for w in range(wins):
                    at, slot = GW * g + w, w // BK
                    if w % BK == 0:
                        n = min(BK, wins)
                        dve.wait_ge(s_ek[slot], 16 * BK * g + 16 * n)
                        if not (isinstance(g, int) and g == 0):
                            dve.wait_ge(s_oh, GW * (g - 1) + BK * (slot + 1))
                        nc.vector.tensor_tensor(wkeys[:, slot, 0:n, :], ekeys[:, slot, 0:n, :, 1],
                                                win_off[:, bass.ds(at, n)].unsqueeze(2).to_broadcast([P, n, KCH]),
                                                ALU.subtract).then_inc(s_wk, 1)
                        dve.wait_ge(s_wk, 2 * g + slot + 1)
                    if not (isinstance(g, int) and g == 0 and w < OHR):
                        dve.wait_ge(s_cnt, at - OHR + 1)
                    r = w % OHR
                    for k in range(KCH):
                        nc.vector.tensor_scalar(oh_src[:, r, k, :], iota_h[:, 0:P], ekeys[:, slot, w % BK, k, 0:1], None, ALU.is_equal)
                        last = nc.vector.tensor_scalar(oh_key[:, r, k, :], iota_h[:], wkeys[:, slot, w % BK, k:k + 1], None, ALU.is_equal)
                    last.then_inc(s_oh, 1)
                    if isinstance(g, int) and g == 0 and 4 <= w < NT + 4:
                        t = w - 4
                        dve.wait_ge(s_xhi, t + 1)
                        nc.vector.scalar_tensor_tensor(xs[:, 1, t, :], xn[:, t, :], dinvs[:, t:t + 1], xs[:, 0, t, :],
                                                       ALU.mult, ALU.subtract).then_inc(s_xs, 1)
                    if lagged and w == 4:
                        neighbour_u(g - 2, GN)
                    if lagged and w == 16:
                        norm_stats(g - 2, GN)
                if lagged and wins < GW:
                    neighbour_u(g - 2, GN)
                    norm_stats(g - 2, GN)

            step(0, GW, False)
            step(1, GW, False)
            with dve.Fori(2, NG) as g:
                step(g, GW, True)
            step(NG, TAILW, True)
            step(NG + 1, 0, True)
            neighbour_u(NG, TAILN)
            norm_stats(NG, N - NG * GN)

            general = dve.value_load(flag[0:1, 0:1], min_val=0, max_val=2 * E)
            with dve.If(general > 0):
                dve.wait_ge(s_stat, 2 * (NG + 1))
                nc.vector.tensor_tensor(gen_xs[:, :], xs[:, 0, :, :].rearrange("p t d -> p (t d)"),
                                        xs[:, 1, :, :].rearrange("p t d -> p (t d)"), ALU.add).then_inc(g_xst, 1)

                def gen_group(g, cols, valid):
                    base = (EC + 1) * g
                    dve.wait_ge(g_mm, base + 1)
                    nc.vector.tensor_copy(zbuf[:, 0, 0:cols], psZ[0][:, 0:cols])
                    nc.vector.tensor_copy(zbuf[:, 1, 0:cols], psZ[1][:, 0:cols]).then_inc(g_add, 1)
                    with dve.Fori(0, EC) as c:
                        dve.wait_ge(g_add, base + c + 1)
                        nc.vector.tensor_tensor(gkey[:], dstf[:, bass.ds(c, 1)], goff_i[0:EP, bass.ds(g, 1)], ALU.add).then_inc(g_idx2, 1)
                        dve.wait_ge(g_idx2, EC * g + c + 1)
                        nc.vector.tensor_scalar(gen_oh[:, 0:cols], iota_i[0:EP, 0:cols], gkey[:, 0:1], None, ALU.is_equal).then_inc(g_oh, 1)
                        dve.wait_ge(g_mm, base + c + 2)
                        nc.vector.tensor_tensor(zbuf[:, 0, 0:cols], zbuf[:, 0, 0:cols], psZ[0][:, 0:cols], ALU.add)
                        nc.vector.tensor_tensor(zbuf[:, 1, 0:cols], zbuf[:, 1, 0:cols], psZ[1][:, 0:cols], ALU.add).then_inc(g_add, 1)
                    dve.wait_ge(g_y, g + 1)
                    for m in range(DH):
                        at = agg_at(g, m, cols)
                        nc.vector.tensor_tensor(at, psY[m][:, 0:cols], dinvb[:, bass.ds(GN * g, cols)], ALU.mult).then_inc(g_u, 1)
                        dve.wait_ge(g_u, 4 * g + 2 * m + 1)
                        nc.vector.tensor_scalar(at, at, biasT[:, m:m + 1], None, ALU.add).then_inc(g_u, 1)
                        dve.wait_ge(g_u, 4 * g + 2 * m + 2)
                        nc.vector.bn_stats(stats[:, m, bass.ds(g, 1), :].rearrange("p a b -> p (a b)"), agg_at(g, m, valid))

                with dve.Fori(0, NG) as g:
                    gen_group(g, GN, GN)
                gen_group(NG, TAILN, N - NG * GN)

        @block.tensor
        def _(pe):
            def degree(i, first, final):
                for r in range(HR):
                    pe.wait_ge(s_hoh, HR * i + r + 1)
                    nc.tensor.matmul(psC[0][:, 0:NT], hist_lo[:, r, :], hist_hi[:, bass.ds(HR * i + r, 1), :].rearrange("p a b -> p (a b)"),
                                     start=(first and r == 0), stop=(final and r == HR - 1)).then_inc(s_hmm, 1)

            degree(0, True, False)
            with pe.Fori(1, EC // HR - 1) as i:
                degree(i, False, False)
            degree(EC // HR - 1, False, True)
            pe.wait_ge(s_deg, 1)
            nc.tensor.matmul(psY[0][0:NT, 0:9], degr[:], below[:], start=True, stop=True).then_inc(s_cum, 1)
            pe.wait_ge(s_cumsb, 1)
            nc.tensor.matmul(psY[1][0:NT, 0:1], upper[:], cum[:, 8:9], start=True, stop=True).then_inc(s_pref, 1)
            pe.wait_ge(s_cumsb, 2)
            nc.tensor.matmul(psY[0][0:1, 16:17], descs[:], ones[0:EP, 0:1], start=True, stop=False)
            nc.tensor.matmul(psY[0][0:1, 16:17], overs[:], ones[0:NT, 0:1], start=False, stop=True).then_inc(s_flagmm, 1)
            for g in range(NG + 1):
                cols = GN if g < NG else P
                pe.wait_ge(s_diag, g + 1)
                if g >= 2:
                    pe.wait_ge(s_dinvb, g - 1)
                nc.tensor.matmul(psZ[g % 2][:, 0:cols], ones[:], diag4[:, g, 0:cols], start=True, stop=True).then_inc(s_dbmm, 1)
            pe.wait_ge(s_dinvb, NG + 1)

            def sum_parts(g, h, cols, tiles):
                parts = [(p, s) for p in range(2) for s in range(NT)]
                for i, (p, s) in enumerate(parts):
                    yield dict(out=psZ[h][:, 0:cols], lhsT=xs[:, p, s, P * h:P * h + P], rhs=C[:, parity(g), s, 0:cols],
                               start=(i == 0), stop=False)
                for j in range(tiles):
                    n = min(P, cols - P * j)
                    for p in range(2):
                        t = bass.ds(4 * g + j, 1)
                        yield dict(out=psZ[h][:, P * j:P * j + n],
                                   lhsT=xs[:, p, t, P * h:P * h + P].rearrange("p a b -> p (a b)") if not isinstance(g, int) else xs[:, p, 4 * g + j, P * h:P * h + P],
                                   rhs=ident16[:, 0:n], start=False, stop=(j == tiles - 1 and p == 1))

            def products(g, cols):
                for m in range(DH):
                    for k in range(DH):
                        last = nc.tensor.matmul(psY[m][:, 0:cols], wgcn[:, k, P * m:P * m + P], zbuf[:, k, 0:cols],
                                                start=(k == 0), stop=(k == DH - 1))
                    yield last

            def run(todo, n):
                for _ in range(n):
                    m = next(todo, None)
                    if m is None:
                        return
                    final = m["stop"]
                    ins = nc.tensor.matmul(m["out"], m["lhsT"], m["rhs"], start=m["start"], stop=m["stop"])
                    if final:
                        ins.then_inc(s_z, 1)

            def step(g, wins, sums, lagged, cols=GN, tiles=4):
                todo = [iter(())] * 2
                if sums:
                    todo = [sum_parts(g - 1, h, cols, tiles) for h in range(DH)]
                for w in range(wins):
                    pe.wait_ge(s_oh, GW * g + w + 1)
                    if not (isinstance(g, int) and g == 0 and w < 4):
                        pe.wait_ge(s_cev, GW * g + w - 3)
                    for k in range(KCH):
                        last = nc.tensor.matmul(psC[w % 4][:, 0:CNT], oh_src[:, w % OHR, k, :], oh_key[:, w % OHR, k, :],
                                                start=(k == 0), stop=(k == KCH - 1))
                    last.then_inc(s_cnt, 1)
                    if wins == GW and sums:
                        if w == 1:
                            pe.wait_ge(s_cev, GW * g)
                            if not lagged:
                                pe.wait_ge(s_xs, NT)
                        if 1 <= w < 15:
                            run(todo[0], 5)
                        elif 15 <= w < 29:
                            run(todo[1], 5)
                if sums and wins < GW:
                    pe.wait_ge(s_cev, min(GW * g, NG * GW + TAILW) if wins else NG * GW + TAILW)
                for h in range(DH):
                    run(todo[h], 1000)
                if sums:
                    pe.wait_ge(s_zev, 2 * g)
                    if lagged:
                        pe.wait_ge(s_yev, 2 * (g - 1))
                    for last in products(g - 1, cols):
                        last.then_inc(s_y, 1)

            pe.wait_ge(s_wt, 32)
            step(0, GW, False, False)
            step(1, GW, True, False)
            with pe.Fori(2, NG) as g:
                step(g, GW, True, True)
            step(NG, TAILW, True, True)
            step(NG + 1, 0, True, True, TAILN, 1)

            general = pe.value_load(flag[0:1, 0:1], min_val=0, max_val=2 * E)
            with pe.If(general > 0):
                def gen_group(g, cols, tiles):
                    base = (EC + 1) * g
                    for h in range(DH):
                        for j in range(tiles):
                            n = min(P, cols - P * j)
                            for p in range(2):
                                t = bass.ds(4 * g + j, 1)
                                last = nc.tensor.matmul(psZ[h][:, P * j:P * j + n], xs[:, p, t, P * h:P * h + P].rearrange("p a b -> p (a b)"),
                                                        ident16[:, 0:n], start=(p == 0 and j == 0), stop=(j == tiles - 1 and p == 1))
                    last.then_inc(g_mm, 1)
                    with pe.Fori(0, EC) as c:
                        pe.wait_ge(g_row, 16 * (EC * g + c) + 16)
                        pe.wait_ge(g_oh, EC * g + c + 1)
                        for h in range(DH):
                            last = nc.tensor.matmul(psZ[h][:, 0:cols], gen_rows[:, P * h:P * h + P], gen_oh[:, 0:cols], start=True, stop=True)
                        last.then_inc(g_mm, 1)
                    pe.wait_ge(g_add, base + EC + 1)
                    for last in products(g, cols):
                        pass
                    last.then_inc(g_y, 1)

                pe.wait_ge(g_xst, 1)
                with pe.Fori(0, NG) as g:
                    gen_group(g, GN, 4)
                gen_group(NG, TAILN, 1)

        ctx1.close()

        fh = sb("fh", [P, DH, NPAD], f32r, ctx2)
        fl = sb("fl", [P, DH, NPAD], f32r, ctx2)
        wraw = sb("wraw", [P, 2, 3, DH, D], fp32, ctx2)
        wh = sb("wh", [P, 2, 3, DH, D], f32r, ctx2)
        wl = sb("wl", [P, 2, 3, DH, D], f32r, ctx2)
        rbuf = sb("rbuf", [P, 2, DH, GN], fp32, ctx2)
        h1h = sb("h1h", [P, 2, DH, GN], f32r, ctx2)
        h1l = sb("h1l", [P, 2, DH, GN], f32r, ctx2)
        h2h = sb("h2h", [P, 2, DH, GN], f32r, ctx2)
        h2l = sb("h2l", [P, 2, DH, GN], f32r, ctx2)
        gammaT, betaT = sb("gammaT", [P, DH], fp32, ctx2), sb("betaT", [P, DH], fp32, ctx2)
        b1T, b2T = sb("b1T", [P, NEXP, DH], fp32, ctx2), sb("b2T", [P, NEXP, DH], fp32, ctx2)
        b3s = sb("b3s", [NEXP, D], fp32, ctx2)
        rw1s, rw1h, rw1l = sb("rw1s", [P, DH, RH], fp32, ctx2), sb("rw1h", [P, DH, RH], f32r, ctx2), sb("rw1l", [P, DH, RH], f32r, ctx2)
        rb1T, rw2s, rb2b = sb("rb1T", [P, 1], fp32, ctx2), sb("rw2s", [RH, NEXP], fp32, ctx2), sb("rb2b", [P, NEXP], fp32, ctx2)
        mvb, bnr = sb("mvb", [P, DH, 2], fp32, ctx2), sb("bnr", [P, DH], fp32, ctx2)
        bna, bnb = sb("bna", [P, DH], fp32, ctx2), sb("bnb", [P, DH], fp32, ctx2)
        st6b, mv2, rstd2 = sb("st6b", [P, NT, 6], fp32, ctx2), sb("mv2", [P, NT, 2], fp32, ctx2), sb("rstd2", [P, NT], fp32, ctx2)
        ftok = sb("ftok", [P, 8, D], fp32, ctx2)
        rhb = sb("rhb", [P, 2, GN], fp32, ctx2)
        lg, pr, eq, f1, f2 = (sb(n, [P, NT, NEXP], fp32, ctx2) for n in ("lg", "pr", "eq", "f1", "f2"))
        m1, m2, mk, e2, g1, g2 = (sb(n, [P, NT], fp32, ctx2) for n in ("m1", "m2", "mk", "e2", "g1", "g2"))
        rank_i, rank = sb("rank_i", [P, NEXP], i32, ctx2), sb("rank", [P, NEXP], fp32, ctx2)
        gate = sb("gate", [P, NEXP, NT], fp32, ctx2)
        gT = agg[0:NEXP, 0:NT * P]
        bank = [ps(f"bank{i}", [P, 512], ctx2) for i in range(8)]

        t_w, t_raw = sem("small_weights_loaded"), [sem(f"raw_weights_loaded{i}") for i in range(2)]
        t_act, t_pe, t_gp = sem("act_turn"), sem("pe_turn"), sem("pool_turn")
        t_dve = sem("dve_chain")
        t_bnv, t_bns, t_bn = sem("bn_var_ready"), sem("bn_std_ready"), sem("bn_ready")
        t_relu, t_tr, t_x1 = sem("relu_ready"), sem("y_transposed"), sem("x1_ready")
        t_v2, t_s2, t_f, t_ft, t_fh, t_fl = (sem("ln_var_ready"), sem("ln_std_ready"), sem("f_ready"), sem("f_transposed"),
                                             sem("f_hi_ready"), sem("f_ready_T"))
        t_rw, t_rh, t_rhs, t_lg = sem("router_weights_split"), sem("router_hidden_done"), sem("router_hidden_ready"), sem("logits_done")
        t_sub, t_exp, t_dm, t_e2, t_gate = (sem("logits_shifted"), sem("exp_ready"), sem("gap_ready"), sem("gap_exp_ready"), sem("gates_ready"))
        t_split, t_wsplit, t_rank = sem("weights_hi_ready"), sem("weights_split"), sem("rank_ready")
        t_l, t_r, t_h = [sem(f"layer{i}_done") for i in (1, 2)], [sem(f"layer{i}_relu_ready") for i in (1, 2)], [sem(f"layer{i}_parts_ready") for i in (1, 2)]
        t_l3, t_comb = sem("layer3_done"), sem("outputs_combined")
        t_gt, t_gts, t_b3, t_fin, t_out = sem("gates_transposed"), sem("gates_T_ready"), sem("b3_done"), sem("output_ready"), sem("output_stored")

        UNITS = NG + 1
        hb = ((h1h, h1l), (h2h, h2l))
        bT = (b1T, b2T)

        def tiles_of(g):
            return 4 if g < NG else 1

        def rows_of(t):
            return P if t < FULL else TAILN

        pe_slot, unit_slot = [0], [0]

        def slot_of(g):
            return unit_slot[0]

        def relu_unit(what, e, q, X, layer):
            unit_slot[0] = X
            what(e, 2 * q + X, layer, GN)

        def tail_unit(what, e, layer):
            what(e, NG, layer, TAILN)

        def gate_t(t, r):
            return gate[0:r, :, t]

        def three(into, pairs):
            last = None
            terms = [(a[i], b[j]) for a, b in pairs for i, j in ((0, 0), (0, 1), (1, 0))]
            for n, (a, b) in enumerate(terms):
                last = nc.tensor.matmul(into, a, b, start=(n == 0), stop=(n == len(terms) - 1))
            return last

        block2 = ctx2.enter_context(nc.Block())

        @block2.sync
        def _(sp):
            with nc.allow_non_contiguous_dma(reason="one value per partition"):
                sp.dma_start(gammaT[:], gamma.rearrange("(k p) -> p k", p=P)).then_inc(t_w, 16)
                sp.dma_start(betaT[:], beta.rearrange("(k p) -> p k", p=P)).then_inc(t_w, 16)
                sp.dma_start(rb1T[:], rb1.rearrange("(k p) -> p k", p=P)).then_inc(t_w, 16)
                for e in range(NEXP):
                    sp.dma_start(b1T[:, e, :], b1[e, :].rearrange("(k p) -> p k", p=P)).then_inc(t_w, 16)
                    sp.dma_start(b2T[:, e, :], b2[e, :].rearrange("(k p) -> p k", p=P)).then_inc(t_w, 16)
            sp.dma_start(rw1s[:], rw1.rearrange("(k p) n -> p k n", p=P)).then_inc(t_w, 16)
            sp.dma_start(rw2s[:], rw2).then_inc(t_w, 16)
            sp.dma_start(rb2b[:], rb2.rearrange("(o n) -> o n", o=1).to_broadcast([P, NEXP])).then_inc(t_w, 16)
            sp.dma_start(b3s[:], b3).then_inc(t_w, 16)

            def load_expert(e, slot):
                for i, w in enumerate((w1, w2, w3)):
                    sp.dma_start(wraw[:, slot, i, :, :], w[bass.ds(e, 1), :, :].rearrange("e (k p) n -> p (e k) n", p=P)).then_inc(t_raw[slot], 16)

            load_expert(0, 0)
            load_expert(1, 1)
            with sp.Fori(1, NEXP // 2) as pair:
                for slot in range(2):
                    sp.wait_ge(t_wsplit, 2 * pair + slot - 1)
                    sp.sem_inc(s_turn, 1)
                    load_expert(2 * pair + slot, slot)
            for g in range(UNITS):
                sp.wait_ge(t_fin, 4 * g + tiles_of(g))
                if g < NG:
                    sp.dma_start(out[GN * g:GN * (g + 1), :].rearrange("(t p) d -> p t d", p=P), xx[:, 4 * g:4 * g + 4, :]).then_inc(t_out, 16)
                else:
                    sp.dma_start(out[FULL * P:N, :], xx[0:LAST, FULL, :]).then_inc(t_out, 16)
            sp.wait_ge(t_out, 16 * UNITS)

        @block2.gpsimd
        def _(gp):
            nc.gpsimd.iota(rank_i[:], pattern=[[-1, NEXP]], base=NEXP, channel_multiplier=0).then_inc(t_rank, 1)
            gp.wait_ge(t_w, 16 * 19)
            nc.gpsimd.tensor_copy(rw1h[:], rw1s[:]).then_inc(t_rw, 1)
            gp.wait_ge(t_rw, 1)
            nc.gpsimd.tensor_tensor(rw1l[:], rw1s[:], rw1h[:].bitcast(fp32), ALU.subtract).then_inc(t_rw, 1)

            def split(pair, slot, first):
                e = 2 * pair + slot
                gp.wait_ge(t_raw[slot], 48 * pair + 48)
                if not first:
                    gp.wait_ge(t_l3, NT * (e - 1))
                gp.sem_inc(t_gp, 1)
                nc.gpsimd.tensor_copy(wh[:, slot], wraw[:, slot]).then_inc(t_split, 1)
                gp.wait_ge(t_split, e + 1)
                nc.gpsimd.tensor_tensor(wl[:, slot], wraw[:, slot], wh[:, slot].bitcast(fp32), ALU.subtract).then_inc(t_wsplit, 1)

            split(0, 0, True)
            split(0, 1, True)
            with gp.Fori(1, NEXP // 2) as pair:
                split(pair, 0, False)
                split(pair, 1, False)

        @block2.scalar
        def _(act):
            act.wait_ge(t_bnv, 1)
            nc.scalar.activation(bnr[:], mvb[:, :, 1], ACT.Sqrt, bias=eps1[:]).then_inc(t_bns, 1)
            act.wait_ge(t_bn, 1)
            for g in range(UNITS):
                cols = GN if g < NG else TAILN
                for m in range(DH):
                    at = agg[:, m * NPAD + GN * g:m * NPAD + GN * g + cols]
                    nc.scalar.activation(at, at, ACT.Relu, bias=bnb[:, m:m + 1], scale=bna[:, m:m + 1]).then_inc(t_relu, 1)
            act.wait_ge(t_v2, 1)
            nc.scalar.activation(rstd2[:], mv2[:, :, 1], ACT.Sqrt, bias=eps1[:]).then_inc(t_s2, 1)
            for g in range(UNITS + 1):
                if g < UNITS:
                    cols = GN if g < NG else TAILN
                    act.wait_ge(t_ft, g + 1)
                    for m in range(DH):
                        nc.scalar.activation(fh[:, m, GN * g:GN * g + cols], bank[4 + 2 * (g % 2) + m][:, 0:cols], ACT.Copy).then_inc(t_fh, 1)
                if g >= 1:
                    cols = GN if g - 1 < NG else TAILN
                    act.wait_ge(t_rh, g)
                    if g >= 3:
                        act.wait_ge(t_lg, g - 2)
                    nc.scalar.activation(rhb[:, (g - 1) % 2, 0:cols], bank[(g - 1) % 2][:, 0:cols], ACT.Relu, bias=rb1T[:, 0:1]).then_inc(t_rhs, 1)
            act.wait_ge(t_sub, 1)
            nc.scalar.activation(pr[:], lg[:], ACT.Exp).then_inc(t_exp, 1)
            act.wait_ge(t_dm, 1)
            nc.scalar.activation(e2[:], m2[:], ACT.Exp).then_inc(t_e2, 1)

            def relu_parts(e, g, layer, cols):
                u, X = UNITS * e + g, 0 if cols < GN else slot_of(g)
                for m in range(DH):
                    act.wait_ge(t_l[layer], 2 * u + m + 1)
                    act.sem_inc(t_act, 1)
                    b = bT[layer][:, bass.ds(e, 1), m:m + 1].rearrange("p a b -> p (a b)")
                    src_ = bank[2 * X + m][:, 0:cols]
                    nc.scalar.activation(rbuf[:, X, m, 0:cols], src_, ACT.Relu, bias=b)
                    nc.scalar.activation(hb[layer][0][:, X, m, 0:cols], src_, ACT.Relu, bias=b).then_inc(t_r[layer], 1)

            with act.Fori(0, NEXP) as e:
                with act.Fori(0, NG // 2) as q:
                    for layer in range(2):
                        for X in range(2):
                            relu_unit(relu_parts, e, q, X, layer)
                for layer in range(2):
                    tail_unit(relu_parts, e, layer)
            for g in range(UNITS):
                n = P * tiles_of(g) if g < NG else TAILN
                act.wait_ge(t_gt, g + 1)
                nc.scalar.activation(gT[:, GN * g:GN * g + n], bank[g % 2][0:NEXP, 0:n], ACT.Copy).then_inc(t_gts, 1)

        @block2.vector
        def _(dve):
            chain = [0]

            def link(ins):
                chain[0] += 1
                ins.then_inc(t_dve, 1)
                dve.wait_ge(t_dve, chain[0])

            for m in range(DH):
                last = nc.vector.bn_aggr(mvb[:, m, :], stats[:, m, :, :].rearrange("p a b -> p (a b)"))
            last.then_inc(t_bnv, 1)
            dve.wait_ge(t_w, 16 * 19)
            dve.wait_ge(t_bns, 1)
            link(nc.vector.reciprocal(bnr[:], bnr[:]))
            link(nc.vector.tensor_tensor(bna[:], bnr[:], gammaT[:], ALU.mult))
            link(nc.vector.tensor_tensor(bnr[:], mvb[:, :, 0], bna[:], ALU.mult))
            nc.vector.tensor_tensor(bnb[:], betaT[:], bnr[:], ALU.subtract).then_inc(t_bn, 1)
            for t in range(NT):
                g, r = t // 4, rows_of(t)
                dve.wait_ge(t_tr, min(NT, t - t % 2 + 2))
                src_ = bank[2 * (g % 2) + (t % 4) // 2][0:r, D * (t % 2):D * (t % 2) + D]
                nc.vector.tensor_tensor(xx[0:r, t, :], xx[0:r, t, :], src_, ALU.add).then_inc(t_x1, 1)
                if t >= 1:
                    dve.wait_ge(t_x1, t)
                    nc.vector.bn_stats(st6b[:, t - 1, :], xx[:, t - 1, :])
            dve.wait_ge(t_x1, NT)
            link(nc.vector.bn_stats(st6b[:, NT - 1, :], xx[:, NT - 1, :]))
            for t in range(NT):
                last = nc.vector.bn_aggr(mv2[:, t, :], st6b[:, t, :])
            last.then_inc(t_v2, 1)
            dve.wait_ge(t_s2, 1)
            link(nc.vector.reciprocal(rstd2[:], rstd2[:]))
            for g in range(UNITS + 1):
                if g < UNITS:
                    if g >= 2:
                        dve.wait_ge(t_ft, g - 1)
                    for j in range(tiles_of(g)):
                        t = 4 * g + j
                        last = nc.vector.tensor_scalar(ftok[:, t % 8, :], xx[:, t, :], mv2[:, t, 0:1], rstd2[:, t:t + 1], ALU.subtract, ALU.mult)
                    last.then_inc(t_f, 1)
                if g >= 1:
                    cols = GN if g - 1 < NG else TAILN
                    for m in range(DH):
                        at = slice(GN * (g - 1), GN * (g - 1) + cols)
                        dve.wait_ge(t_fh, 2 * (g - 1) + m + 1)
                        nc.vector.tensor_tensor(fl[:, m, at], bank[4 + 2 * ((g - 1) % 2) + m][:, 0:cols], fh[:, m, at].bitcast(fp32),
                                                ALU.subtract).then_inc(t_fl, 1)
            bc = [P, NT, NEXP]
            dve.wait_ge(t_rank, 1)
            nc.vector.tensor_copy(rank[:], rank_i[:])
            nc.vector.memset(lg[:], 0.0)
            dve.wait_ge(t_lg, UNITS)
            link(nc.vector.memset(pr[:], 0.0))
            logits = bank[2][:, 0:NT * 8].rearrange("p (t e) -> p t e", e=8)[:, :, 0:NEXP]
            rb = rb2b[:].unsqueeze(1)
            nc.vector.tensor_tensor(lg[:, 0:FULL, :], logits[:, 0:FULL, :], rb.to_broadcast([P, FULL, NEXP]), ALU.add)
            link(nc.vector.tensor_tensor(lg[0:TAILN, FULL:NT, :], logits[0:TAILN, FULL:NT, :], rb[0:TAILN].to_broadcast([TAILN, 1, NEXP]), ALU.add))
            link(nc.vector.reduce_max(m1[:], lg[:], AX.X))
            nc.vector.tensor_tensor(lg[:], lg[:], m1[:].unsqueeze(2).to_broadcast(bc), ALU.subtract).then_inc(t_sub, 1)
            dve.wait_ge(t_exp, 1)
            link(nc.vector.reduce_sum(m2[:], pr[:], AX.X))
            link(nc.vector.reciprocal(m2[:], m2[:]))
            link(nc.vector.tensor_tensor(pr[:], pr[:], m2[:].unsqueeze(2).to_broadcast(bc), ALU.mult))

            def pick(top, chosen):
                link(nc.vector.reduce_max(top[:], pr[:], AX.X))
                link(nc.vector.tensor_tensor(eq[:], pr[:], top[:].unsqueeze(2).to_broadcast(bc), ALU.is_equal))
                link(nc.vector.tensor_tensor(eq[:], eq[:], rank[:].unsqueeze(1).to_broadcast(bc), ALU.mult))
                link(nc.vector.reduce_max(mk[:], eq[:], AX.X))
                link(nc.vector.tensor_tensor(chosen[:], eq[:], mk[:].unsqueeze(2).to_broadcast(bc), ALU.is_equal))

            pick(m1, f1)
            link(nc.vector.scalar_tensor_tensor(pr[:], f1[:], -2.0, pr[:], ALU.mult, ALU.add))
            pick(m2, f2)
            nc.vector.tensor_tensor(m2[:], m2[:], m1[:], ALU.subtract).then_inc(t_dm, 1)
            dve.wait_ge(t_e2, 1)
            link(nc.vector.tensor_scalar(g1[:], e2[:], 1.0, None, ALU.add))
            link(nc.vector.reciprocal(g1[:], g1[:]))
            link(nc.vector.tensor_tensor(g2[:], e2[:], g1[:], ALU.mult))
            nc.vector.tensor_tensor(f1[:], f1[:], g1[:].unsqueeze(2).to_broadcast(bc), ALU.mult)
            link(nc.vector.tensor_tensor(f2[:], f2[:], g2[:].unsqueeze(2).to_broadcast(bc), ALU.mult))
            nc.vector.tensor_tensor(gate[:].rearrange("p e t -> p t e"), f1[:], f2[:], ALU.add).then_inc(t_gate, 1)
            dve.wait_ge(t_gate, 1)

            def low_part(e, g, layer, cols):
                u, X = UNITS * e + g, 0 if cols < GN else slot_of(g)
                for m in range(DH):
                    dve.wait_ge(t_r[layer], 2 * u + m + 1)
                    nc.vector.tensor_tensor(hb[layer][1][:, X, m, 0:cols], rbuf[:, X, m, 0:cols],
                                            hb[layer][0][:, X, m, 0:cols].bitcast(fp32), ALU.subtract).then_inc(t_h[layer], 1)

            def combine(e, t, b, ahead, rows=P):
                v = NT * e + t
                dve.wait_ge(t_l3, v + ahead + 1)
                at = xx[0:rows, bass.ds(t, 1), :].rearrange("p a b -> p (a b)")
                w = gate[0:rows].rearrange("p e t -> p (e t)")[:, bass.ds(v, 1)]
                nc.vector.scalar_tensor_tensor(at, b[0:rows, :], w, at, ALU.mult, ALU.add).then_inc(t_comb, 1)

            dve.sem_inc(t_comb, 1)
            with dve.Fori(0, NEXP) as e:
                with dve.Fori(0, NG // 2) as q:
                    for layer in range(2):
                        for X in range(2):
                            relu_unit(low_part, e, q, X, layer)
                    for j in range(8):
                        combine(e, 8 * q + j, bank[4 + j // 2][:, D * (j % 2):D * (j % 2) + D], 1 - j % 2)
                for layer in range(2):
                    tail_unit(low_part, e, layer)
                combine(e, FULL, bank[4][:, 0:D], 0, TAILN)
            for t in range(NT):
                r = rows_of(t)
                dve.wait_ge(t_b3, t + 1)
                if t == 0:
                    dve.wait_ge(t_comb, NT * NEXP + 1)
                src_ = bank[4 + t % 4][0:r, 0:D]
                nc.vector.tensor_tensor(xx[0:r, t, :], xx[0:r, t, :], src_, ALU.add).then_inc(t_fin, 1)

        @block2.tensor
        def _(pe):
            for t in range(NT):
                g, r = t // 4, rows_of(t)
                if t % 4 == 0:
                    pe.wait_ge(t_relu, 2 * g + 2)
                    if g >= 2:
                        pe.wait_ge(t_x1, 4 * (g - 1))
                for m in range(DH):
                    last = nc.tensor.transpose(bank[2 * (g % 2) + (t % 4) // 2][0:r, D * (t % 2) + P * m:D * (t % 2) + P * m + P],
                                               agg[:, m * NPAD + P * t:m * NPAD + P * t + r], identf[:])
                last.then_inc(t_tr, 1)
            pe.wait_ge(t_rw, 2)
            for g in range(UNITS + 2):
                if g < UNITS:
                    pe.wait_ge(t_f, g + 1)
                    if g >= 2:
                        pe.wait_ge(t_fl, 2 * (g - 1))
                    for m in range(DH):
                        for j in range(tiles_of(g)):
                            t = 4 * g + j
                            r = rows_of(t)
                            last = nc.tensor.transpose(bank[4 + 2 * (g % 2) + m][:, P * j:P * j + r], ftok[0:r, t % 8, P * m:P * m + P], identf[0:r, 0:r])
                    last.then_inc(t_ft, 1)
                if 1 <= g <= UNITS:
                    k_, cols = g - 1, GN if g - 1 < NG else TAILN
                    at = slice(GN * k_, GN * k_ + cols)
                    pe.wait_ge(t_fl, 2 * k_ + 2)
                    if k_ >= 2:
                        pe.wait_ge(t_rhs, k_ - 1)
                    if k_ < 2:
                        pe.wait_ge(t_x1, NT)
                    three(bank[k_ % 2][:, 0:cols], [((rw1h[:, k, :], rw1l[:, k, :]), (fh[:, k, at], fl[:, k, at])) for k in range(DH)]).then_inc(t_rh, 1)
                if g >= 2:
                    k_ = g - 2
                    pe.wait_ge(t_rhs, k_ + 1)
                    for j in range(tiles_of(k_)):
                        t = 4 * k_ + j
                        r = rows_of(t)
                        last = nc.tensor.matmul(bank[2][0:r, 8 * t:8 * t + NEXP], rhb[:, k_ % 2, P * j:P * j + r], rw2s[:], start=True, stop=True)
                    last.then_inc(t_lg, 1)
            pe.wait_ge(t_sub, 1)

            def layer_unit(e, g, layer, cols):
                X = 0 if cols < GN else slot_of(g)
                s_ = pe_slot[0]
                if layer == 1:
                    pe.wait_ge(t_h[0], 2 * (UNITS * e + g) + 2)
                for m in range(DH):
                    cs = slice(P * m, P * m + P)
                    if layer == 0:
                        rhs = [(fh[:, k, bass.ds(GN * g, cols)], fl[:, k, bass.ds(GN * g, cols)]) for k in range(DH)]
                    else:
                        rhs = [(h1h[:, X, k, 0:cols], h1l[:, X, k, 0:cols]) for k in range(DH)]
                    three(bank[2 * X + m][:, 0:cols], [((wh[:, s_, layer, k, cs], wl[:, s_, layer, k, cs]), rhs[k]) for k in range(DH)]).then_inc(t_l[layer], 1)

            def out_unit(e, g, X, tiles):
                s_ = pe_slot[0]
                pe.wait_ge(t_h[1], 2 * (UNITS * e + g) + 2)
                if X == 0:
                    pe.wait_ge(t_comb, NT * e + 4 * g + 1)
                for j in range(tiles):
                    three(bank[4 + 2 * X + j // 2][:, D * (j % 2):D * (j % 2) + D],
                          [((h2h[:, X, k, P * j:P * j + P], h2l[:, X, k, P * j:P * j + P]), (wh[:, s_, 2, k, :], wl[:, s_, 2, k, :])) for k in range(DH)]
                          ).then_inc(t_l3, 1)

            with pe.Fori(0, NEXP // 2) as pair:
                for slot in range(2):
                    e = 2 * pair + slot
                    pe_slot[0] = slot
                    pe.wait_ge(t_wsplit, e + 1)
                    pe.sem_inc(t_pe, 1)
                    with pe.Fori(0, NG // 2) as q:
                        for layer in range(2):
                            for X in range(2):
                                relu_unit(layer_unit, e, q, X, layer)
                        for X in range(2):
                            out_unit(e, 2 * q + X, X, 4)
                    for layer in range(2):
                        tail_unit(layer_unit, e, layer)
                    out_unit(e, NG, 0, 1)
            for g in range(UNITS):
                n = tiles_of(g)
                if g >= 2:
                    pe.wait_ge(t_gts, g - 1)
                for j in range(n):
                    t = 4 * g + j
                    r = rows_of(t)
                    last = nc.tensor.transpose(bank[g % 2][0:NEXP, P * j:P * j + r], gate_t(t, r), identf[0:r, 0:r])
                last.then_inc(t_gt, 1)
            for t in range(NT):
                r = rows_of(t)
                if t % 4 == 0:
                    pe.wait_ge(t_gts, t // 4 + 1)
                if t < 4:
                    pe.wait_ge(t_comb, NT * NEXP + 1)
                else:
                    pe.wait_ge(t_fin, t - 3)
                nc.tensor.matmul(bank[4 + t % 4][0:r, 0:D], gT[:, P * t:P * t + r], b3s[:], start=True, stop=True).then_inc(t_b3, 1)

        ctx2.close()


_INS = ["x", "src", "dst", "L0_gnn_W", "L0_gnn_bias", "L0_gnn_gamma", "L0_gnn_beta",
        "L0_ffn_router_w1", "L0_ffn_router_b1", "L0_ffn_router_w2", "L0_ffn_router_b2",
        "L0_ffn_expert_w1", "L0_ffn_expert_b1", "L0_ffn_expert_w2", "L0_ffn_expert_b2",
        "L0_ffn_expert_w3", "L0_ffn_expert_b3"]


def kernel(**inputs):
    import numpy as _np
    import concourse.bacc as _bacc
    from concourse import mybir as _mybir
    from concourse.bass_utils import run_bass_kernel_spmd as _run

    nc = _bacc.Bacc("TRN2", target_bir_lowering=False, num_devices=1)
    arrays, args = {}, []
    for name in _INS:
        a = _np.ascontiguousarray(inputs[name])
        arrays[f"in_{name}"] = a
        args.append(nc.dram_tensor(f"in_{name}", a.shape, _mybir.dt.from_np(a.dtype), kind="ExternalInput").ap())
    args.append(nc.dram_tensor("out_0", [N, D], fp32, kind="ExternalOutput").ap())
    build(nc, *args)
    r = _run(nc, [arrays], core_ids=[0])
    return r.results[0]["out_0"]
```

```python
import concourse.bass as bass
from concourse import mybir
from contextlib import ExitStack

fp32 = mybir.dt.float32
fp16 = mybir.dt.float16
f32r = mybir.dt.float32r
i32 = mybir.dt.int32
ALU = mybir.AluOpType
ACT = mybir.ActivationFunctionType
AX = mybir.AxisListType

N, D, E = 3125, 256, 50000
P = 128
NT = -(-N // P)
FULL = N // P
LAST = N - FULL * P
DH = D // P
EP, EC = 125, 400
WIN = 16
KCH = 3
CAP = KCH * P
CNT = NT * WIN
GW = 32
GN = GW * WIN
NG = N // GN
TAILW = -(-(N - NG * GN) // WIN)
TAILN = TAILW * WIN
NPAD = NG * GN + TAILN
BK = 8
NS = GW // BK
OHR = 4
HR = 20
HLO = 64
HHI = NT * P // HLO
NEXP, H, RH = 6, 256, 128
UN = 512
UT = UN // P
UMAX = (2 * N - NEXP) // UN + NEXP
UMIN = -(-2 * N // UN)
SC = UMAX * UT
MB = 10
FW = D + NEXP
NRAW = 2 * NEXP + 6
EPS = 1e-5
XSCALE = 256.0


def build(nc, x, src, dst, W, bias, gamma, beta, rw1, rb1, rw2, rb2, w1, b1, w2, b2, w3, b3, out):
    ctx, ctx1, ctx2 = ExitStack(), ExitStack(), ExitStack()
    with ctx:
        def sb(name, shape, dt, scope=ctx):
            return scope.enter_context(nc.sbuf_tensor(name, shape, dt))

        def ps(name, shape, scope=ctx, dt=fp32):
            return scope.enter_context(nc.psum_tensor(name, shape, dt))

        def sem(name):
            return ctx.enter_context(nc.semaphore(name))

        keys_d = nc.dram_tensor("keys_d", [(E + CAP) * 2], fp32, kind="Internal").ap()
        xs_d = nc.dram_tensor("xs_d", [NT * P, D], fp32, kind="Internal").ap()

        xx = sb("xx", [P, NT, D], fp32)
        agg = sb("agg", [P, NT * D], fp32)
        xn = agg[:, :].rearrange("p (t d) -> p t d", t=NT)
        stats = sb("stats", [P, DH, NG + 1, 6], fp32)
        identf = sb("identf", [P, P], fp32)
        nmr = sb("nmr", [P, NT], fp32)
        eps1 = sb("eps1", [P, 1], fp32)
        gammaT, betaT = sb("gammaT", [P, DH], fp32), sb("betaT", [P, DH], fp32)
        rb1T, rw2s, rb2b, rw1s = sb("rb1T", [P, 1], fp32), sb("rw2s", [RH, NEXP], fp32), sb("rb2b", [P, NEXP], fp32), sb("rw1s", [P, DH, RH], fp32)
        b12T = sb("b12T", [P, NEXP, 2, DH], fp32)
        b3b = sb("b3b", [P, NEXP, D], fp32)
        t_gb, t_w, t_raw = sem("gamma_beta_loaded"), sem("small_weights_loaded"), sem("expert_weights_loaded")

        C = sb("C", [P, 2, NT, GN], fp16, ctx1)
        xs = sb("xs", [P, 2, NT, D], fp16, ctx1)
        oh_src = sb("oh_src", [P, OHR, KCH, P], fp16, ctx1)
        oh_key = sb("oh_key", [P, OHR, KCH, CNT], fp16, ctx1)
        ekeys = sb("ekeys", [P, NS, BK, KCH, 2], fp32, ctx1)
        wkeys = sb("wkeys", [P, NS, BK, KCH], fp32, ctx1)
        dinvb = sb("dinvb", [P, NT * P], fp32, ctx1)
        zbuf = sb("zbuf", [P, DH, GN], fp32, ctx1)
        ubuf = sb("ubuf", [P, DH, GN], fp32, ctx1)
        wgcn = sb("wgcn", [P, DH, D], fp32, ctx1)
        biasT = sb("biasT", [P, DH], fp32, ctx1)
        iota_i = sb("iota_i", [P, GN], i32, ctx1)
        iota_h = sb("iota_h", [P, CNT], fp16, ctx1)
        win_i = sb("win_i", [P, NG * GW + TAILW], i32, ctx1)
        win_off = sb("win_off", [P, NG * GW + TAILW], fp32, ctx1)
        diff_i = sb("diff_i", [P, P], i32, ctx1)
        mask_i = sb("mask_i", [P, 8], i32, ctx1)
        ident16 = sb("ident16", [P, P], fp16, ctx1)
        below = sb("below", [P, 8], fp32, ctx1)
        upper = sb("upper", [NT, NT], fp32, ctx1)
        ones = sb("ones", [P, P], fp32, ctx1)
        srci = sb("srci", [EP, EC], i32, ctx1)
        dsti = sb("dsti", [EP, EC], i32, ctx1)
        nexti = sb("nexti", [EP, EC], i32, ctx1)
        ti = sb("ti", [EP, 4, EC], i32, ctx1)
        dstlo = sb("dstlo", [EP, EC], fp16, ctx1)
        dsthi = sb("dsthi", [EP, EC], fp16, ctx1)
        pack = sb("pack", [EP, EC, 2], fp32, ctx1)
        padk = sb("padk", [P, 6], fp32, ctx1)
        desc = sb("desc", [EP, EC], fp32, ctx1)
        descs = sb("descs", [EP, 1], fp32, ctx1)
        mv = sb("mv", [P, NT, 2], fp32, ctx1)
        st6 = sb("st6", [P, NT, 6], fp32, ctx1)
        rstd = sb("rstd", [P, NT], fp32, ctx1)
        deg = sb("deg", [P, NT], fp32, ctx1)
        dinv = sb("dinv", [P, NT], fp32, ctx1)
        dinvs = sb("dinvs", [P, NT], fp32, ctx1)
        total = sb("total", [NT, 1], fp32, ctx1)
        rowf = sb("rowf", [1, NT * 8], fp32, ctx1)
        over = sb("over", [1, NT * 8 - 1], fp32, ctx1)
        overs = sb("overs", [1, 1], fp32, ctx1)
        row = sb("row", [1, NT * 8], i32, ctx1)
        flag = sb("flag", [1, 1], i32, ctx1)
        degr = sb("degr", [P, NT], fp32, ctx1)
        dinvz = sb("dinvz", [P, NT], fp32, ctx1)
        dstf = sb("dstf", [EP, EC], fp32, ctx1)
        goff_i = sb("goff_i", [P, NG + 1], i32, ctx1)
        gkey = sb("gkey", [EP, 1], fp32, ctx1)
        gidx = sb("gidx", [EP, 1], i32, ctx1)
        diag4 = C[:, 1, :, :].rearrange("p a b -> p (a b)").bitcast(fp32)[:, 0:(NG + 1) * GN].rearrange("p (g n) -> p g n", n=GN)
        gen_oh = C[0:EP, 0, :, :].rearrange("p a b -> p (a b)").bitcast(fp32)[:, 0:GN]
        gen_xs = C[:, 1, :, :].rearrange("p a b -> p (a b)").bitcast(fp32)
        gen_rows = ubuf[0:EP, 0, 0:D]
        hist = C[0:EP, 0, :, :].rearrange("p a b -> p (a b)")
        hist_lo = hist[:, 0:2 * HR * HLO].rearrange("p (s r n) -> p s r n", s=2, n=HLO)
        hist_hi = hist[:, 2 * HR * HLO:2 * HR * (HLO + HHI)].rearrange("p (s r n) -> p s r n", s=2, n=HHI)

        psC = [ps(f"psC{i}", [P, 512], ctx1) for i in range(4)]
        psZ = [ps(f"psZ{i}", [P, 512], ctx1) for i in range(2)]
        psY = [ps(f"psY{i}", [P, 512], ctx1) for i in range(2)]

        s_dst, s_edge, s_x, s_wt, s_cst = sem("dst_loaded"), sem("edges_loaded"), sem("x_loaded"), sem("weights_loaded"), sem("constants_ready")
        s_dve = sem("dve_step")
        s_packed, s_keys = sem("keys_packed"), sem("keys_in_dram")
        s_hoh, s_hmm = sem("degree_onehots_ready"), sem("degree_chunks_done")
        s_deg, s_cum, s_pref, s_flagmm = sem("deg_ready"), sem("cum_done"), sem("prefix_done"), sem("flag_done")
        s_cumsb, s_row, s_over = sem("totals_in_sbuf"), sem("window_starts_ready"), sem("full_windows_counted")
        s_flag = sem("flag_ready")
        s_var, s_std, s_rstd, s_xn, s_sqd = sem("var_ready"), sem("std_ready"), sem("rstd_ready"), sem("xn_ready"), sem("sqrt_deg_ready")
        s_pool = sem("pool_step")
        s_dinv, s_xhi, s_xs = sem("dinv_ready"), sem("xs_hi_ready"), sem("xs_ready")
        s_diag, s_dbmm, s_dinvb = sem("diag_ready"), sem("dinv_row_done"), sem("dinv_row_ready")
        s_turn = sem("key_loads_turn")
        s_ek = [sem(f"edge_keys_loaded{i}") for i in range(NS)]
        s_wk = sem("window_keys_ready")
        s_oh, s_cnt, s_cev = sem("onehots_ready"), sem("counts_done"), sem("counts_evicted")
        s_z, s_zev, s_y, s_yev, s_agg = sem("z_done"), sem("z_evicted"), sem("y_done"), sem("y_evicted"), sem("agg_ready")
        s_stat = sem("stats_ready")
        g_zero, g_xst, g_xsd = sem("gen_z_zeroed"), sem("gen_xs_staged"), sem("gen_xs_in_dram")
        g_row, g_oh, g_mm, g_add, g_y, g_u, g_idx, g_idx2 = (sem("gen_rows_gathered"), sem("gen_onehot_ready"), sem("gen_product_done"),
                                              sem("gen_z_added"), sem("gen_y_done"), sem("gen_u_ready"), sem("gen_index_ready"), sem("gen_key_ready"))

        g_turn = sem("gen_turn")
        windows = NG * GW + TAILW

        def parity(g):
            return g % 2 if isinstance(g, int) else bass.ds(g % 2, 1)

        def agg_at(g, m, cols):
            return agg[:, bass.ds(GN * g + m * NPAD, cols)]

        block = ctx1.enter_context(nc.Block())

        @block.sync
        def _(sp):
            sp.dma_start(dsti[:], dst.rearrange("(p c) -> p c", p=EP)).then_inc(s_dst, 16)
            sp.dma_start(srci[:], src.rearrange("(p c) -> p c", p=EP)).then_inc(s_edge, 16)
            sp.dma_start(nexti[0:EP - 1, :], dst[1:1 + (EP - 1) * EC].rearrange("(p c) -> p c", p=EP - 1)).then_inc(s_edge, 16)
            sp.dma_start(nexti[EP - 1:EP, 0:EC - 1], dst[1 + (EP - 1) * EC:E].rearrange("(p c) -> p c", p=1)).then_inc(s_edge, 16)
            sp.dma_start(nexti[EP - 1:EP, EC - 1:EC], dst[E - 1:E].rearrange("(p c) -> p c", p=1)).then_inc(s_edge, 16)
            sp.dma_start(wgcn[:], W.rearrange("(k p) n -> p k n", p=P)).then_inc(s_wt, 16)
            with nc.allow_non_contiguous_dma(reason="bias, one value per partition"):
                sp.dma_start(biasT[:], bias.rearrange("(k p) -> p k", p=P)).then_inc(s_wt, 16)
            sp.wait_ge(s_packed, 2)
            sp.dma_start(keys_d[0:2 * E].rearrange("(p c) -> p c", p=EP), pack[:].rearrange("p c k -> p (c k)")).then_inc(s_keys, 16)
            sp.dma_start(keys_d[2 * E:2 * (E + CAP)].rearrange("(p c) -> p c", p=P), padk[:]).then_inc(s_keys, 16)
            sp.wait_ge(s_keys, 32)
            sp.wait_ge(s_row, 1)

            def load_keys(first, count, slot):
                for w in range(count):
                    at = sp.value_load(row[0:1, bass.ds(first + w, 1)], min_val=0, max_val=2 * E)
                    sp.dma_start(ekeys[:, slot, w, :, :].rearrange("p k c -> p (k c)"),
                                 keys_d[bass.ds(at, 2 * CAP)].rearrange("(p c) -> p c", p=P)).then_inc(s_ek[slot], 16)

            for slot in range(NS):
                load_keys(BK * slot, BK, slot)
            with sp.Fori(1, NG) as g:
                for slot in range(NS):
                    sp.wait_ge(s_oh, GW * (g - 1) + BK * (slot + 1))
                    sp.sem_inc(s_turn, 1)
                    load_keys(GW * g + BK * slot, BK, slot)
            sp.wait_ge(s_oh, GW * (NG - 1) + BK)
            load_keys(GW * NG, TAILW, 0)
            with nc.allow_non_contiguous_dma(reason="one value per partition"):
                sp.dma_start(gammaT[:], gamma.rearrange("(k p) -> p k", p=P)).then_inc(t_gb, 16)
                sp.dma_start(betaT[:], beta.rearrange("(k p) -> p k", p=P)).then_inc(t_gb, 16)
                sp.dma_start(rb1T[:], rb1.rearrange("(k p) -> p k", p=P)).then_inc(t_w, 16)
                sp.dma_start(rw1s[:], rw1.rearrange("(k p) n -> p k n", p=P)).then_inc(t_w, 16)
                sp.dma_start(rw2s[:], rw2).then_inc(t_w, 16)
                sp.dma_start(rb2b[:], rb2.rearrange("(o n) -> o n", o=1).to_broadcast([P, NEXP])).then_inc(t_w, 16)
                for layer, b in enumerate((b1, b2)):
                    for m in range(DH):
                        sp.dma_start(b12T[:, :, layer, m], b[:, P * m:P * m + P].rearrange("e p -> p e")).then_inc(t_raw, 16)
            sp.dma_start(b3b[:].rearrange("p e d -> p (e d)"), b3.rearrange("(o e) d -> o (e d)", o=1).to_broadcast([P, NEXP * D])).then_inc(t_raw, 16)

        @block.gpsimd
        def _(gp):
            nc.gpsimd.iota(iota_i[:], pattern=[[1, GN]], base=0, channel_multiplier=0)
            nc.gpsimd.iota(diff_i[:], pattern=[[1, P]], base=0, channel_multiplier=-1)
            nc.gpsimd.iota(mask_i[:], pattern=[[WIN, 8]], base=0, channel_multiplier=-1)
            nc.gpsimd.iota(goff_i[:], pattern=[[-GN, NG + 1]], base=0, channel_multiplier=0)
            nc.gpsimd.iota(win_i[:], pattern=[[CNT, windows]], base=0, channel_multiplier=0).then_inc(s_cst, 1)
            for t in range(NT):
                gp.wait_ge(s_pool, t + 1)
                nc.gpsimd.tensor_tensor(xx[:, t, :], xx[:, t, :], xn[:, t, :], ALU.add).then_inc(s_xn, 1)

            gp.wait_ge(s_flag, 1)
            general = gp.value_load(flag[0:1, 0:1], min_val=0, max_val=2 * E)
            with gp.If(general > 0):
                gp.wait_ge(g_xst, 1)
                gp.dma_start(xs_d.rearrange("(t p) d -> p t d", p=P), gen_xs[:, :].rearrange("p (t d) -> p t d", t=NT)).then_inc(g_xsd, 16)
                gp.wait_ge(g_xsd, 16)
                with gp.Fori(0, NG + 1) as g:
                    with gp.Fori(0, EC) as c:
                        gp.wait_ge(g_add, (EC + 1) * g + c + 1)
                        nc.gpsimd.tensor_copy(gidx[:], srci[:, bass.ds(c, 1)]).then_inc(g_idx, 1)
                        gp.wait_ge(g_idx, EC * g + c + 1)
                        gp.sem_inc(g_turn, 1)
                        gp.indirect_dma_start(out=gen_rows, out_offset=None, in_=xs_d[:, :],
                                              in_offset=bass.IndirectOffsetOnAxis(ap=gidx[:, 0:1], axis=0)).then_inc(g_row, 16)

        @block.scalar
        def _(act):
            act.dma_start(xx[:, 0:FULL, :], x[0:FULL * P, :].rearrange("(t p) d -> p t d", p=P)).then_inc(s_x, 16)
            act.wait_ge(s_cst, 2)
            act.dma_start(xx[0:LAST, FULL, :], x[FULL * P:N, :]).then_inc(s_x, 16)
            act.wait_ge(s_var, 1)
            nc.scalar.activation(rstd[:], mv[:, :, 1], ACT.Sqrt, bias=eps1[:]).then_inc(s_std, 1)
            act.wait_ge(s_rstd, 1)
            for t in range(NT):
                nc.scalar.activation(xn[:, t, :], xx[:, t, :], ACT.Identity, bias=nmr[:, t:t + 1], scale=rstd[:, t:t + 1]).then_inc(s_pool, 1)
            act.wait_ge(s_deg, 1)
            nc.scalar.activation(dinv[:], deg[:], ACT.Sqrt).then_inc(s_sqd, 1)
            for g in range(NG + 1):
                act.wait_ge(s_dbmm, g + 1)
                cols = GN if g < NG else P
                nc.scalar.activation(dinvb[:, GN * g:GN * g + cols], psZ[g % 2][:, 0:cols], ACT.Copy).then_inc(s_dinvb, 1)

            def evict_z(g, h, cols):
                act.wait_ge(s_z, 2 * g + h + 1)
                nc.scalar.activation(zbuf[:, h, 0:cols], psZ[h][:, 0:cols], ACT.Copy).then_inc(s_zev, 1)

            def add_bias(g, cols):
                for m in range(DH):
                    act.wait_ge(s_yev, 2 * g + m + 1)
                    at = agg_at(g, m, cols)
                    nc.scalar.activation(at, ubuf[:, m, 0:cols], ACT.Identity, bias=biasT[:, m:m + 1]).then_inc(s_agg, 1)

            def step(g, wins, sums, lagged, cols, zcols=GN):
                for w in range(wins):
                    act.wait_ge(s_cnt, GW * g + w + 1)
                    nc.scalar.activation(C[:, parity(g), :, WIN * w:WIN * w + WIN],
                                         psC[w % 4][:, 0:CNT].rearrange("p (s n) -> p s n", s=NT), ACT.Copy).then_inc(s_cev, 1)
                    if isinstance(g, int) and g == 0 and w < NT:
                        if w == 0:
                            act.wait_ge(s_dinv, 1)
                            act.wait_ge(s_pool, NT)
                        nc.scalar.activation(xs[:, 0, w, :], xn[:, w, :], ACT.Copy, scale=dinvs[:, w:w + 1]).then_inc(s_xhi, 1)
                    if w == 12 and lagged:
                        add_bias(g - 2, GN)
                    if sums and w == 17:
                        if lagged:
                            act.wait_ge(s_y, 2 * (g - 1))
                        evict_z(g - 1, 0, zcols)
                    if lagged and w == 1:
                        evict_z(g - 2, 1, GN)
                if wins < GW:
                    add_bias(g - 2, GN)
                    act.wait_ge(s_y, 2 * (g - 1))
                    evict_z(g - 1, 0, zcols)
                    evict_z(g - 1, 1, zcols)

            step(0, GW, False, False, GN)
            step(1, GW, True, False, GN)
            act.wait_ge(s_xs, NT)
            act.wait_ge(s_xn, NT)
            with act.Fori(2, NG) as g:
                step(g, GW, True, True, GN)
            step(NG, TAILW, True, True, GN)
            step(NG + 1, 0, True, True, GN, TAILN)
            add_bias(NG, TAILN)


        @block.vector
        def _(dve):
            chain = [0]

            def link(ins):
                chain[0] += 1
                ins.then_inc(s_dve, 1)
                dve.wait_ge(s_dve, chain[0])

            nc.vector.memset(eps1[:], EPS)
            nc.vector.memset(ones[:], 1.0)
            nc.vector.memset(padk[:], -float(CNT * (windows + 1)))
            nc.vector.memset(xx[:, FULL, :], 0.0).then_inc(s_cst, 1)
            dve.wait_ge(s_cst, 2)
            nc.vector.tensor_copy(iota_h[:], iota_i[:, 0:CNT])
            nc.vector.tensor_copy(win_off[:], win_i[:])
            nc.vector.tensor_scalar(ident16[:], diff_i[:], 0.0, None, ALU.is_equal)
            nc.vector.tensor_scalar(identf[:], diff_i[:], 0.0, None, ALU.is_equal)
            nc.vector.tensor_scalar(below[:], mask_i[:], 0.0, None, ALU.is_gt)
            nc.vector.tensor_scalar(upper[:], diff_i[0:NT, 0:NT], 0.0, None, ALU.is_gt)
            dve.wait_ge(s_dst, 16)
            nc.vector.tensor_scalar(ti[:, 0, :], dsti[:], HLO - 1, None, ALU.bitwise_and)
            link(nc.vector.tensor_scalar(ti[:, 1, :], dsti[:], 6, None, ALU.logical_shift_right))
            nc.vector.tensor_copy(dstlo[:], ti[:, 0, :])
            link(nc.vector.tensor_copy(dsthi[:], ti[:, 1, :]))
            dve.wait_ge(s_edge, 64)
            nc.vector.tensor_scalar(ti[:, 0, :], srci[:], 7, 4, ALU.logical_shift_right, ALU.logical_shift_left)
            nc.vector.tensor_scalar(ti[:, 1, :], dsti[:], 4, None, ALU.logical_shift_right)
            nc.vector.tensor_scalar(ti[:, 2, :], dsti[:], WIN - 1, None, ALU.bitwise_and)
            link(nc.vector.tensor_scalar(ti[:, 3, :], srci[:], P - 1, None, ALU.bitwise_and))
            nc.vector.tensor_copy(pack[:, :, 0], ti[:, 3, :]).then_inc(s_packed, 1)
            link(nc.vector.scalar_tensor_tensor(dstf[:], ti[:, 1, :], float(CNT), ti[:, 0, :], ALU.mult, ALU.add))
            nc.vector.tensor_tensor(pack[:, :, 1], dstf[:], ti[:, 2, :], ALU.add).then_inc(s_packed, 1)
            dve.wait_ge(s_x, 32)
            for t in range(NT):
                last = nc.vector.bn_stats(st6[:, t, :], xx[:, t, :])
            link(last)
            for t in range(NT):
                last = nc.vector.bn_aggr(mv[:, t, :], st6[:, t, :])
            last.then_inc(s_var, 1)

            def degree(i, slot, first):
                if not first:
                    dve.wait_ge(s_hmm, 2 * i + slot - 1)
                at = bass.ds(2 * HR * i + HR * slot, HR)
                nc.vector.tensor_tensor(hist_lo[:, slot], iota_h[0:EP, 0:HLO].unsqueeze(1).to_broadcast([EP, HR, HLO]),
                                        dstlo[:, at].unsqueeze(2).to_broadcast([EP, HR, HLO]), ALU.is_equal)
                nc.vector.tensor_tensor(hist_hi[:, slot], iota_h[0:EP, 0:HHI].unsqueeze(1).to_broadcast([EP, HR, HHI]),
                                        dsthi[:, at].unsqueeze(2).to_broadcast([EP, HR, HHI]), ALU.is_equal).then_inc(s_hoh, 1)

            degree(0, 0, True)
            degree(0, 1, True)
            dve.wait_ge(s_std, 1)
            link(nc.vector.reciprocal(rstd[:], rstd[:]))
            nc.vector.scalar_tensor_tensor(nmr[:], mv[:, :, 0], -1.0, rstd[:], ALU.mult, ALU.mult).then_inc(s_rstd, 1)
            with dve.Fori(1, EC // HR // 2) as i:
                degree(i, 0, False)
                degree(i, 1, False)
            dve.wait_ge(s_hmm, EC // HR)
            counts = psC[0][0:HLO, 0:HHI].rearrange("p (t k) -> p k t", k=2)
            nc.vector.tensor_copy(degr[0:HLO, :], counts[:, 0, :])
            link(nc.vector.tensor_copy(degr[HLO:P, :], counts[:, 1, :]))
            nc.vector.tensor_scalar(deg[:], degr[:], 1.0, 1.0, ALU.add, ALU.max).then_inc(s_deg, 1)
            dve.wait_ge(s_cum, 1)
            nc.vector.tensor_copy(total[:], psY[0][0:NT, 0:1]).then_inc(s_cumsb, 1)
            dve.wait_ge(s_pref, 1)
            nc.vector.tensor_scalar(row[:], psY[1][0:1, 0:NT * 8], 2.0, None, ALU.mult).then_inc(s_row, 1)
            link(nc.vector.tensor_copy(rowf[:], psY[1][0:1, 0:NT * 8]))
            link(nc.vector.tensor_tensor(over[:], rowf[:, 1:NT * 8], rowf[:, 0:NT * 8 - 1], ALU.subtract))
            link(nc.vector.tensor_scalar(over[:], over[:], float(CAP), None, ALU.is_gt))
            nc.vector.reduce_sum(overs[:], over[:], AX.X)
            link(nc.vector.tensor_tensor(desc[:], dsti[:], nexti[:], ALU.is_gt))
            nc.vector.reduce_sum(descs[:], desc[:], AX.X).then_inc(s_over, 1)
            nc.vector.tensor_copy(dstf[:], dsti[:])
            dve.wait_ge(s_sqd, 1)
            link(nc.vector.reciprocal(dinv[:], dinv[:]))
            nc.vector.tensor_scalar(dinvz[:], dinv[:], 1.0 / XSCALE, None, ALU.mult)
            link(nc.vector.tensor_scalar(dinvs[:], dinv[:], XSCALE, None, ALU.mult))
            for g in range(NG + 1):
                k = 4 if g < NG else 1
                ins = nc.vector.tensor_tensor(diag4[:, g, 0:k * P].rearrange("p (k n) -> p k n", k=k),
                                              identf[:].unsqueeze(1).to_broadcast([P, k, P]),
                                              dinvz[:, 4 * g:4 * g + k].unsqueeze(2).to_broadcast([P, k, P]), ALU.mult)
                ins.then_inc(s_diag, 1)
            dve.wait_ge(s_diag, 1)
            nc.vector.memset(gkey[:], 0.0).then_inc(s_dinv, 1)
            dve.wait_ge(s_flagmm, 1)
            nc.vector.tensor_copy(flag[:], psY[0][0:1, 16:17]).then_inc(s_flag, 1)

            def neighbour_u(g, cols):
                for m in range(DH):
                    dve.wait_ge(s_y, 2 * g + m + 1)
                    nc.vector.tensor_tensor(ubuf[:, m, 0:cols], psY[m][:, 0:cols], dinvb[:, bass.ds(GN * g, cols)],
                                            ALU.mult).then_inc(s_yev, 1)

            def norm_stats(g, cols):
                for m in range(DH):
                    dve.wait_ge(s_agg, 2 * g + m + 1)
                    nc.vector.bn_stats(stats[:, m, bass.ds(g, 1), :].rearrange("p a b -> p (a b)"), agg_at(g, m, cols)).then_inc(s_stat, 1)

            def step(g, wins, lagged):
                for w in range(wins):
                    at, slot = GW * g + w, w // BK
                    if w % BK == 0:
                        n = min(BK, wins)
                        dve.wait_ge(s_ek[slot], 16 * BK * g + 16 * n)
                        if not (isinstance(g, int) and g == 0):
                            dve.wait_ge(s_oh, GW * (g - 1) + BK * (slot + 1))
                        nc.vector.tensor_tensor(wkeys[:, slot, 0:n, :], ekeys[:, slot, 0:n, :, 1],
                                                win_off[:, bass.ds(at, n)].unsqueeze(2).to_broadcast([P, n, KCH]),
                                                ALU.subtract).then_inc(s_wk, 1)
                        dve.wait_ge(s_wk, NS * g + slot + 1)
                    if not (isinstance(g, int) and g == 0 and w < OHR):
                        dve.wait_ge(s_cnt, at - OHR + 1)
                    r = w % OHR
                    for k in range(KCH):
                        nc.vector.tensor_scalar(oh_src[:, r, k, :], iota_h[:, 0:P], ekeys[:, slot, w % BK, k, 0:1], None, ALU.is_equal)
                        last = nc.vector.tensor_scalar(oh_key[:, r, k, :], iota_h[:], wkeys[:, slot, w % BK, k:k + 1], None, ALU.is_equal)
                    last.then_inc(s_oh, 1)
                    if isinstance(g, int) and g == 0 and 4 <= w < NT + 4:
                        t = w - 4
                        dve.wait_ge(s_xhi, t + 1)
                        nc.vector.scalar_tensor_tensor(xs[:, 1, t, :], xn[:, t, :], dinvs[:, t:t + 1], xs[:, 0, t, :],
                                                       ALU.mult, ALU.subtract).then_inc(s_xs, 1)
                    if lagged and w == 8:
                        neighbour_u(g - 2, GN)
                    if lagged and w == 16:
                        norm_stats(g - 2, GN)
                if lagged and wins < GW:
                    neighbour_u(g - 2, GN)
                    norm_stats(g - 2, GN)

            step(0, GW, False)
            step(1, GW, False)
            with dve.Fori(2, NG) as g:
                step(g, GW, True)
            step(NG, TAILW, True)
            step(NG + 1, 0, True)
            neighbour_u(NG, TAILN)
            norm_stats(NG, N - NG * GN)

            general = dve.value_load(flag[0:1, 0:1], min_val=0, max_val=2 * E)
            with dve.If(general > 0):
                dve.wait_ge(s_stat, 2 * (NG + 1))
                nc.vector.tensor_tensor(gen_xs[:, :], xs[:, 0, :, :].rearrange("p t d -> p (t d)"),
                                        xs[:, 1, :, :].rearrange("p t d -> p (t d)"), ALU.add).then_inc(g_xst, 1)

                def gen_group(g, cols, valid):
                    base = (EC + 1) * g
                    dve.wait_ge(g_mm, base + 1)
                    nc.vector.tensor_copy(zbuf[:, 0, 0:cols], psZ[0][:, 0:cols])
                    nc.vector.tensor_copy(zbuf[:, 1, 0:cols], psZ[1][:, 0:cols]).then_inc(g_add, 1)
                    with dve.Fori(0, EC) as c:
                        dve.wait_ge(g_add, base + c + 1)
                        nc.vector.tensor_tensor(gkey[:], dstf[:, bass.ds(c, 1)], goff_i[0:EP, bass.ds(g, 1)], ALU.add).then_inc(g_idx2, 1)
                        dve.wait_ge(g_idx2, EC * g + c + 1)
                        nc.vector.tensor_scalar(gen_oh[:, 0:cols], iota_i[0:EP, 0:cols], gkey[:, 0:1], None, ALU.is_equal).then_inc(g_oh, 1)
                        dve.wait_ge(g_mm, base + c + 2)
                        nc.vector.tensor_tensor(zbuf[:, 0, 0:cols], zbuf[:, 0, 0:cols], psZ[0][:, 0:cols], ALU.add)
                        nc.vector.tensor_tensor(zbuf[:, 1, 0:cols], zbuf[:, 1, 0:cols], psZ[1][:, 0:cols], ALU.add).then_inc(g_add, 1)
                    dve.wait_ge(g_y, 2 * g + 2)
                    for m in range(DH):
                        at = agg_at(g, m, cols)
                        nc.vector.tensor_tensor(at, psY[m][:, 0:cols], dinvb[:, bass.ds(GN * g, cols)], ALU.mult).then_inc(g_u, 1)
                        dve.wait_ge(g_u, 4 * g + 2 * m + 1)
                        nc.vector.tensor_scalar(at, at, biasT[:, m:m + 1], None, ALU.add).then_inc(g_u, 1)
                        dve.wait_ge(g_u, 4 * g + 2 * m + 2)
                        nc.vector.bn_stats(stats[:, m, bass.ds(g, 1), :].rearrange("p a b -> p (a b)"), agg_at(g, m, valid))

                with dve.Fori(0, NG) as g:
                    gen_group(g, GN, GN)
                gen_group(NG, TAILN, N - NG * GN)

        @block.tensor
        def _(pe):
            def degree(i, slot, first, final):
                pe.wait_ge(s_hoh, 2 * i + slot + 1)
                for r in range(HR):
                    last = nc.tensor.matmul(psC[0][0:HLO, 0:HHI], hist_lo[:, slot, r, :], hist_hi[:, slot, r, :],
                                            start=(first and r == 0), stop=(final and r == HR - 1))
                last.then_inc(s_hmm, 1)

            degree(0, 0, True, False)
            degree(0, 1, False, False)
            with pe.Fori(1, EC // HR // 2 - 1) as i:
                degree(i, 0, False, False)
                degree(i, 1, False, False)
            degree(EC // HR // 2 - 1, 0, False, False)
            degree(EC // HR // 2 - 1, 1, False, True)
            pe.wait_ge(s_deg, 1)
            nc.tensor.matmul(psY[0][0:NT, 0:1], degr[:], ones[:, 0:1], start=True, stop=True).then_inc(s_cum, 1)
            starts = psY[1][0:1, 0:NT * 8].rearrange("p (t j) -> p j t", j=8)
            for j in range(8):
                nc.tensor.matmul(starts[:, j, :], below[:, j:j + 1], degr[:], start=(j == 0), stop=False)
            pe.wait_ge(s_cumsb, 1)
            for j in range(8):
                last = nc.tensor.matmul(starts[:, j, :], total[:], upper[:], start=False, stop=(j == 7))
            last.then_inc(s_pref, 1)
            pe.wait_ge(s_over, 1)
            nc.tensor.matmul(psY[0][0:1, 16:17], descs[:], ones[0:EP, 0:1], start=True, stop=False)
            nc.tensor.matmul(psY[0][0:1, 16:17], overs[:], ones[0:1, 0:1], start=False, stop=True).then_inc(s_flagmm, 1)
            for g in range(NG + 1):
                cols = GN if g < NG else P
                pe.wait_ge(s_diag, g + 1)
                if g >= 2:
                    pe.wait_ge(s_dinvb, g - 1)
                nc.tensor.matmul(psZ[g % 2][:, 0:cols], ones[:], diag4[:, g, 0:cols], start=True, stop=True).then_inc(s_dbmm, 1)
            pe.wait_ge(s_dinvb, NG + 1)

            def sum_parts(g, h, cols, tiles):
                parts = [(p, s) for p in range(2) for s in range(NT)]
                for i, (p, s) in enumerate(parts):
                    yield dict(out=psZ[h][:, 0:cols], lhsT=xs[:, p, s, P * h:P * h + P], rhs=C[:, parity(g), s, 0:cols],
                               start=(i == 0), stop=False)
                for j in range(tiles):
                    n = min(P, cols - P * j)
                    for p in range(2):
                        t = bass.ds(4 * g + j, 1)
                        yield dict(out=psZ[h][:, P * j:P * j + n],
                                   lhsT=xs[:, p, t, P * h:P * h + P].rearrange("p a b -> p (a b)") if not isinstance(g, int) else xs[:, p, 4 * g + j, P * h:P * h + P],
                                   rhs=ident16[:, 0:n], start=False, stop=(j == tiles - 1 and p == 1))

            def products(g, cols, done=s_y):
                for m in range(DH):
                    for k in range(DH):
                        last = nc.tensor.matmul(psY[m][:, 0:cols], wgcn[:, k, P * m:P * m + P], zbuf[:, k, 0:cols],
                                                start=(k == 0), stop=(k == DH - 1))
                    last.then_inc(done, 1)

            def run(todo, n):
                for _ in range(n):
                    m = next(todo, None)
                    if m is None:
                        return
                    final = m["stop"]
                    ins = nc.tensor.matmul(m["out"], m["lhsT"], m["rhs"], start=m["start"], stop=m["stop"])
                    if final:
                        ins.then_inc(s_z, 1)

            def step(g, wins, sums, lagged, third=True, cols=GN, tiles=4):
                todo = [iter(())] * 2
                if sums:
                    todo = [sum_parts(g - 1, h, cols, tiles) for h in range(DH)]
                for w in range(wins):
                    pe.wait_ge(s_oh, GW * g + w + 1)
                    if not (isinstance(g, int) and g == 0 and w < 4):
                        pe.wait_ge(s_cev, GW * g + w - 3)
                    for k in range(KCH):
                        last = nc.tensor.matmul(psC[w % 4][:, 0:CNT], oh_src[:, w % OHR, k, :], oh_key[:, w % OHR, k, :],
                                                start=(k == 0), stop=(k == KCH - 1))
                    last.then_inc(s_cnt, 1)
                    if sums and w == 1:
                        pe.wait_ge(s_cev, GW * g)
                        pe.wait_ge(s_zev, 2 * g - 3) if lagged else pe.wait_ge(s_xs, NT)
                    if sums and 1 <= w < 16:
                        run(todo[0], 4)
                    if lagged and w == 3:
                        pe.wait_ge(s_zev, 2 * (g - 1))
                        if third:
                            pe.wait_ge(s_yev, 2 * (g - 2))
                        products(g - 2, GN)
                    if sums and w >= 16:
                        run(todo[1], 4)
                if 0 < wins < GW:
                    run(todo[0], 1000)
                    run(todo[1], 1000)
                if wins == 0:
                    pe.wait_ge(s_zev, 2 * (g - 1))
                    pe.wait_ge(s_yev, 2 * (g - 2))
                    products(g - 2, GN)
                    pe.wait_ge(s_cev, NG * GW + TAILW)
                    run(todo[0], 1000)
                    run(todo[1], 1000)
                    pe.wait_ge(s_zev, 2 * g)
                    pe.wait_ge(s_yev, 2 * (g - 1))
                    products(g - 1, cols)

            pe.wait_ge(s_wt, 32)
            step(0, GW, False, False)
            step(1, GW, True, False)
            step(2, GW, True, True, False)
            with pe.Fori(3, NG) as g:
                step(g, GW, True, True)
            step(NG, TAILW, True, True)
            step(NG + 1, 0, True, True, True, TAILN, 1)

            general = pe.value_load(flag[0:1, 0:1], min_val=0, max_val=2 * E)
            with pe.If(general > 0):
                def gen_group(g, cols, tiles):
                    base = (EC + 1) * g
                    for h in range(DH):
                        for j in range(tiles):
                            n = min(P, cols - P * j)
                            for p in range(2):
                                t = bass.ds(4 * g + j, 1)
                                last = nc.tensor.matmul(psZ[h][:, P * j:P * j + n], xs[:, p, t, P * h:P * h + P].rearrange("p a b -> p (a b)"),
                                                        ident16[:, 0:n], start=(p == 0 and j == 0), stop=(j == tiles - 1 and p == 1))
                    last.then_inc(g_mm, 1)
                    with pe.Fori(0, EC) as c:
                        pe.wait_ge(g_row, 16 * (EC * g + c) + 16)
                        pe.wait_ge(g_oh, EC * g + c + 1)
                        for h in range(DH):
                            last = nc.tensor.matmul(psZ[h][:, 0:cols], gen_rows[:, P * h:P * h + P], gen_oh[:, 0:cols], start=True, stop=True)
                        last.then_inc(g_mm, 1)
                    pe.wait_ge(g_add, base + EC + 1)
                    products(g, cols, g_y)

                pe.wait_ge(g_xst, 1)
                with pe.Fori(0, NG) as g:
                    gen_group(g, GN, 4)
                gen_group(NG, TAILN, 1)

        ctx1.close()

        wraw12 = sb("wraw12", [P, NEXP, 2, DH, D], fp32, ctx2)
        wraw3 = sb("wraw3", [P, NEXP, DH, D], fp32, ctx2)
        w12h, w12l = (sb(n, [P, 2, 2, DH, D], f32r, ctx2) for n in ("w12h", "w12l"))
        w3h, w3l = (sb(n, [P, 2, DH, D], f32r, ctx2) for n in ("w3h", "w3l"))
        frows = sb("frows", [P, 2, UT, FW], fp32, ctx2)
        fuh, ful = (sb(n, [P, DH, UN], f32r, ctx2) for n in ("fuh", "ful"))
        r1, r2 = (sb(n, [P, DH, UN], fp32, ctx2) for n in ("r1", "r2"))
        h1h, h1l, h2h, h2l = (sb(n, [P, DH, UN], f32r, ctx2) for n in ("h1h", "h1l", "h2h", "h2l"))
        ybuf = sb("ybuf", [P, 2, UT, D], fp32, ctx2)
        b12u = sb("b12u", [P, 2, 2, DH], fp32, ctx2)
        rw1h, rw1l = sb("rw1h", [P, DH, RH], f32r, ctx2), sb("rw1l", [P, DH, RH], f32r, ctx2)
        mvb, bnr = sb("mvb", [P, DH, 2], fp32, ctx2), sb("bnr", [P, DH], fp32, ctx2)
        bna, bnb = sb("bna", [P, DH], fp32, ctx2), sb("bnb", [P, DH], fp32, ctx2)
        st6b, mv2, rstd2 = sb("st6b", [P, NT, 6], fp32, ctx2), sb("mv2", [P, NT, 2], fp32, ctx2), sb("rstd2", [P, NT], fp32, ctx2)
        lg, pr, eq, f1, f2, g12 = (sb(n, [P, NT, NEXP], fp32, ctx2) for n in ("lg", "pr", "eq", "f1", "f2", "g12"))
        m1, m2, mk, e2, g1, g2 = (sb(n, [P, NT], fp32, ctx2) for n in ("m1", "m2", "mk", "e2", "g1", "g2"))
        rank_i, rank = sb("rank_i", [P, NEXP], i32, ctx2), sb("rank", [P, NEXP], fp32, ctx2)
        gate = sb("gate", [P, NT, NEXP], fp32, ctx2)
        lane_i, lane = sb("lane_i", [P, P], i32, ctx2), sb("lane", [P, P], fp32, ctx2)
        order_i, earlier, ones2 = sb("order_i", [P, P], i32, ctx2), sb("earlier", [P, P], fp32, ctx2), sb("ones2", [P, P], fp32, ctx2)
        token_i, token = sb("token_i", [P, NT], i32, ctx2), sb("token", [P, NT], fp32, ctx2)
        here, tile_no, away = sb("here", [P, NT], fp32, ctx2), sb("tile_no", [P, 2, NT], fp32, ctx2), sb("away", [P, NT], fp32, ctx2)
        lane_no = sb("lane_no", [P, 1], fp32, ctx2)
        lane_h = sb("lane_h", [P, P], fp16, ctx2)
        tile_i = sb("tile_i", [P, 2, NT], i32, ctx2)
        SH = 16
        run = [sb(f"run{i}", [P, SH + NT, NEXP], fp32, ctx2) for i in range(2)]
        chosen, place = sb("chosen", [P, NT, NEXP], fp32, ctx2), sb("place", [P, NT, NEXP], fp32, ctx2)
        units_i, units = sb("units_i", [P, NEXP], i32, ctx2), sb("units", [P, NEXP], fp32, ctx2)
        ends = [sb(f"ends{i}", [P, 4 + NEXP], fp32, ctx2) for i in range(2)]
        base = sb("base", [P, NEXP], fp32, ctx2)
        past, of_unit = sb("past", [P, UMAX, NEXP], fp32, ctx2), sb("of_unit", [P, UMAX], fp32, ctx2)
        expert_of, used = sb("expert_of", [P, UMAX], i32, ctx2), sb("used", [P, 1], i32, ctx2)
        pos, pos_i, plo_i, phi_i = sb("pos", [P, 2, NT], fp32, ctx2), *(sb(n, [P, 2, NT], i32, ctx2) for n in ("pos_i", "plo_i", "phi_i"))
        plo, phi = sb("plo", [P, 2, NT], fp32, ctx2), sb("phi", [P, 2, NT], fp32, ctx2)
        slot_eq, slot_hi = sb("slot_eq", [P, 2 * NT, SC], fp16, ctx2), sb("slot_hi", [P, 2 * NT, 2, SC], fp16, ctx2)
        slot_lo = xx[:].rearrange("p t d -> p (t d)").bitcast(fp16)[:, 0:2 * NT * P].rearrange("p (t n) -> p t n", n=P)
        found = sb("found", [P, SC], fp32, ctx2)
        empty, beyond = sb("empty", [P, SC], fp32, ctx2), sb("beyond", [P, 1], fp32, ctx2)
        gidx_all, sidx_all = sb("gidx_all", [P, SC], i32, ctx2), sb("sidx_all", [P, SC], i32, ctx2)
        gidx2, sidx = sb("gidx2", [P, 2, UT], i32, ctx2), sb("sidx", [P, UT], i32, ctx2)
        sgate = sb("sgate", [P, SC], fp32, ctx2)
        ftok = agg[:, :].rearrange("p (t d) -> p t d", t=NT)
        bank = [ps(f"bank{i}", [P, 512], ctx2) for i in range(8)]
        f_d = nc.dram_tensor("f_d", [N, FW], fp32, kind="Internal").ap()

        t_act, t_gp = sem("act_turn"), sem("pool_turn")
        t_dve = sem("dve_chain")
        t_bnv, t_bns, t_bn = sem("bn_var_ready"), sem("bn_std_ready"), sem("bn_ready")
        t_relu, t_tr, t_x1 = sem("relu_ready"), sem("y_transposed"), sem("x1_ready")
        t_v2, t_s2, t_f, t_ft, t_fh, t_fl = (sem("ln_var_ready"), sem("ln_std_ready"), sem("f_ready"), sem("f_transposed"),
                                             sem("f_hi_ready"), sem("f_parts_ready"))
        t_rw, t_rh, t_rhs, t_lg = sem("router_weights_split"), sem("router_hidden_done"), sem("router_hidden_ready"), sem("logits_done")
        t_sub, t_exp, t_dm, t_e2, t_gate = (sem("logits_shifted"), sem("exp_ready"), sem("gap_ready"), sem("gap_exp_ready"), sem("gates_ready"))
        t_tab, t_cho, t_pfx, t_moh, t_prod, t_slots = (sem("iotas_ready"), sem("choices_counted"), sem("prefixes_done"),
                                                       sem("slot_onehots_ready"), sem("slot_products_done"), sem("slot_tables_ready"))
        t_eq, t_lane = sem("slot_places_ready"), sem("slot_lanes_ready")
        t_init, t_fd = sem("x1_stored"), sem("f_and_gates_stored")
        u_gix, u_six, u_fc = sem("unit_gather_index_ready"), sem("unit_scatter_index_ready"), sem("unit_gates_copied")
        u_g = [sem(f"unit_rows_gathered{i}") for i in range(2)]
        u_w12h, u_w12, u_w3h, u_w3 = sem("unit_w12_hi_ready"), sem("unit_w12_ready"), sem("unit_w3_hi_ready"), sem("unit_w3_ready")
        u_T, u_fh, u_fl = sem("unit_transposed"), sem("unit_f_hi_ready"), sem("unit_f_ready")
        u_l, u_r, u_h = [sem(f"unit_layer{i}_done") for i in (1, 2)], [sem(f"unit_relu{i}_ready") for i in (1, 2)], [sem(f"unit_parts{i}_ready") for i in (1, 2)]
        u_l3, u_ys, u_y, u_sc = sem("unit_layer3_done"), sem("unit_layer3_read"), sem("unit_output_ready"), sem("unit_output_added")

        GROUPS = NG + 1
        rb_, hb = (r1, r2), ((h1h, h1l), (h2h, h2l))
        fparts = ((fuh, ful), (h1h, h1l))

        def tiles_of(g):
            return 4 if g < NG else 1

        def rows_of(t):
            return P if t < FULL else TAILN

        def units_loop(engine, step, finish):
            step(0, 0)
            step(1, 1)
            with engine.Fori(1, UMIN // 2) as pair:
                step(2 * pair, 0)
                step(2 * pair + 1, 1)
            step(UMIN - 1, 0)
            many = engine.value_load(used[0:1, 0:1], min_val=UMIN, max_val=UMAX)
            with engine.If(many < UMIN + 1):
                finish(UMIN - 1, 0)
            for u in range(UMIN, UMAX):
                with engine.If(many > u):
                    step(u, u % 2)
                    with engine.If(many < u + 2):
                        finish(u, u % 2)

        def after(u, first):
            return not isinstance(u, int) or u >= first

        def three(into, pairs):
            last = None
            terms = [(a[i], b[j]) for a, b in pairs for i, j in ((0, 0), (0, 1), (1, 0))]
            for n, (a, b) in enumerate(terms):
                last = nc.tensor.matmul(into, a, b, start=(n == 0), stop=(n == len(terms) - 1))
            return last

        block2 = ctx2.enter_context(nc.Block())

        @block2.sync
        def _(sp):
            for layer, w in enumerate((w1, w2)):
                for e in range(NEXP):
                    sp.dma_start(wraw12[:, e, layer], w[e].rearrange("(k p) n -> p k n", p=P)).then_inc(t_raw, 16)
            sp.dma_start(wraw3[:].rearrange("p e k n -> p (e k) n"), w3.rearrange("e (k p) n -> p (e k) n", p=P)).then_inc(t_raw, 16)
            sp.wait_ge(t_x1, NT)
            sp.dma_start(out[0:FULL * P, :].rearrange("(t p) d -> p t d", p=P), xx[:, 0:FULL, :]).then_inc(t_init, 16)
            sp.dma_start(out[FULL * P:N, :], xx[0:LAST, FULL, :]).then_inc(t_init, 16)
            for g in range(GROUPS):
                sp.wait_ge(t_f, g + 1)
                if g < NG:
                    sp.dma_start(f_d[GN * g:GN * (g + 1), 0:D].rearrange("(t p) d -> p t d", p=P), ftok[:, 4 * g:4 * g + 4, :]).then_inc(t_fd, 16)
                else:
                    sp.dma_start(f_d[FULL * P:N, 0:D], ftok[0:LAST, FULL, :]).then_inc(t_fd, 16)
            sp.wait_ge(t_gate, 1)
            with nc.allow_non_contiguous_dma(reason="the gates at the end of the rows"):
                sp.dma_start(f_d[0:FULL * P, D:FW].rearrange("(t p) e -> p t e", p=P), gate[:, 0:FULL, :]).then_inc(t_fd, 16)
                sp.dma_start(f_d[FULL * P:N, D:FW], gate[0:LAST, FULL, :]).then_inc(t_fd, 16)

        @block2.gpsimd
        def _(gp):
            nc.gpsimd.iota(rank_i[:], pattern=[[-1, NEXP]], base=NEXP, channel_multiplier=0)
            nc.gpsimd.iota(lane_i[:], pattern=[[1, P]], base=0, channel_multiplier=0)
            nc.gpsimd.iota(tile_i[:], pattern=[[0, 2], [1, NT]], base=1, channel_multiplier=0)
            nc.gpsimd.iota(order_i[:], pattern=[[1, P]], base=0, channel_multiplier=-1)
            nc.gpsimd.iota(token_i[:], pattern=[[P, NT]], base=1, channel_multiplier=1).then_inc(t_tab, 1)
            gp.wait_ge(t_w, 16 * 4)
            nc.gpsimd.tensor_copy(rw1h[:], rw1s[:]).then_inc(t_rw, 1)
            gp.wait_ge(t_rw, 1)
            nc.gpsimd.tensor_tensor(rw1l[:], rw1s[:], rw1h[:].bitcast(fp32), ALU.subtract).then_inc(t_rw, 1)
            gp.wait_ge(t_slots, 1)
            gp.wait_ge(t_fd, 16 * (GROUPS + 2))
            gp.wait_ge(t_init, 32)

            def gather(v, X):
                if after(v, 2):
                    gp.wait_ge(u_T, 2 * v - 2)
                    gp.wait_ge(u_fc, v - 1)
                    gp.sem_inc(t_gp, 1)
                nc.gpsimd.tensor_copy(gidx2[:, X, :], gidx_all[:, bass.ds(UT * v, UT)]).then_inc(u_gix, 1)
                gp.wait_ge(u_gix, v + 1)
                gp.sem_inc(t_gp, 1)
                for j in range(UT):
                    gp.indirect_dma_start(out=frows[:, X, j, :], out_offset=None, in_=f_d[:, :],
                                          in_offset=bass.IndirectOffsetOnAxis(ap=gidx2[:, X, j:j + 1], axis=0)).then_inc(u_g[X], 16)

            def scatter(v, X):
                gp.wait_ge(u_y, UT * v + UT)
                if after(v, 1):
                    gp.wait_ge(u_sc, 16 * UT * v)
                gp.sem_inc(t_gp, 1)
                nc.gpsimd.tensor_copy(sidx[:], sidx_all[:, bass.ds(UT * v, UT)]).then_inc(u_six, 1)
                gp.wait_ge(u_six, v + 1)
                gp.sem_inc(t_gp, 1)
                for j in range(UT):
                    gp.indirect_dma_start(out=out[:, :], out_offset=bass.IndirectOffsetOnAxis(ap=sidx[:, j:j + 1], axis=0),
                                          in_=ybuf[:, X, j, :], in_offset=None, bounds_check=N - 1, oob_is_err=False,
                                          compute_op=ALU.add).then_inc(u_sc, 16)

            for v in range(4):
                gather(v, v % 2)
            scatter(0, 0)
            gather(4, 0)
            scatter(1, 1)
            gather(5, 1)
            with gp.Fori(3, UMIN // 2) as pair:
                for X in range(2):
                    scatter(2 * pair - 4 + X, X)
                    gather(2 * pair + X, X)
            for v in (UMIN - 1, UMIN):
                scatter(v - 4, v % 2)
                gather(v, v % 2)
            many = gp.value_load(used[0:1, 0:1], min_val=UMIN, max_val=UMAX)
            for v in range(UMIN + 1, UMIN + 4):
                scatter(v - 4, v % 2)
                with gp.If(many > v - 1):
                    gather(v, v % 2)
            gp.wait_ge(u_sc, 16 * UT * UMIN)
            for v in range(UMIN, UMAX):
                with gp.If(many > v):
                    scatter(v, v % 2)
                    if v + 4 < UMAX:
                        with gp.If(many > v + 3):
                            gather(v + 4, v % 2)
                    gp.wait_ge(u_sc, 16 * UT * (v + 1))

        @block2.scalar
        def _(act):
            act.wait_ge(t_bnv, 1)
            nc.scalar.activation(bnr[:], mvb[:, :, 1], ACT.Sqrt, bias=eps1[:]).then_inc(t_bns, 1)
            act.wait_ge(t_bn, 1)
            for g in range(GROUPS):
                cols = GN if g < NG else TAILN
                for m in range(DH):
                    at = agg[:, m * NPAD + GN * g:m * NPAD + GN * g + cols]
                    nc.scalar.activation(at, at, ACT.Relu, bias=bnb[:, m:m + 1], scale=bna[:, m:m + 1]).then_inc(t_relu, 1)
            act.wait_ge(t_v2, 1)
            nc.scalar.activation(rstd2[:], mv2[:, :, 1], ACT.Sqrt, bias=eps1[:]).then_inc(t_s2, 1)
            for g in range(GROUPS + 1):
                if g < GROUPS:
                    cols = GN if g < NG else TAILN
                    act.wait_ge(t_ft, g + 1)
                    for m in range(DH):
                        nc.scalar.activation(fparts[g % 2][0][:, m, 0:cols], bank[4 + 2 * (g % 2) + m][:, 0:cols], ACT.Copy).then_inc(t_fh, 1)
                if g >= 1:
                    cols = GN if g - 1 < NG else TAILN
                    act.wait_ge(t_rh, g)
                    if g >= 3:
                        act.wait_ge(t_lg, g - 2)
                    nc.scalar.activation(r1[:, (g - 1) % 2, 0:cols], bank[(g - 1) % 2][:, 0:cols], ACT.Relu, bias=rb1T[:, 0:1]).then_inc(t_rhs, 1)
            act.wait_ge(t_sub, 1)
            nc.scalar.activation(pr[:], lg[:], ACT.Exp).then_inc(t_exp, 1)
            act.wait_ge(t_dm, 1)
            nc.scalar.activation(e2[:], m2[:], ACT.Exp).then_inc(t_e2, 1)
            for i in range(2 * NT // MB):
                at = slice(MB * i, MB * i + MB)
                act.wait_ge(t_eq, i + 1)
                nc.scalar.activation(slot_hi[:, at, 1, :], slot_eq[:, at, :], ACT.Copy, scale=lane_no[:, 0:1]).then_inc(t_lane, 1)

            def first_weights(u, X):
                if after(u, 2):
                    act.wait_ge(u_r[1], 2 * u - 2)
                act.sem_inc(t_act, 1)
                e = act.value_load(expert_of[0:1, bass.ds(u, 1)], min_val=0, max_val=NEXP - 1)
                nc.scalar.activation(b12u[:, X], b12T[:, bass.ds(e, 1)].rearrange("p o l m -> p (o l) m"), ACT.Copy).then_inc(u_w12h, 1)
                nc.scalar.activation(w12h[:, X], wraw12[:, bass.ds(e, 1)].rearrange("p o l k n -> p (o l) k n"), ACT.Copy).then_inc(u_w12h, 1)

            def last_weights(u, X):
                if after(u, 2):
                    act.wait_ge(u_l3, 2 * u - 2)
                act.sem_inc(t_act, 1)
                e = act.value_load(expert_of[0:1, bass.ds(u, 1)], min_val=0, max_val=NEXP - 1)
                nc.scalar.activation(w3h[:, X], wraw3[:, bass.ds(e, 1)].rearrange("p o k n -> p (o k) n"), ACT.Copy).then_inc(u_w3h, 1)

            def high_part(u):
                for m in range(DH):
                    act.wait_ge(u_T, 2 * u + m + 1)
                    nc.scalar.activation(fuh[:, m, :], bank[m][:], ACT.Copy).then_inc(u_fh, 1)

            def relu_parts(u, X, layer):
                for m in range(DH):
                    act.wait_ge(u_l[layer], 2 * u + m + 1)
                    src_, b = bank[2 + 2 * layer + m][:], b12u[:, X, layer, m:m + 1]
                    nc.scalar.activation(rb_[layer][:, m, :], src_, ACT.Relu, bias=b)
                    nc.scalar.activation(hb[layer][0][:, m, :], src_, ACT.Relu, bias=b).then_inc(u_r[layer], 1)

            def act_step(u, X):
                if not isinstance(u, int) or u < UMAX - 1:
                    first_weights(u + 1, 1 - X)
                act.wait_ge(u_w12h, 2 * u + 1)
                relu_parts(u, X, 0)
                if not isinstance(u, int) or u < UMAX - 1:
                    high_part(u + 1)
                last_weights(u, X)
                relu_parts(u, X, 1)

            act.wait_ge(t_raw, 16 * NRAW)
            act.wait_ge(t_slots, 1)
            first_weights(0, 0)
            high_part(0)
            units_loop(act, act_step, lambda u, X: None)

        @block2.vector
        def _(dve):
            chain = [0]

            def link(ins):
                chain[0] += 1
                ins.then_inc(t_dve, 1)
                dve.wait_ge(t_dve, chain[0])

            for m in range(DH):
                last = nc.vector.bn_aggr(mvb[:, m, :], stats[:, m, :, :].rearrange("p a b -> p (a b)"))
            last.then_inc(t_bnv, 1)
            dve.wait_ge(t_gb, 32)
            dve.wait_ge(t_bns, 1)
            link(nc.vector.reciprocal(bnr[:], bnr[:]))
            link(nc.vector.tensor_tensor(bna[:], bnr[:], gammaT[:], ALU.mult))
            link(nc.vector.tensor_tensor(bnr[:], mvb[:, :, 0], bna[:], ALU.mult))
            nc.vector.tensor_tensor(bnb[:], betaT[:], bnr[:], ALU.subtract).then_inc(t_bn, 1)
            for t in range(NT):
                g, r = t // 4, rows_of(t)
                dve.wait_ge(t_tr, min(NT, t - t % 2 + 2))
                src_ = bank[2 * (g % 2) + (t % 4) // 2][0:r, D * (t % 2):D * (t % 2) + D]
                nc.vector.tensor_tensor(xx[0:r, t, :], xx[0:r, t, :], src_, ALU.add).then_inc(t_x1, 1)
                if t >= 1:
                    dve.wait_ge(t_x1, t)
                    nc.vector.bn_stats(st6b[:, t - 1, :], xx[:, t - 1, :])
            dve.wait_ge(t_x1, NT)
            link(nc.vector.bn_stats(st6b[:, NT - 1, :], xx[:, NT - 1, :]))
            for t in range(NT):
                last = nc.vector.bn_aggr(mv2[:, t, :], st6b[:, t, :])
            last.then_inc(t_v2, 1)
            dve.wait_ge(t_s2, 1)
            link(nc.vector.reciprocal(rstd2[:], rstd2[:]))
            for g in range(GROUPS + 1):
                if g < GROUPS:
                    for j in range(tiles_of(g)):
                        t = 4 * g + j
                        last = nc.vector.tensor_scalar(ftok[:, t, :], xx[:, t, :], mv2[:, t, 0:1], rstd2[:, t:t + 1], ALU.subtract, ALU.mult)
                    last.then_inc(t_f, 1)
                if g >= 1:
                    cols = GN if g - 1 < NG else TAILN
                    for m in range(DH):
                        dve.wait_ge(t_fh, 2 * (g - 1) + m + 1)
                        hi, lo = fparts[(g - 1) % 2]
                        nc.vector.tensor_tensor(lo[:, m, 0:cols], bank[4 + 2 * ((g - 1) % 2) + m][:, 0:cols], hi[:, m, 0:cols].bitcast(fp32),
                                                ALU.subtract).then_inc(t_fl, 1)
            bc = [P, NT, NEXP]
            dve.wait_ge(t_tab, 1)
            nc.vector.tensor_copy(rank[:], rank_i[:])
            nc.vector.tensor_copy(lane[:], lane_i[:])
            nc.vector.tensor_scalar(earlier[:], order_i[:], 0.0, None, ALU.is_gt)
            nc.vector.memset(ones2[:], 1.0)
            for buf in run:
                nc.vector.memset(buf[:, 0:SH, :], 0.0)
            for buf in ends:
                nc.vector.memset(buf[:, 0:4], 0.0)
            nc.vector.tensor_copy(lane_h[:], lane_i[:])
            nc.vector.tensor_copy(tile_no[:], tile_i[:])
            link(nc.vector.tensor_copy(token[:], token_i[:]))
            nc.vector.tensor_scalar(lane_no[:], token[:, 0:1], -1.0, None, ALU.add)
            link(nc.vector.tensor_scalar(here[:], token[:], float(N), None, ALU.is_le))
            link(nc.vector.tensor_scalar(away[:], here[:], 1.0, float(2 * SC), ALU.subtract, ALU.mult))
            dve.wait_ge(t_w, 16 * 4)
            nc.vector.memset(lg[:], 0.0)
            dve.wait_ge(t_lg, GROUPS)
            link(nc.vector.memset(pr[:], 0.0))
            logits = bank[2][:, 0:NT * 8].rearrange("p (t e) -> p t e", e=8)[:, :, 0:NEXP]
            rb = rb2b[:].unsqueeze(1)
            nc.vector.tensor_tensor(lg[:, 0:FULL, :], logits[:, 0:FULL, :], rb.to_broadcast([P, FULL, NEXP]), ALU.add)
            link(nc.vector.tensor_tensor(lg[0:TAILN, FULL:NT, :], logits[0:TAILN, FULL:NT, :], rb[0:TAILN].to_broadcast([TAILN, 1, NEXP]), ALU.add))
            link(nc.vector.reduce_max(m1[:], lg[:], AX.X))
            nc.vector.tensor_tensor(lg[:], lg[:], m1[:].unsqueeze(2).to_broadcast(bc), ALU.subtract).then_inc(t_sub, 1)
            dve.wait_ge(t_exp, 1)
            link(nc.vector.reduce_sum(m2[:], pr[:], AX.X))
            link(nc.vector.reciprocal(m2[:], m2[:]))
            link(nc.vector.tensor_tensor(pr[:], pr[:], m2[:].unsqueeze(2).to_broadcast(bc), ALU.mult))

            def pick(top, chosen):
                link(nc.vector.reduce_max(top[:], pr[:], AX.X))
                link(nc.vector.tensor_tensor(eq[:], pr[:], top[:].unsqueeze(2).to_broadcast(bc), ALU.is_equal))
                link(nc.vector.tensor_tensor(eq[:], eq[:], rank[:].unsqueeze(1).to_broadcast(bc), ALU.mult))
                link(nc.vector.reduce_max(mk[:], eq[:], AX.X))
                link(nc.vector.tensor_tensor(chosen[:], eq[:], mk[:].unsqueeze(2).to_broadcast(bc), ALU.is_equal))

            pick(m1, f1)
            link(nc.vector.scalar_tensor_tensor(pr[:], f1[:], -2.0, pr[:], ALU.mult, ALU.add))
            pick(m2, f2)
            nc.vector.tensor_tensor(m2[:], m2[:], m1[:], ALU.subtract).then_inc(t_dm, 1)
            link(nc.vector.tensor_tensor(chosen[:], f1[:], f2[:], ALU.add))
            link(nc.vector.tensor_tensor(chosen[:], chosen[:], here[:].unsqueeze(2).to_broadcast(bc), ALU.mult))
            src_, shift, turn = chosen[:], 1, 0
            link(nc.vector.tensor_copy(run[1][:, SH:, :], chosen[:]))
            while shift < NT:
                a, b = run[1 - turn], run[turn]
                ins = nc.vector.tensor_tensor(b[:, SH:, :], a[:, SH:, :], a[:, SH - shift:SH - shift + NT, :], ALU.add)
                link(ins)
                shift, turn = 2 * shift, 1 - turn
            total = run[1 - turn]
            nc.vector.tensor_copy(base[:], total[:, SH + NT - 1, :]).then_inc(t_cho, 1)
            link(nc.vector.tensor_tensor(place[:], total[:, SH:, :], chosen[:], ALU.subtract))
            dve.wait_ge(t_pfx, 1)
            link(nc.vector.tensor_scalar(units_i[:], bank[7][:, 8:8 + NEXP], float(UN - 1), None, ALU.add))
            link(nc.vector.tensor_scalar(units_i[:], units_i[:], UN.bit_length() - 1, None, ALU.logical_shift_right))
            nc.vector.tensor_copy(units[:], units_i[:])
            link(nc.vector.tensor_copy(ends[0][:, 4:], units_i[:]))
            for i, shift in enumerate((1, 2, 4)):
                a, b = ends[i % 2], ends[1 - i % 2]
                link(nc.vector.tensor_tensor(b[:, 4:], a[:, 4:], a[:, 4 - shift:4 - shift + NEXP], ALU.add))
            end = ends[1][:, 4:]
            link(nc.vector.tensor_tensor(units[:], end, units[:], ALU.subtract))
            link(nc.vector.scalar_tensor_tensor(base[:], units[:], float(UN), bank[7][:, 0:NEXP], ALU.mult, ALU.add))
            link(nc.vector.tensor_tensor(place[:], place[:], base[:].unsqueeze(1).to_broadcast(bc), ALU.add))
            for k, f in enumerate((f1, f2)):
                link(nc.vector.tensor_tensor(eq[:], f[:], place[:], ALU.mult))
                link(nc.vector.reduce_sum(pos[:, k, :], eq[:], AX.X))
            link(nc.vector.tensor_copy(pos_i[:], pos[:]))
            nc.vector.tensor_scalar(plo_i[:], pos_i[:], P - 1, None, ALU.bitwise_and)
            link(nc.vector.tensor_scalar(phi_i[:], pos_i[:], 7, None, ALU.logical_shift_right))
            nc.vector.tensor_copy(plo[:], plo_i[:])
            link(nc.vector.tensor_copy(phi[:], phi_i[:]))
            link(nc.vector.tensor_tensor(phi[:], phi[:], away[:].unsqueeze(1).to_broadcast([P, 2, NT]), ALU.add))
            dve.wait_ge(t_init, 32)
            flat = [b[:].rearrange("p k t -> p (k t)") for b in (plo, phi, tile_no)]
            for i in range(2 * NT // MB):
                at = slice(MB * i, MB * i + MB)
                lo_, hi_, no_ = (f[:, at].unsqueeze(2) for f in flat)
                nc.vector.tensor_tensor(slot_eq[:, at, :], lane_h[:, 0:SC].unsqueeze(1).to_broadcast([P, MB, SC]), hi_.to_broadcast([P, MB, SC]), ALU.is_equal).then_inc(t_eq, 1)
                nc.vector.tensor_tensor(slot_lo[:, at, :], lane_h[:].unsqueeze(1).to_broadcast([P, MB, P]), lo_.to_broadcast([P, MB, P]), ALU.is_equal)
                dve.wait_ge(t_eq, i + 1)
                nc.vector.tensor_tensor(slot_hi[:, at, 0, :], slot_eq[:, at, :], no_.to_broadcast([P, MB, SC]), ALU.mult).then_inc(t_moh, 1)
            dve.wait_ge(t_e2, 1)
            link(nc.vector.tensor_scalar(g1[:], e2[:], 1.0, None, ALU.add))
            link(nc.vector.reciprocal(g1[:], g1[:]))
            link(nc.vector.tensor_tensor(g2[:], e2[:], g1[:], ALU.mult))
            nc.vector.tensor_tensor(g12[:], f1[:], g1[:].unsqueeze(2).to_broadcast(bc), ALU.mult)
            link(nc.vector.tensor_tensor(gate[:], f2[:], g2[:].unsqueeze(2).to_broadcast(bc), ALU.mult))
            nc.vector.tensor_tensor(gate[:], gate[:], g12[:], ALU.add).then_inc(t_gate, 1)
            link(nc.vector.tensor_tensor(past[:], lane[:, 0:UMAX].unsqueeze(2).to_broadcast([P, UMAX, NEXP]),
                                         end.unsqueeze(1).to_broadcast([P, UMAX, NEXP]), ALU.is_ge))
            nc.vector.tensor_copy(used[:], end[:, NEXP - 1:NEXP])
            link(nc.vector.reduce_sum(of_unit[:], past[:], AX.X))
            link(nc.vector.tensor_scalar(expert_of[:], of_unit[:], float(NEXP - 1), None, ALU.min))
            link(nc.vector.tensor_scalar(beyond[:], token[:, 0:1], float(N + P), None, ALU.add))
            dve.wait_ge(t_prod, 1)
            tiles_, lanes_ = bank[6][:, 0:SC], bank[6][:, SC:2 * SC]
            link(nc.vector.tensor_copy(found[:], lanes_))
            link(nc.vector.scalar_tensor_tensor(found[:], tiles_, float(P), found[:], ALU.mult, ALU.add))
            nc.vector.tensor_scalar(gidx_all[:], found[:], -float(P), 0.0, ALU.add, ALU.max)
            link(nc.vector.tensor_scalar(empty[:], tiles_, 0.5, beyond[:, 0:1], ALU.is_lt, ALU.mult))
            nc.vector.scalar_tensor_tensor(sidx_all[:], found[:], -float(P), empty[:], ALU.add, ALU.add).then_inc(t_slots, 1)
            dve.wait_ge(t_slots, 1)
            dve.wait_ge(t_raw, 16 * NRAW)

            def first_weights(u, X):
                e = dve.value_load(expert_of[0:1, bass.ds(u, 1)], min_val=0, max_val=NEXP - 1)
                dve.wait_ge(u_w12h, 2 * u + 2)
                nc.vector.tensor_tensor(w12l[:, X], wraw12[:, bass.ds(e, 1)].rearrange("p o l k n -> p (o l) k n"), w12h[:, X].bitcast(fp32),
                                        ALU.subtract).then_inc(u_w12, 1)

            def last_weights(u, X):
                e = dve.value_load(expert_of[0:1, bass.ds(u, 1)], min_val=0, max_val=NEXP - 1)
                dve.wait_ge(u_w3h, u + 1)
                nc.vector.tensor_tensor(w3l[:, X], wraw3[:, bass.ds(e, 1)].rearrange("p o k n -> p (o k) n"), w3h[:, X].bitcast(fp32),
                                        ALU.subtract).then_inc(u_w3, 1)

            def low_rows(u, X):
                e = dve.value_load(expert_of[0:1, bass.ds(u, 1)], min_val=0, max_val=NEXP - 1)
                dve.wait_ge(u_T, 2 * u + 1)
                nc.vector.tensor_copy(sgate[:, bass.ds(UT * u, UT)].unsqueeze(2), frows[:, X, :, bass.ds(D + e, 1)]).then_inc(u_fc, 1)
                for m in range(DH):
                    dve.wait_ge(u_fh, 2 * u + m + 1)
                    nc.vector.tensor_tensor(ful[:, m, :], bank[m][:], fuh[:, m, :].bitcast(fp32), ALU.subtract).then_inc(u_fl, 1)

            def low_part(u, X, layer):
                for m in range(DH):
                    dve.wait_ge(u_r[layer], 2 * u + m + 1)
                    nc.vector.tensor_tensor(hb[layer][1][:, m, :], rb_[layer][:, m, :], hb[layer][0][:, m, :].bitcast(fp32),
                                            ALU.subtract).then_inc(u_h[layer], 1)

            def outputs(u, X):
                e = dve.value_load(expert_of[0:1, bass.ds(u, 1)], min_val=0, max_val=NEXP - 1)
                if after(u, 2):
                    dve.wait_ge(u_sc, 16 * UT * (u - 1))
                for h in range(2):
                    dve.wait_ge(u_l3, 2 * u + h + 1)
                    nc.vector.tensor_tensor(ybuf[:, X, 2 * h:2 * h + 2, :], bank[6 + h][:].rearrange("p (j n) -> p j n", j=2),
                                            b3b[:, bass.ds(e, 1), :].to_broadcast([P, 2, D]), ALU.add).then_inc(u_ys, 1)
                dve.wait_ge(u_fc, u + 1)
                for j in range(UT):
                    if j % 2 == 0:
                        dve.wait_ge(u_ys, 2 * u + j // 2 + 1)
                    nc.vector.tensor_scalar(ybuf[:, X, j, :], ybuf[:, X, j, :], sgate[:, bass.ds(UT * u + j, 1)], None, ALU.mult).then_inc(u_y, 1)

            def dve_step(u, X):
                if not isinstance(u, int) or u < UMAX - 1:
                    first_weights(u + 1, 1 - X)
                low_part(u, X, 0)
                if not isinstance(u, int) or u < UMAX - 1:
                    low_rows(u + 1, 1 - X)
                last_weights(u, X)
                if after(u, 1):
                    outputs(u - 1, 1 - X)
                low_part(u, X, 1)

            first_weights(0, 0)
            low_rows(0, 0)
            units_loop(dve, dve_step, outputs)

        @block2.tensor
        def _(pe):
            for t in range(NT):
                g, r = t // 4, rows_of(t)
                if t % 4 == 0:
                    pe.wait_ge(t_relu, 2 * g + 2)
                    if g >= 2:
                        pe.wait_ge(t_x1, 4 * (g - 1))
                for m in range(DH):
                    last = nc.tensor.transpose(bank[2 * (g % 2) + (t % 4) // 2][0:r, D * (t % 2) + P * m:D * (t % 2) + P * m + P],
                                               agg[:, m * NPAD + P * t:m * NPAD + P * t + r], identf[:])
                last.then_inc(t_tr, 1)
            pe.wait_ge(t_rw, 2)
            for g in range(GROUPS + 2):
                if g < GROUPS:
                    pe.wait_ge(t_f, g + 1)
                    if g >= 2:
                        pe.wait_ge(t_fl, 2 * (g - 1))
                    for m in range(DH):
                        for j in range(tiles_of(g)):
                            t = 4 * g + j
                            r = rows_of(t)
                            last = nc.tensor.transpose(bank[4 + 2 * (g % 2) + m][:, P * j:P * j + r], ftok[0:r, t, P * m:P * m + P], identf[0:r, 0:r])
                    last.then_inc(t_ft, 1)
                if 1 <= g <= GROUPS:
                    k_, cols = g - 1, GN if g - 1 < NG else TAILN
                    hi, lo = fparts[k_ % 2]
                    pe.wait_ge(t_fl, 2 * k_ + 2)
                    if k_ >= 2:
                        pe.wait_ge(t_rhs, k_ - 1)
                    if k_ < 2:
                        pe.wait_ge(t_x1, NT)
                    three(bank[k_ % 2][:, 0:cols], [((rw1h[:, k, :], rw1l[:, k, :]), (hi[:, k, 0:cols], lo[:, k, 0:cols])) for k in range(DH)]).then_inc(t_rh, 1)
                if g >= 2:
                    k_ = g - 2
                    pe.wait_ge(t_rhs, k_ + 1)
                    for j in range(tiles_of(k_)):
                        t = 4 * k_ + j
                        r = rows_of(t)
                        last = nc.tensor.matmul(bank[2][0:r, 8 * t:8 * t + NEXP], r1[:, k_ % 2, P * j:P * j + r], rw2s[:], start=True, stop=True)
                    last.then_inc(t_lg, 1)
            pe.wait_ge(t_cho, 1)
            nc.tensor.matmul(bank[7][:, 0:NEXP], earlier[:], base[:], start=True, stop=True)
            nc.tensor.matmul(bank[7][:, 8:8 + NEXP], ones2[:], base[:], start=True, stop=True).then_inc(t_pfx, 1)
            for i in range(2 * NT):
                if i % MB == 0:
                    pe.wait_ge(t_moh, i // MB + 1)
                    pe.wait_ge(t_lane, i // MB + 1)
                last = nc.tensor.matmul(bank[6][:, 0:2 * SC], slot_lo[:, i, :], slot_hi[:, i, :, :].rearrange("p h n -> p (h n)"), start=i == 0, stop=i == 2 * NT - 1)
            last.then_inc(t_prod, 1)

            def rows_unit(u, X, round_):
                pe.wait_ge(u_g[X], 16 * UT * (round_ + 1))
                for m in range(DH):
                    for j in range(UT):
                        last = nc.tensor.transpose(bank[m][:, P * j:P * j + P], frows[:, X, j, P * m:P * m + P], identf[:])
                    last.then_inc(u_T, 1)

            def layer_unit(u, X, layer):
                fhl = (fuh, ful) if layer == 0 else (h1h, h1l)
                for m in range(DH):
                    cs = slice(P * m, P * m + P)
                    three(bank[2 + 2 * layer + m][:], [((w12h[:, X, layer, k, cs], w12l[:, X, layer, k, cs]), (fhl[0][:, k, :], fhl[1][:, k, :]))
                                                       for k in range(DH)]).then_inc(u_l[layer], 1)

            def out_unit(u, X):
                pe.wait_ge(u_h[1], 2 * u + 2)
                pe.wait_ge(u_w3, u + 1)
                if after(u, 1):
                    pe.wait_ge(u_ys, 2 * u)
                for h in range(2):
                    for j in (2 * h, 2 * h + 1):
                        last = three(bank[6 + h][:, D * (j % 2):D * (j % 2) + D],
                                     [((h2h[:, k, P * j:P * j + P], h2l[:, k, P * j:P * j + P]), (w3h[:, X, k, :], w3l[:, X, k, :])) for k in range(DH)])
                    last.then_inc(u_l3, 1)

            def pe_step(u, X):
                pe.wait_ge(u_w12, u + 1)
                pe.wait_ge(u_fl, 2 * u + 2)
                layer_unit(u, X, 0)
                if not isinstance(u, int) or u < UMAX - 1:
                    rows_unit(u + 1, 1 - X, (u + 1) // 2)
                if after(u, 1):
                    out_unit(u - 1, 1 - X)
                pe.wait_ge(u_h[0], 2 * u + 2)
                layer_unit(u, X, 1)

            rows_unit(0, 0, 0)
            units_loop(pe, pe_step, out_unit)

        ctx2.close()


_INS = ["x", "src", "dst", "L0_gnn_W", "L0_gnn_bias", "L0_gnn_gamma", "L0_gnn_beta",
        "L0_ffn_router_w1", "L0_ffn_router_b1", "L0_ffn_router_w2", "L0_ffn_router_b2",
        "L0_ffn_expert_w1", "L0_ffn_expert_b1", "L0_ffn_expert_w2", "L0_ffn_expert_b2",
        "L0_ffn_expert_w3", "L0_ffn_expert_b3"]


def kernel(**inputs):
    import numpy as _np
    import concourse.bacc as _bacc
    from concourse import mybir as _mybir
    from concourse.bass_utils import run_bass_kernel_spmd as _run

    nc = _bacc.Bacc("TRN2", target_bir_lowering=False, num_devices=1)
    arrays, args = {}, []
    for name in _INS:
        a = _np.ascontiguousarray(inputs[name])
        arrays[f"in_{name}"] = a
        args.append(nc.dram_tensor(f"in_{name}", a.shape, _mybir.dt.from_np(a.dtype), kind="ExternalInput").ap())
    args.append(nc.dram_tensor("out_0", [N, D], fp32, kind="ExternalOutput").ap())
    build(nc, *args)
    r = _run(nc, [arrays], core_ids=[0])
    return r.results[0]["out_0"]
```

```python
import concourse.bass as bass
from concourse import mybir
from contextlib import ExitStack

fp32 = mybir.dt.float32
fp16 = mybir.dt.float16
f32r = mybir.dt.float32r
i32 = mybir.dt.int32
ALU = mybir.AluOpType
ACT = mybir.ActivationFunctionType
AX = mybir.AxisListType

N, D, E = 3125, 256, 50000
P = 128
NT = -(-N // P)
FULL = N // P
LAST = N - FULL * P
DH = D // P
EP, EC = 125, 400
WIN = 12
WPT = -(-P // WIN)
KCH = 2
CAP = KCH * P
CNT = NT * WIN
GN = 4 * P
HG = GN // 2
GW = 4 * WPT
NG = N // GN
TAILN = 64
TAILW = -(-TAILN // WIN)
NPAD = NG * GN + TAILN
BK = WPT
NS = GW // BK
OHR = 4
HR = 20
HS = 3
HS2 = 5
ROUNDS = (EC // HR - HS2) // HS
HLO = 64
HHI = NT * P // HLO
NEXP, H, RH = 6, 256, 128
UN = 384
UT = UN // P
UMAX = (2 * N - NEXP) // UN + NEXP
UMIN = -(-2 * N // UN)
SC = UMAX * UT
MB = 10
FW = D + NEXP
NRAW = 2 * NEXP + 6
EPS = 1e-5
XSCALE = 256.0


def build(nc, x, src, dst, W, bias, gamma, beta, rw1, rb1, rw2, rb2, w1, b1, w2, b2, w3, b3, out):
    ctx, ctx1, ctx2 = ExitStack(), ExitStack(), ExitStack()
    with ctx:
        def sb(name, shape, dt, scope=ctx):
            return scope.enter_context(nc.sbuf_tensor(name, shape, dt))

        def ps(name, shape, scope=ctx, dt=fp32):
            return scope.enter_context(nc.psum_tensor(name, shape, dt))

        def sem(name):
            return ctx.enter_context(nc.semaphore(name))

        keys_d = nc.dram_tensor("keys_d", [(E + CAP) * 2], fp32, kind="Internal").ap()
        xs_d = nc.dram_tensor("xs_d", [NT * P, D], fp32, kind="Internal").ap()

        xx = sb("xx", [P, NT, D], fp32)
        agg = sb("agg", [P, NT * D], fp32)
        xn = agg[:, :].rearrange("p (t d) -> p t d", t=NT)
        stats = sb("stats", [P, DH, NG + 1, 6], fp32)
        identf = sb("identf", [P, P], fp32)
        nmr = sb("nmr", [P, NT], fp32)
        eps1 = sb("eps1", [P, 1], fp32)
        gammaT, betaT = sb("gammaT", [P, DH], fp32), sb("betaT", [P, DH], fp32)
        rb1T, rw2s, rb2b, rw1s = sb("rb1T", [P, 1], fp32), sb("rw2s", [RH, NEXP], fp32), sb("rb2b", [P, NEXP], fp32), sb("rw1s", [P, DH, RH], fp32)
        b12T = sb("b12T", [P, NEXP, 2, DH], fp32)
        b3b = sb("b3b", [P, NEXP, D], fp32)
        t_gb, t_w, t_raw = sem("gamma_beta_loaded"), sem("small_weights_loaded"), sem("expert_weights_loaded")

        C = sb("C", [P, 2, NT, GN], fp16, ctx1)
        xs = sb("xs", [P, 2, NT, D], fp16, ctx1)
        oh_src = sb("oh_src", [P, OHR, KCH, P], fp16, ctx1)
        oh_key = sb("oh_key", [P, OHR, KCH, CNT], fp16, ctx1)
        ekeys = sb("ekeys", [P, NS, BK, KCH, 2], fp32, ctx1)
        wkeys = sb("wkeys", [P, NS, BK, KCH], fp32, ctx1)
        dinvb = sb("dinvb", [P, NT * P], fp32, ctx1)
        zh, zl = (sb(n, [P, DH, GN], f32r, ctx1) for n in ("zh", "zl"))
        wgh, wgl = (sb(n, [P, DH, D], f32r, ctx1) for n in ("wgh", "wgl"))
        zbuf = sb("zbuf", [P, DH, GN], fp32, ctx1)
        ubuf = sb("ubuf", [P, DH, GN], fp32, ctx1)
        wgcn = sb("wgcn", [P, DH, D], fp32, ctx1)
        biasT = sb("biasT", [P, DH], fp32, ctx1)
        iota_i = sb("iota_i", [P, GN], i32, ctx1)
        iota_h = sb("iota_h", [P, CNT], fp16, ctx1)
        win_i = sb("win_i", [P, NG * GW + TAILW], i32, ctx1)
        win_off = sb("win_off", [P, NG * GW + TAILW], fp32, ctx1)
        diff_i = sb("diff_i", [P, P], i32, ctx1)
        mask_i = sb("mask_i", [P, WPT], i32, ctx1)
        ident16 = sb("ident16", [P, P], fp16, ctx1)
        below = sb("below", [P, WPT], fp32, ctx1)
        upper = sb("upper", [NT, NT], fp32, ctx1)
        ones = sb("ones", [P, P], fp32, ctx1)
        srci = sb("srci", [EP, EC], i32, ctx1)
        dsti = sb("dsti", [EP, EC], i32, ctx1)
        nexti = sb("nexti", [EP, EC], i32, ctx1)
        ti = sb("ti", [EP, 4, EC], i32, ctx1)
        dstlo = sb("dstlo", [EP, EC], fp16, ctx1)
        dsthi = sb("dsthi", [EP, EC], fp16, ctx1)
        pack = sb("pack", [EP, EC, 2], fp32, ctx1)
        padk = sb("padk", [P, 2 * KCH], fp32, ctx1)
        desc = sb("desc", [EP, EC], fp32, ctx1)
        descs = sb("descs", [EP, 1], fp32, ctx1)
        mv = sb("mv", [P, NT, 2], fp32, ctx1)
        st6 = sb("st6", [P, NT, 6], fp32, ctx1)
        rstd = sb("rstd", [P, NT], fp32, ctx1)
        deg = sb("deg", [P, NT], fp32, ctx1)
        dinv = sb("dinv", [P, NT], fp32, ctx1)
        dinvs = sb("dinvs", [P, NT], fp32, ctx1)
        total = sb("total", [NT, 1], fp32, ctx1)
        rowf = sb("rowf", [1, NT * WPT], fp32, ctx1)
        over = sb("over", [1, NT * WPT - 1], fp32, ctx1)
        overs = sb("overs", [1, 1], fp32, ctx1)
        row = sb("row", [1, NT * WPT], i32, ctx1)
        flag = sb("flag", [1, 1], i32, ctx1)
        degr = sb("degr", [P, NT], fp32, ctx1)
        dinvz = sb("dinvz", [P, NT], fp32, ctx1)
        dstf = sb("dstf", [EP, EC], fp32, ctx1)
        goff_i = sb("goff_i", [P, NG + 1], i32, ctx1)
        gkey = sb("gkey", [EP, 1], fp32, ctx1)
        gidx = sb("gidx", [EP, 1], i32, ctx1)
        diag4 = C[:, 1, :, :].rearrange("p a b -> p (a b)").bitcast(fp32)[:, 0:(NG + 1) * GN].rearrange("p (g n) -> p g n", n=GN)
        gen_oh = C[0:EP, 0, :, :].rearrange("p a b -> p (a b)").bitcast(fp32)[:, 0:GN]
        gen_xs = C[:, 1, :, :].rearrange("p a b -> p (a b)").bitcast(fp32)
        gen_rows = ubuf[0:EP, 0, 0:D]
        hist = C[0:EP, 0, :, :].rearrange("p a b -> p (a b)")
        hist_lo = hist[:, 0:HS * HR * HLO].rearrange("p (s r n) -> p s r n", s=HS, n=HLO)
        hist2 = C[0:EP, 1, :, :].rearrange("p a b -> p (a b)")
        hist2_lo = hist2[:, 0:HS2 * HR * HLO].rearrange("p (s r n) -> p s r n", s=HS2, n=HLO)
        hist2_hi = hist2[:, HS2 * HR * HLO:HS2 * HR * (HLO + HHI)].rearrange("p (s r n) -> p s r n", s=HS2, n=HHI)
        hist_hi = hist[:, HS * HR * HLO:HS * HR * (HLO + HHI)].rearrange("p (s r n) -> p s r n", s=HS, n=HHI)

        psC = [ps(f"psC{i}", [P, 512], ctx1) for i in range(4)]
        psZ = [ps(f"psZ{i}", [P, 512], ctx1) for i in range(2)]
        psY = [ps(f"psY{i}", [P, 512], ctx1) for i in range(2)]

        s_dst, s_edge, s_x, s_wt, s_cst = sem("dst_loaded"), sem("edges_loaded"), sem("x_loaded"), sem("weights_loaded"), sem("constants_ready")
        s_dve = sem("dve_step")
        s_packed, s_keys = sem("keys_packed"), sem("keys_in_dram")
        s_hdiff, s_hsq, s_hoh2 = sem("degree_differences_ready"), sem("degree_squares_ready"), sem("degree_onehots_ready_act")
        s_dk, s_hoh, s_hmm = sem("degree_keys_ready"), sem("degree_onehots_ready"), sem("degree_chunks_done")
        s_deg, s_cum, s_pref, s_flagmm = sem("deg_ready"), sem("cum_done"), sem("prefix_done"), sem("flag_done")
        s_cumsb, s_row, s_over = sem("totals_in_sbuf"), sem("window_starts_ready"), sem("full_windows_counted")
        s_flag = sem("flag_ready")
        s_var, s_std, s_rstd, s_xn, s_sqd = sem("var_ready"), sem("std_ready"), sem("rstd_ready"), sem("xn_ready"), sem("sqrt_deg_ready")
        s_pool = sem("pool_step")
        s_dinv, s_xhi, s_xs = sem("dinv_ready"), sem("xs_hi_ready"), sem("xs_ready")
        s_diag, s_dbmm, s_dinvb = sem("diag_ready"), sem("dinv_row_done"), sem("dinv_row_ready")
        s_turn, s_gturn = sem("key_loads_turn"), sem("key_loads_turn_pool")
        s_ek = [sem(f"edge_keys_loaded{i}") for i in range(NS)]
        lots = (2, 2, 2, 2, BK - 8)
        s_first = [sem(f"first_keys_loaded{i}") for i in range(len(lots))]
        s_wk = sem("window_keys_ready")
        s_oh, s_cnt, s_cev = sem("onehots_ready"), sem("counts_done"), sem("counts_evicted")
        s_zhi, s_wg = sem("z_hi_ready"), sem("gcn_weights_split")
        s_z, s_zev, s_y, s_yev, s_agg = sem("z_done"), sem("z_parts_ready"), sem("y_done"), sem("y_evicted"), sem("agg_ready")
        s_stat = sem("stats_ready")
        g_xst, g_xsd = sem("gen_xs_staged"), sem("gen_xs_in_dram")
        g_row, g_oh, g_mm, g_add, g_y, g_u, g_idx, g_idx2 = (sem("gen_rows_gathered"), sem("gen_onehot_ready"), sem("gen_product_done"),
                                              sem("gen_z_added"), sem("gen_y_done"), sem("gen_u_ready"), sem("gen_index_ready"), sem("gen_key_ready"))

        g_turn = sem("gen_turn")
        windows = NG * GW + TAILW

        def three(into, pairs):
            last = None
            terms = [(a[i], b[j]) for a, b in pairs for i, j in ((0, 0), (0, 1), (1, 0))]
            for n, (a, b) in enumerate(terms):
                last = nc.tensor.matmul(into, a, b, start=(n == 0), stop=(n == len(terms) - 1))
            return last

        def degree_onehots(i, j):
            at = bass.ds(HS * HR * i + HR * j, HR)
            nc.vector.tensor_tensor(hist_lo[:, j], iota_h[0:EP, 0:HLO].unsqueeze(1).to_broadcast([EP, HR, HLO]),
                                    dstlo[:, at].unsqueeze(2).to_broadcast([EP, HR, HLO]), ALU.is_equal)
            return nc.vector.tensor_tensor(hist_hi[:, j], iota_h[0:EP, 0:HHI].unsqueeze(1).to_broadcast([EP, HR, HHI]),
                                           dsthi[:, at].unsqueeze(2).to_broadcast([EP, HR, HHI]), ALU.is_equal)

        def load_keys(engine, first, count, slot, done=None):
            for w in range(count):
                at = engine.value_load(row[0:1, bass.ds(first + w, 1)], min_val=0, max_val=2 * E)
                engine.dma_start(ekeys[:, slot, w, :, :].rearrange("p k c -> p (k c)"),
                                 keys_d[bass.ds(at, 2 * CAP)].rearrange("(p c) -> p c", p=P)).then_inc(done[w] if done else s_ek[slot], 16)

        def columns(w):
            return P * (w // WPT) + WIN * (w % WPT), min(WIN, P - WIN * (w % WPT))

        def g_after(g, first):
            return not isinstance(g, int) or g >= first

        def parity(g):
            return g % 2 if isinstance(g, int) else bass.ds(g % 2, 1)

        def agg_at(g, m, cols):
            return agg[:, bass.ds(GN * g + m * NPAD, cols)]

        block = ctx1.enter_context(nc.Block())

        @block.sync
        def _(sp):
            sp.dma_start(dsti[:], dst.rearrange("(p c) -> p c", p=EP)).then_inc(s_dst, 16)
            sp.dma_start(srci[:], src.rearrange("(p c) -> p c", p=EP)).then_inc(s_edge, 16)
            sp.dma_start(nexti[0:EP - 1, :], dst[1:1 + (EP - 1) * EC].rearrange("(p c) -> p c", p=EP - 1)).then_inc(s_edge, 16)
            sp.dma_start(nexti[EP - 1:EP, 0:EC - 1], dst[1 + (EP - 1) * EC:E].rearrange("(p c) -> p c", p=1)).then_inc(s_edge, 16)
            sp.dma_start(nexti[EP - 1:EP, EC - 1:EC], dst[E - 1:E].rearrange("(p c) -> p c", p=1)).then_inc(s_edge, 16)
            sp.dma_start(wgcn[:], W.rearrange("(k p) n -> p k n", p=P)).then_inc(s_wt, 16)
            with nc.allow_non_contiguous_dma(reason="bias, one value per partition"):
                sp.dma_start(biasT[:], bias.rearrange("(k p) -> p k", p=P)).then_inc(s_wt, 16)
            sp.wait_ge(s_packed, 2)
            sp.dma_start(keys_d[0:2 * E].rearrange("(p c) -> p c", p=EP), pack[:].rearrange("p c k -> p (c k)")).then_inc(s_keys, 16)
            sp.dma_start(keys_d[2 * E:2 * (E + CAP)].rearrange("(p c) -> p c", p=P), padk[:]).then_inc(s_keys, 16)
            sp.wait_ge(s_keys, 32)
            sp.wait_ge(s_row, 1)

            load_keys(sp, 0, BK, 0, [s for s, n in zip(s_first, lots) for _ in range(n)])
            load_keys(sp, BK * 2, BK, 2)
            with sp.Fori(1, NG) as g:
                for slot in (0, 2):
                    sp.wait_ge(s_oh, GW * (g - 1) + BK * (slot + 1))
                    sp.sem_inc(s_turn, 1)
                    load_keys(sp, GW * g + BK * slot, BK, slot)
            sp.wait_ge(s_oh, GW * (NG - 1) + BK)
            load_keys(sp, GW * NG, TAILW, 0)
            with nc.allow_non_contiguous_dma(reason="one value per partition"):
                sp.dma_start(gammaT[:], gamma.rearrange("(k p) -> p k", p=P)).then_inc(t_gb, 16)
                sp.dma_start(betaT[:], beta.rearrange("(k p) -> p k", p=P)).then_inc(t_gb, 16)
                sp.dma_start(rb1T[:], rb1.rearrange("(k p) -> p k", p=P)).then_inc(t_w, 16)
                sp.dma_start(rw1s[:], rw1.rearrange("(k p) n -> p k n", p=P)).then_inc(t_w, 16)
                sp.dma_start(rw2s[:], rw2).then_inc(t_w, 16)
                sp.dma_start(rb2b[:], rb2.rearrange("(o n) -> o n", o=1).to_broadcast([P, NEXP])).then_inc(t_w, 16)
                for layer, b in enumerate((b1, b2)):
                    for m in range(DH):
                        sp.dma_start(b12T[:, :, layer, m], b[:, P * m:P * m + P].rearrange("e p -> p e")).then_inc(t_raw, 16)
            sp.dma_start(b3b[:].rearrange("p e d -> p (e d)"), b3.rearrange("(o e) d -> o (e d)", o=1).to_broadcast([P, NEXP * D])).then_inc(t_raw, 16)

        @block.gpsimd
        def _(gp):
            nc.gpsimd.iota(iota_i[:], pattern=[[1, GN]], base=0, channel_multiplier=0)
            nc.gpsimd.iota(diff_i[:], pattern=[[1, P]], base=0, channel_multiplier=-1)
            nc.gpsimd.iota(mask_i[:], pattern=[[WIN, WPT]], base=0, channel_multiplier=-1)
            nc.gpsimd.iota(goff_i[:], pattern=[[-GN, NG + 1]], base=0, channel_multiplier=0)
            nc.gpsimd.iota(win_i[:], pattern=[[CNT, windows]], base=0, channel_multiplier=0).then_inc(s_cst, 1)
            gp.wait_ge(s_dk, 1)
            for j in range(HS2):
                at = slice(HS * HR * ROUNDS + HR * j, HS * HR * ROUNDS + HR * j + HR)
                nc.gpsimd.tensor_tensor(hist2_lo[:, j], iota_h[0:EP, 0:HLO].unsqueeze(1).to_broadcast([EP, HR, HLO]),
                                        dstlo[:, at].unsqueeze(2).to_broadcast([EP, HR, HLO]), ALU.subtract)
                nc.gpsimd.tensor_tensor(hist2_hi[:, j], iota_h[0:EP, 0:HHI].unsqueeze(1).to_broadcast([EP, HR, HHI]),
                                        dsthi[:, at].unsqueeze(2).to_broadcast([EP, HR, HHI]), ALU.subtract).then_inc(s_hdiff, 1)
            for t in range(NT):
                gp.wait_ge(s_pool, t + 1)
                nc.gpsimd.tensor_tensor(xx[:, t, :], xx[:, t, :], xn[:, t, :], ALU.add).then_inc(s_xn, 1)

            gp.wait_ge(s_wt, 32)
            nc.gpsimd.tensor_copy(wgh[:], wgcn[:]).then_inc(s_wg, 1)
            gp.wait_ge(s_wg, 1)
            nc.gpsimd.tensor_tensor(wgl[:], wgcn[:], wgh[:].bitcast(fp32), ALU.subtract).then_inc(s_wg, 1)
            gp.wait_ge(s_keys, 32)
            gp.wait_ge(s_row, 1)
            gp.sem_inc(s_gturn, 1)
            for slot in (1, 3):
                load_keys(gp, BK * slot, BK, slot)
            with gp.Fori(1, NG) as g:
                for slot in (1, 3):
                    gp.wait_ge(s_oh, GW * (g - 1) + BK * (slot + 1))
                    gp.sem_inc(s_gturn, 1)
                    load_keys(gp, GW * g + BK * slot, BK, slot)

            gp.wait_ge(s_flag, 1)
            general = gp.value_load(flag[0:1, 0:1], min_val=0, max_val=2 * E)
            with gp.If(general > 0):
                gp.wait_ge(g_xst, 1)
                gp.dma_start(xs_d.rearrange("(t p) d -> p t d", p=P), gen_xs[:, :].rearrange("p (t d) -> p t d", t=NT)).then_inc(g_xsd, 16)
                gp.wait_ge(g_xsd, 16)
                with gp.Fori(0, NG + 1) as g:
                    with gp.Fori(0, EC) as c:
                        gp.wait_ge(g_add, (EC + 1) * g + c + 1)
                        nc.gpsimd.tensor_copy(gidx[:], srci[:, bass.ds(c, 1)]).then_inc(g_idx, 1)
                        gp.wait_ge(g_idx, EC * g + c + 1)
                        gp.sem_inc(g_turn, 1)
                        gp.indirect_dma_start(out=gen_rows, out_offset=None, in_=xs_d[:, :],
                                              in_offset=bass.IndirectOffsetOnAxis(ap=gidx[:, 0:1], axis=0)).then_inc(g_row, 16)

        @block.scalar
        def _(act):
            act.dma_start(xx[:, 0:FULL, :], x[0:FULL * P, :].rearrange("(t p) d -> p t d", p=P)).then_inc(s_x, 16)
            act.wait_ge(s_cst, 2)
            act.dma_start(xx[0:LAST, FULL, :], x[FULL * P:N, :]).then_inc(s_x, 16)

            def degree_onehots_act(j):
                act.wait_ge(s_hdiff, j + 1)
                for part in (hist2_lo, hist2_hi):
                    nc.scalar.activation(part[:, j], part[:, j], ACT.Square).then_inc(s_hsq, 1)
                for i, part in enumerate((hist2_lo, hist2_hi)):
                    act.wait_ge(s_hsq, 2 * j + i + 1)
                    ins = nc.scalar.activation(part[:, j], part[:, j], ACT.Relu, scale=-1.0, bias=ones[0:EP, 0:1])
                ins.then_inc(s_hoh2, 1)

            for j in range(HS2 - 1):
                degree_onehots_act(j)
            act.wait_ge(s_var, 1)
            nc.scalar.activation(rstd[:], mv[:, :, 1], ACT.Sqrt, bias=eps1[:]).then_inc(s_std, 1)
            degree_onehots_act(HS2 - 1)
            act.wait_ge(s_rstd, 1)
            for t in range(NT):
                nc.scalar.activation(xn[:, t, :], xx[:, t, :], ACT.Identity, bias=nmr[:, t:t + 1], scale=rstd[:, t:t + 1]).then_inc(s_pool, 1)
            act.wait_ge(s_deg, 1)
            nc.scalar.activation(dinv[:], deg[:], ACT.Sqrt).then_inc(s_sqd, 1)
            def evict_z(g, c, cols=HG):
                act.wait_ge(s_z, 2 * g + c + 1)
                nc.scalar.activation(zh[:, :, HG * c:HG * c + cols], psZ[c][:].rearrange("p (h n) -> p h n", h=DH)[:, :, 0:cols], ACT.Copy).then_inc(s_zhi, 1)

            def add_bias(g, cols):
                for m in range(DH):
                    act.wait_ge(s_yev, 2 * g + m + 1)
                    at = agg_at(g, m, cols)
                    nc.scalar.activation(at, ubuf[:, m, 0:cols], ACT.Identity, bias=biasT[:, m:m + 1]).then_inc(s_agg, 1)

            def step(g, wins):
                for w in range(wins):
                    act.wait_ge(s_cnt, GW * g + w + 1)
                    at, n = columns(w)
                    nc.scalar.activation(C[:, parity(g), :, at:at + n],
                                         psC[w % 4][:, 0:CNT].rearrange("p (s n) -> p s n", s=NT)[:, :, 0:n], ACT.Copy).then_inc(s_cev, 1)
                    if isinstance(g, int) and g == 0 and w < NT:
                        if w == 0:
                            act.wait_ge(s_dinv, 1)
                            act.wait_ge(s_pool, NT)
                        nc.scalar.activation(xs[:, 0, w, :], xn[:, w, :], ACT.Copy, scale=dinvs[:, w:w + 1]).then_inc(s_xhi, 1)
                    if isinstance(g, int) and g == 0 and 18 <= w < NT + 18:
                        t = w - 18
                        nc.scalar.activation(diag4[:, t // 4, P * (t % 4):P * (t % 4) + P], identf[:], ACT.Copy, scale=dinvz[:, t:t + 1]).then_inc(s_diag, 1)
                    if g_after(g, 1) and w == 1:
                        if g_after(g, 2):
                            act.wait_ge(s_y, 2 * g - 2)
                        evict_z(g - 1, 0)
                    if g_after(g, 1) and w == 23:
                        evict_z(g - 1, 1)
                    if g_after(g, 1) and w == 34:
                        add_bias(g - 1, GN)

            step(0, GW)
            for g in range(NG + 1):
                act.wait_ge(s_dbmm, g + 1)
                cols = GN if g < NG else P
                nc.scalar.activation(dinvb[:, GN * g:GN * g + cols], psY[g % 2][:, 0:cols], ACT.Copy).then_inc(s_dinvb, 1)
            act.wait_ge(s_xs, NT)
            act.wait_ge(s_xn, NT)
            step(1, GW)
            with act.Fori(2, NG) as g:
                step(g, GW)
            step(NG, TAILW)
            evict_z(NG - 1, 1)
            act.wait_ge(s_y, 2 * NG)
            evict_z(NG, 0, TAILN)
            add_bias(NG - 1, GN)
            add_bias(NG, TAILN)


        @block.vector
        def _(dve):
            chain = [0]

            def link(ins):
                chain[0] += 1
                ins.then_inc(s_dve, 1)
                dve.wait_ge(s_dve, chain[0])

            nc.vector.memset(eps1[:], EPS)
            nc.vector.memset(ones[:], 1.0)
            nc.vector.memset(padk[:], -float(CNT * (windows + 1)))
            nc.vector.memset(xx[:, FULL, :], 0.0).then_inc(s_cst, 1)
            dve.wait_ge(s_cst, 2)
            nc.vector.tensor_copy(iota_h[:], iota_i[:, 0:CNT])
            nc.vector.tensor_copy(win_off[:], win_i[:])
            nc.vector.tensor_scalar(ident16[:], diff_i[:], 0.0, None, ALU.is_equal)
            nc.vector.tensor_scalar(identf[:], diff_i[:], 0.0, None, ALU.is_equal)
            nc.vector.tensor_scalar(below[:], mask_i[:], 0.0, None, ALU.is_gt)
            nc.vector.tensor_scalar(upper[:], diff_i[0:NT, 0:NT], 0.0, None, ALU.is_gt)
            dve.wait_ge(s_dst, 16)
            nc.vector.tensor_scalar(ti[:, 0, :], dsti[:], HLO - 1, None, ALU.bitwise_and)
            link(nc.vector.tensor_scalar(ti[:, 1, :], dsti[:], 6, None, ALU.logical_shift_right))
            nc.vector.tensor_copy(dstlo[:], ti[:, 0, :])
            nc.vector.tensor_copy(dsthi[:], ti[:, 1, :]).then_inc(s_dk, 1)
            dve.wait_ge(s_dk, 1)

            def degree(i, first=False):
                for j in range(HS):
                    if not first:
                        dve.wait_ge(s_hmm, HS * (i - 1) + j + 1)
                    degree_onehots(i, j).then_inc(s_hoh, 1)

            degree(0, True)
            dve.wait_ge(s_edge, 64)
            nc.vector.tensor_scalar(ti[:, 0, :], srci[:], 7, None, ALU.logical_shift_right)
            nc.vector.tensor_scalar(ti[:, 1, :], dsti[:], 7, None, ALU.logical_shift_right)
            nc.vector.tensor_scalar(ti[:, 3, :], srci[:], P - 1, None, ALU.bitwise_and)
            link(nc.vector.tensor_scalar(ti[:, 2, :], dsti[:], P - 1, None, ALU.bitwise_and))
            link(nc.vector.tensor_scalar(ti[:, 2, :], ti[:, 2, :], 43.0, None, ALU.mult))
            link(nc.vector.tensor_scalar(ti[:, 2, :], ti[:, 2, :], 9, None, ALU.logical_shift_right))
            nc.vector.tensor_copy(pack[:, :, 0], ti[:, 3, :]).then_inc(s_packed, 1)
            link(nc.vector.scalar_tensor_tensor(dstf[:], ti[:, 1, :], float(CNT * WPT - P), dsti[:], ALU.mult, ALU.add))
            link(nc.vector.scalar_tensor_tensor(dstf[:], ti[:, 2, :], float(CNT - WIN), dstf[:], ALU.mult, ALU.add))
            nc.vector.scalar_tensor_tensor(pack[:, :, 1], ti[:, 0, :], float(WIN), dstf[:], ALU.mult, ALU.add).then_inc(s_packed, 1)
            dve.wait_ge(s_x, 32)
            for t in range(NT):
                last = nc.vector.bn_stats(st6[:, t, :], xx[:, t, :])
            link(last)
            for t in range(NT):
                last = nc.vector.bn_aggr(mv[:, t, :], st6[:, t, :])
            last.then_inc(s_var, 1)
            degree(1)
            dve.wait_ge(s_std, 1)
            link(nc.vector.reciprocal(rstd[:], rstd[:]))
            nc.vector.scalar_tensor_tensor(nmr[:], mv[:, :, 0], -1.0, rstd[:], ALU.mult, ALU.mult).then_inc(s_rstd, 1)
            with dve.Fori(2, ROUNDS) as i:
                degree(i)
            dve.wait_ge(s_hmm, EC // HR)
            counts = psC[0][0:HLO, 0:HHI].rearrange("p (t k) -> p k t", k=2)
            nc.vector.tensor_copy(degr[0:HLO, :], counts[:, 0, :])
            link(nc.vector.tensor_copy(degr[HLO:P, :], counts[:, 1, :]))
            nc.vector.tensor_scalar(deg[:], degr[:], 1.0, 1.0, ALU.add, ALU.max).then_inc(s_deg, 1)
            dve.wait_ge(s_cum, 1)
            nc.vector.tensor_copy(total[:], psY[0][0:NT, 0:1]).then_inc(s_cumsb, 1)
            dve.wait_ge(s_pref, 1)
            nc.vector.tensor_scalar(row[:], psY[1][0:1, 0:NT * WPT], 2.0, None, ALU.mult).then_inc(s_row, 1)
            link(nc.vector.tensor_copy(rowf[:], psY[1][0:1, 0:NT * WPT]))
            link(nc.vector.tensor_tensor(over[:], rowf[:, 1:NT * WPT], rowf[:, 0:NT * WPT - 1], ALU.subtract))
            link(nc.vector.tensor_scalar(over[:], over[:], float(CAP), None, ALU.is_gt))
            nc.vector.reduce_sum(overs[:], over[:], AX.X)
            link(nc.vector.tensor_tensor(desc[:], dsti[:], nexti[:], ALU.is_gt))
            nc.vector.reduce_sum(descs[:], desc[:], AX.X).then_inc(s_over, 1)
            nc.vector.tensor_copy(dstf[:], dsti[:])
            dve.wait_ge(s_sqd, 1)
            link(nc.vector.reciprocal(dinv[:], dinv[:]))
            link(nc.vector.tensor_scalar(dinvz[:], dinv[:], 1.0 / XSCALE, None, ALU.mult))
            link(nc.vector.tensor_scalar(dinvs[:], dinv[:], XSCALE, None, ALU.mult))
            nc.vector.memset(gkey[:], 0.0).then_inc(s_dinv, 1)
            dve.wait_ge(s_flagmm, 1)
            nc.vector.tensor_copy(flag[:], psY[0][0:1, 16:17]).then_inc(s_flag, 1)

            def low_z(g, c, cols=HG):
                at = slice(HG * c, HG * c + cols)
                dve.wait_ge(s_zhi, 2 * g + c + 1)
                nc.vector.tensor_tensor(zl[:, :, at], psZ[c][:].rearrange("p (h n) -> p h n", h=DH)[:, :, 0:cols], zh[:, :, at].bitcast(fp32),
                                        ALU.subtract).then_inc(s_zev, 1)

            def neighbour_u(g, cols):
                for m in range(DH):
                    dve.wait_ge(s_y, 2 * g + m + 1)
                    nc.vector.tensor_tensor(ubuf[:, m, 0:cols], psY[m][:, 0:cols], dinvb[:, bass.ds(GN * g, cols)],
                                            ALU.mult).then_inc(s_yev, 1)

            def norm_stats(g, cols):
                for m in range(DH):
                    dve.wait_ge(s_agg, 2 * g + m + 1)
                    nc.vector.bn_stats(stats[:, m, bass.ds(g, 1), :].rearrange("p a b -> p (a b)"), agg_at(g, m, cols)).then_inc(s_stat, 1)

            def step(g, wins):
                for w in range(wins):
                    at, slot = GW * g + w, w // BK
                    begin = isinstance(g, int) and g == 0
                    ahead = [sum(lots[:i]) for i in range(len(lots))]
                    if w % BK == 0 or (begin and w in ahead):
                        if begin and slot == 0:
                            n = lots[ahead.index(w)]
                            dve.wait_ge(s_first[ahead.index(w)], 16 * n)
                        else:
                            n = min(BK, wins)
                            dve.wait_ge(s_ek[slot], 16 * BK * (g - (slot == 0)) + 16 * n)
                        if not begin:
                            dve.wait_ge(s_oh, GW * (g - 1) + BK * (slot + 1))
                        lot = slice(w % BK, w % BK + n)
                        nc.vector.tensor_tensor(wkeys[:, slot, lot, :], ekeys[:, slot, lot, :, 1],
                                                win_off[:, bass.ds(at, n)].unsqueeze(2).to_broadcast([P, n, KCH]),
                                                ALU.subtract).then_inc(s_wk, 1)
                        extra = len(lots) - 1
                        dve.wait_ge(s_wk, ahead.index(w) + 1 if begin and slot == 0 else NS * g + slot + 1 + extra)
                    if not (isinstance(g, int) and g == 0 and w < OHR):
                        dve.wait_ge(s_cnt, at - OHR + 1)
                    r = w % OHR
                    for k in range(KCH):
                        nc.vector.tensor_scalar(oh_src[:, r, k, :], iota_h[:, 0:P], ekeys[:, slot, w % BK, k, 0:1], None, ALU.is_equal)
                        last = nc.vector.tensor_scalar(oh_key[:, r, k, :], iota_h[:], wkeys[:, slot, w % BK, k:k + 1], None, ALU.is_equal)
                    last.then_inc(s_oh, 1)
                    if isinstance(g, int) and g == 0 and 4 <= w < NT + 4:
                        t = w - 4
                        dve.wait_ge(s_xhi, t + 1)
                        nc.vector.scalar_tensor_tensor(xs[:, 1, t, :], xn[:, t, :], dinvs[:, t:t + 1], xs[:, 0, t, :],
                                                       ALU.mult, ALU.subtract).then_inc(s_xs, 1)
                    if g_after(g, 1) and w == 3:
                        low_z(g - 1, 0)
                    if g_after(g, 1) and w == 25:
                        low_z(g - 1, 1)
                    if g_after(g, 1) and w == 31:
                        neighbour_u(g - 1, GN)
                    if g_after(g, 1) and w == 40:
                        norm_stats(g - 1, GN)

            step(0, GW)
            step(1, GW)
            with dve.Fori(2, NG) as g:
                step(g, GW)
            step(NG, TAILW)
            low_z(NG - 1, 1)
            low_z(NG, 0, TAILN)
            neighbour_u(NG - 1, GN)
            norm_stats(NG - 1, GN)
            neighbour_u(NG, TAILN)
            norm_stats(NG, N - NG * GN)

            general = dve.value_load(flag[0:1, 0:1], min_val=0, max_val=2 * E)
            with dve.If(general > 0):
                dve.wait_ge(s_stat, 2 * (NG + 1))
                nc.vector.tensor_tensor(gen_xs[:, :], xs[:, 0, :, :].rearrange("p t d -> p (t d)"),
                                        xs[:, 1, :, :].rearrange("p t d -> p (t d)"), ALU.add).then_inc(g_xst, 1)

                def gen_group(g, cols, valid):
                    base = (EC + 1) * g
                    dve.wait_ge(g_mm, base + 1)
                    nc.vector.tensor_copy(zbuf[:, 0, 0:cols], psZ[0][:, 0:cols])
                    nc.vector.tensor_copy(zbuf[:, 1, 0:cols], psZ[1][:, 0:cols]).then_inc(g_add, 1)
                    with dve.Fori(0, EC) as c:
                        dve.wait_ge(g_add, base + c + 1)
                        nc.vector.tensor_tensor(gkey[:], dstf[:, bass.ds(c, 1)], goff_i[0:EP, bass.ds(g, 1)], ALU.add).then_inc(g_idx2, 1)
                        dve.wait_ge(g_idx2, EC * g + c + 1)
                        nc.vector.tensor_scalar(gen_oh[:, 0:cols], iota_i[0:EP, 0:cols], gkey[:, 0:1], None, ALU.is_equal).then_inc(g_oh, 1)
                        dve.wait_ge(g_mm, base + c + 2)
                        nc.vector.tensor_tensor(zbuf[:, 0, 0:cols], zbuf[:, 0, 0:cols], psZ[0][:, 0:cols], ALU.add)
                        nc.vector.tensor_tensor(zbuf[:, 1, 0:cols], zbuf[:, 1, 0:cols], psZ[1][:, 0:cols], ALU.add).then_inc(g_add, 1)
                    dve.wait_ge(g_y, 2 * g + 2)
                    for m in range(DH):
                        at = agg_at(g, m, cols)
                        nc.vector.tensor_tensor(at, psY[m][:, 0:cols], dinvb[:, bass.ds(GN * g, cols)], ALU.mult).then_inc(g_u, 1)
                        dve.wait_ge(g_u, 4 * g + 2 * m + 1)
                        nc.vector.tensor_scalar(at, at, biasT[:, m:m + 1], None, ALU.add).then_inc(g_u, 1)
                        dve.wait_ge(g_u, 4 * g + 2 * m + 2)
                        nc.vector.bn_stats(stats[:, m, bass.ds(g, 1), :].rearrange("p a b -> p (a b)"), agg_at(g, m, valid))

                with dve.Fori(0, NG) as g:
                    gen_group(g, GN, GN)
                gen_group(NG, TAILN, N - NG * GN)

        @block.tensor
        def _(pe):
            def degree(i, first, final):
                for j in range(HS):
                    pe.wait_ge(s_hoh, HS * i + j + 1)
                    for r in range(HR):
                        last = nc.tensor.matmul(psC[0][0:HLO, 0:HHI], hist_lo[:, j, r, :], hist_hi[:, j, r, :],
                                                start=(first and j == 0 and r == 0), stop=(final and j == HS - 1 and r == HR - 1))
                    last.then_inc(s_hmm, 1)

            degree(0, True, False)
            with pe.Fori(1, ROUNDS - 1) as i:
                degree(i, False, False)
            for j in range(HS2):
                pe.wait_ge(s_hoh2, j + 1)
                for r in range(HR):
                    last = nc.tensor.matmul(psC[0][0:HLO, 0:HHI], hist2_lo[:, j, r, :], hist2_hi[:, j, r, :], start=False, stop=False)
                last.then_inc(s_hmm, 1)
            degree(ROUNDS - 1, False, True)
            pe.wait_ge(s_deg, 1)
            nc.tensor.matmul(psY[0][0:NT, 0:1], degr[:], ones[:, 0:1], start=True, stop=True).then_inc(s_cum, 1)
            starts = psY[1][0:1, 0:NT * WPT].rearrange("p (t j) -> p j t", j=WPT)
            for j in range(WPT):
                nc.tensor.matmul(starts[:, j, :], below[:, j:j + 1], degr[:], start=(j == 0), stop=False)
            pe.wait_ge(s_cumsb, 1)
            for j in range(WPT):
                last = nc.tensor.matmul(starts[:, j, :], total[:], upper[:], start=False, stop=(j == WPT - 1))
            last.then_inc(s_pref, 1)
            pe.wait_ge(s_over, 1)
            nc.tensor.matmul(psY[0][0:1, 16:17], descs[:], ones[0:EP, 0:1], start=True, stop=False)
            nc.tensor.matmul(psY[0][0:1, 16:17], overs[:], ones[0:1, 0:1], start=False, stop=True).then_inc(s_flagmm, 1)
            def sum_parts(g, c, cols=HG, tiles=2):
                for h in range(DH):
                    into = psZ[c][:, HG * h:HG * h + cols]
                    parts = [(p, s) for p in range(2) for s in range(NT)]
                    for i, (p, s) in enumerate(parts):
                        yield dict(out=into, lhsT=xs[:, p, s, P * h:P * h + P], rhs=C[:, parity(g), s, HG * c:HG * c + cols],
                                   start=(i == 0), stop=False, final=False,
                                   low=s + 1 if isinstance(g, int) and g == 0 and c + h == 0 and p == 1 else 0)
                    for j in range(tiles):
                        n = min(P, cols - P * j)
                        for p in range(2):
                            t = 4 * g + 2 * c + j
                            stop = j == tiles - 1 and p == 1
                            yield dict(out=into[:, P * j:P * j + n],
                                       lhsT=xs[:, p, bass.ds(t, 1), P * h:P * h + P].rearrange("p a b -> p (a b)") if not isinstance(g, int) else xs[:, p, t, P * h:P * h + P],
                                       rhs=ident16[:, 0:n], start=False, stop=stop, final=stop and h == DH - 1, low=0)

            def products(g, cols):
                for m in range(DH):
                    cs = slice(P * m, P * m + P)
                    three(psY[m][:, 0:cols], [((wgh[:, k, cs], wgl[:, k, cs]), (zh[:, k, 0:cols], zl[:, k, 0:cols])) for k in range(DH)]).then_inc(s_y, 1)

            def general_products(cols):
                for m in range(DH):
                    for k in range(DH):
                        last = nc.tensor.matmul(psY[m][:, 0:cols], wgcn[:, k, P * m:P * m + P], zbuf[:, k, 0:cols],
                                                start=(k == 0), stop=(k == DH - 1))
                    last.then_inc(g_y, 1)

            def run(todo, n):
                for _ in range(n):
                    m = next(todo, None)
                    if m is None:
                        return
                    final = m["final"]
                    if m["low"]:
                        pe.wait_ge(s_xs, m["low"])
                    ins = nc.tensor.matmul(m["out"], m["lhsT"], m["rhs"], start=m["start"], stop=m["stop"])
                    if final:
                        ins.then_inc(s_z, 1)

            def all_products(g, cols):
                pe.wait_ge(s_zev, 2 * g + 2 if cols == GN else 2 * g + 1)
                if g_after(g, 1):
                    pe.wait_ge(s_yev, 2 * g)
                products(g, cols)

            def step(g, wins):
                second = iter(sum_parts(g - 1, 1) if g_after(g, 1) else ())
                first = iter(sum_parts(g, 0))
                begin = 24
                for w in range(wins):
                    pe.wait_ge(s_oh, GW * g + w + 1)
                    if not (isinstance(g, int) and g == 0 and w < 4):
                        pe.wait_ge(s_cev, GW * g + w - 3)
                    for k in range(KCH):
                        last = nc.tensor.matmul(psC[w % 4][:, 0:CNT], oh_src[:, w % OHR, k, :], oh_key[:, w % OHR, k, :],
                                                start=(k == 0), stop=(k == KCH - 1))
                    last.then_inc(s_cnt, 1)
                    if g_after(g, 1) and w == 1:
                        pe.wait_ge(s_cev, GW * g)
                        if g_after(g, 2):
                            pe.wait_ge(s_zev, 2 * g - 2)
                    if w >= 1:
                        run(second, 5)
                    if w == begin:
                        pe.wait_ge(s_cev, GW * g + 2 * WPT)
                        pe.wait_ge(s_zev, 2 * g - 1) if g_after(g, 1) else pe.wait_ge(s_xhi, NT)
                    if w >= begin:
                        run(first, 5)
                    if g_after(g, 1) and w == 27:
                        products_of_last(g)
                if wins == GW:
                    run(first, 1000)
                else:
                    run(second, 1000)
                    pe.wait_ge(s_cev, GW * g + wins)
                    pe.wait_ge(s_zev, 2 * g - 1)
                    run(iter(sum_parts(g, 0, TAILN, 1)), 1000)
                    all_products(g - 1, GN)
                    all_products(g, TAILN)

            def products_of_last(g):
                pe.wait_ge(s_zev, 2 * g)
                if g_after(g, 2):
                    pe.wait_ge(s_yev, 2 * g - 2)
                products(g - 1, GN)

            pe.wait_ge(s_wt, 32)
            pe.wait_ge(s_wg, 2)
            step(0, GW)
            for g in range(NG + 1):
                cols = GN if g < NG else P
                pe.wait_ge(s_diag, min(NT, 4 * g + 4))
                if g >= 2:
                    pe.wait_ge(s_dinvb, g - 1)
                nc.tensor.matmul(psY[g % 2][:, 0:cols], ones[:], diag4[:, g, 0:cols], start=True, stop=True).then_inc(s_dbmm, 1)
            pe.wait_ge(s_dinvb, NG + 1)
            step(1, GW)
            with pe.Fori(2, NG) as g:
                step(g, GW)
            step(NG, TAILW)

            general = pe.value_load(flag[0:1, 0:1], min_val=0, max_val=2 * E)
            with pe.If(general > 0):
                def gen_group(g, cols, tiles):
                    base = (EC + 1) * g
                    for h in range(DH):
                        for j in range(tiles):
                            n = min(P, cols - P * j)
                            for p in range(2):
                                t = bass.ds(4 * g + j, 1)
                                last = nc.tensor.matmul(psZ[h][:, P * j:P * j + n], xs[:, p, t, P * h:P * h + P].rearrange("p a b -> p (a b)"),
                                                        ident16[:, 0:n], start=(p == 0 and j == 0), stop=(j == tiles - 1 and p == 1))
                    last.then_inc(g_mm, 1)
                    with pe.Fori(0, EC) as c:
                        pe.wait_ge(g_row, 16 * (EC * g + c) + 16)
                        pe.wait_ge(g_oh, EC * g + c + 1)
                        for h in range(DH):
                            last = nc.tensor.matmul(psZ[h][:, 0:cols], gen_rows[:, P * h:P * h + P], gen_oh[:, 0:cols], start=True, stop=True)
                        last.then_inc(g_mm, 1)
                    pe.wait_ge(g_add, base + EC + 1)
                    general_products(cols)

                pe.wait_ge(g_xst, 1)
                with pe.Fori(0, NG) as g:
                    gen_group(g, GN, 4)
                gen_group(NG, TAILN, 1)

        ctx1.close()

        wraw12 = sb("wraw12", [P, NEXP, 2, DH, D], fp32, ctx2)
        wraw3 = sb("wraw3", [P, NEXP, DH, D], fp32, ctx2)
        w12h, w12l = (sb(n, [P, 2, 2, DH, D], f32r, ctx2) for n in ("w12h", "w12l"))
        w3h, w3l = (sb(n, [P, 2, DH, D], f32r, ctx2) for n in ("w3h", "w3l"))
        frows = sb("frows", [P, 2, UT, FW], fp32, ctx2)
        fuh, ful = (sb(n, [P, DH, GN], f32r, ctx2) for n in ("fuh", "ful"))
        r1, r2 = (sb(n, [P, DH, GN], fp32, ctx2) for n in ("r1", "r2"))
        h1h, h1l, h2h, h2l = (sb(n, [P, DH, GN], f32r, ctx2) for n in ("h1h", "h1l", "h2h", "h2l"))
        ybuf = sb("ybuf", [P, 2, GN // P, D], fp32, ctx2)
        b12u = sb("b12u", [P, 2, 2, DH], fp32, ctx2)
        rw1h, rw1l = sb("rw1h", [P, DH, RH], f32r, ctx2), sb("rw1l", [P, DH, RH], f32r, ctx2)
        mvb, bnr = sb("mvb", [P, DH, 2], fp32, ctx2), sb("bnr", [P, DH], fp32, ctx2)
        bna, bnb = sb("bna", [P, DH], fp32, ctx2), sb("bnb", [P, DH], fp32, ctx2)
        st6b, mv2, rstd2 = sb("st6b", [P, NT, 6], fp32, ctx2), sb("mv2", [P, NT, 2], fp32, ctx2), sb("rstd2", [P, NT], fp32, ctx2)
        lg, pr, eq, g12 = (sb(n, [P, NT, NEXP], fp32, ctx2) for n in ("lg", "pr", "eq", "g12"))
        f12, eq2 = (sb(n, [P, 2, NT, NEXP], fp32, ctx2) for n in ("f12", "eq2"))
        f1, f2 = f12[:, 0], f12[:, 1]
        m1, m2, mk, e2, g1, g2 = (sb(n, [P, NT], fp32, ctx2) for n in ("m1", "m2", "mk", "e2", "g1", "g2"))
        rank_i, rank = sb("rank_i", [P, NEXP], i32, ctx2), sb("rank", [P, NEXP], fp32, ctx2)
        gate = sb("gate", [P, NT, NEXP], fp32, ctx2)
        lane_i, lane = sb("lane_i", [P, P], i32, ctx2), sb("lane", [P, P], fp32, ctx2)
        order_i, earlier, ones2 = sb("order_i", [P, P], i32, ctx2), sb("earlier", [P, P], fp32, ctx2), sb("ones2", [P, P], fp32, ctx2)
        token_i, token = sb("token_i", [P, NT], i32, ctx2), sb("token", [P, NT], fp32, ctx2)
        here, tile_no, away = sb("here", [P, NT], fp32, ctx2), sb("tile_no", [P, 2, NT], fp32, ctx2), sb("away", [P, NT], fp32, ctx2)
        lane_no = sb("lane_no", [P, 1], fp32, ctx2)
        lane_h = sb("lane_h", [P, P], fp16, ctx2)
        tile_i = sb("tile_i", [P, 2, NT], i32, ctx2)
        SH = 16
        run = [sb(f"run{i}", [P, SH + NT, NEXP], fp32, ctx2) for i in range(2)]
        chosen, place = sb("chosen", [P, NT, NEXP], fp32, ctx2), sb("place", [P, NT, NEXP], fp32, ctx2)
        UNE = -(-N // UN)
        steps_i, steps, exceeded = sb("steps_i", [P, UNE], i32, ctx2), sb("steps", [P, UNE], fp32, ctx2), sb("exceeded", [P, NEXP, UNE], fp32, ctx2)
        tokens_of, units = sb("tokens_of", [P, NEXP], fp32, ctx2), sb("units", [P, NEXP], fp32, ctx2)
        ends = [sb(f"ends{i}", [P, 4 + NEXP], fp32, ctx2) for i in range(2)]
        base = sb("base", [P, NEXP], fp32, ctx2)
        past, of_unit = sb("past", [P, UMAX, NEXP], fp32, ctx2), sb("of_unit", [P, UMAX], fp32, ctx2)
        expert_of, used = sb("expert_of", [P, UMAX], i32, ctx2), sb("used", [P, 1], i32, ctx2)
        pos, pos_i, plo_i, phi_i = sb("pos", [P, 2, NT], fp32, ctx2), *(sb(n, [P, 2, NT], i32, ctx2) for n in ("pos_i", "plo_i", "phi_i"))
        plo, phi = sb("plo", [P, 2, NT], fp32, ctx2), sb("phi", [P, 2, NT], fp32, ctx2)
        slot_eq, slot_hi = sb("slot_eq", [P, 2 * NT, SC], fp16, ctx2), sb("slot_hi", [P, 2 * NT, 2, SC], fp16, ctx2)
        slot_lo = xx[:].rearrange("p t d -> p (t d)").bitcast(fp16)[:, 0:2 * NT * P].rearrange("p (t n) -> p t n", n=P)
        found = sb("found", [P, SC], fp32, ctx2)
        empty, beyond = sb("empty", [P, SC], fp32, ctx2), sb("beyond", [P, 1], fp32, ctx2)
        gidx_all, sidx_all = sb("gidx_all", [P, SC], i32, ctx2), sb("sidx_all", [P, SC], i32, ctx2)
        gidx2, sidx = sb("gidx2", [P, 2, UT], i32, ctx2), sb("sidx", [P, UT], i32, ctx2)
        sgate = sb("sgate", [P, SC], fp32, ctx2)
        ftok = ybuf
        warm = sb("warm", [P, 1], fp32, ctx2)
        nm2 = sb("nm2", [P, NT], fp32, ctx2)
        bank = [ps(f"bank{i}", [P, 512], ctx2) for i in range(8)]
        f_d = nc.dram_tensor("f_d", [N, FW], fp32, kind="Internal").ap()

        t_act, t_gp = sem("act_turn"), sem("pool_turn")
        t_dve = sem("dve_chain")
        t_bnv, t_bns, t_bn = sem("bn_var_ready"), sem("bn_std_ready"), sem("bn_ready")
        t_relu, t_tr, t_x1 = sem("relu_ready"), sem("y_transposed"), sem("x1_ready")
        t_var2, t_v2, t_s2, t_f, t_ft, t_fh, t_fl = (sem("ln_var_ready"), sem("ln_scale_ready"), sem("ln_std_ready"), sem("f_ready"), sem("f_transposed"),
                                             sem("f_hi_ready"), sem("f_parts_ready"))
        t_rw, t_rh, t_rhs, t_lg = sem("router_weights_split"), sem("router_hidden_done"), sem("router_hidden_ready"), sem("logits_done")
        t_sub, t_exp, t_dm, t_e2, t_gate = (sem("logits_shifted"), sem("exp_ready"), sem("gap_ready"), sem("gap_exp_ready"), sem("gates_ready"))
        t_tab, t_cho, t_pfx, t_moh, t_prod, t_slots = (sem("iotas_ready"), sem("choices_counted"), sem("prefixes_done"),
                                                       sem("slot_onehots_ready"), sem("slot_products_done"), sem("slot_tables_ready"))
        t_eq, t_tile, t_lane = sem("slot_places_ready"), sem("slot_tiles_ready"), sem("slot_lanes_ready")
        t_init, t_fd, t_gd = sem("x1_stored"), [sem(f"f_stored{i}") for i in range(2)], sem("gates_stored")
        u_gix, u_six, u_fc = sem("unit_gather_index_ready"), sem("unit_scatter_index_ready"), sem("unit_gates_copied")
        u_g = [sem(f"unit_rows_gathered{i}") for i in range(2)]
        u_w12h, u_w12, u_w3h, u_w3 = sem("unit_w12_hi_ready"), sem("unit_w12_ready"), sem("unit_w3_hi_ready"), sem("unit_w3_ready")
        u_T, u_fh, u_fl = sem("unit_transposed"), sem("unit_f_hi_ready"), sem("unit_f_ready")
        u_l, u_r, u_h = [sem(f"unit_layer{i}_done") for i in (1, 2)], [sem(f"unit_relu{i}_ready") for i in (1, 2)], [sem(f"unit_parts{i}_ready") for i in (1, 2)]
        u_l3, u_ys, u_y, u_sc = sem("unit_layer3_done"), sem("unit_layer3_read"), sem("unit_output_ready"), sem("unit_output_added")

        GROUPS = NG + 1
        rb_, hb = (r1, r2), ((h1h, h1l), (h2h, h2l))
        fparts = ((fuh, ful), (h1h, h1l))

        def tiles_of(g):
            return 4 if g < NG else 1

        def rows_of(t):
            return P if t < FULL else TAILN

        def units_loop(engine, step, finish):
            step(0, 0)
            step(1, 1)
            with engine.Fori(1, UMIN // 2) as pair:
                step(2 * pair, 0)
                step(2 * pair + 1, 1)
            step(UMIN - 1, 0)
            many = engine.value_load(used[0:1, 0:1], min_val=UMIN, max_val=UMAX)
            with engine.If(many < UMIN + 1):
                finish(UMIN - 1, 0)
            for u in range(UMIN, UMAX):
                with engine.If(many > u):
                    step(u, u % 2)
                    with engine.If(many < u + 2):
                        finish(u, u % 2)

        def after(u, first):
            return not isinstance(u, int) or u >= first

        block2 = ctx2.enter_context(nc.Block())

        @block2.sync
        def _(sp):
            def load_weights(i):
                layer, e = i // NEXP, i % NEXP
                sp.dma_start(wraw12[:, e, layer], (w1, w2)[layer][e].rearrange("(k p) n -> p k n", p=P)).then_inc(t_raw, 16)

            load_weights(0)
            load_weights(1)
            for g in range(GROUPS):
                sp.wait_ge(t_f, g + 1)
                if g < NG:
                    sp.dma_start(f_d[GN * g:GN * (g + 1), 0:D].rearrange("(t p) d -> p t d", p=P), ftok[:, g % 2, :, :]).then_inc(t_fd[g % 2], 16)
                else:
                    sp.dma_start(f_d[FULL * P:N, 0:D], ftok[0:LAST, g % 2, 0, :]).then_inc(t_fd[g % 2], 16)
                for i in range(2 * g + 2, min(2 * g + 4, 2 * NEXP)):
                    load_weights(i)
            sp.dma_start(wraw3[:].rearrange("p e k n -> p (e k) n"), w3.rearrange("e (k p) n -> p (e k) n", p=P)).then_inc(t_raw, 16)
            sp.wait_ge(t_x1, NT)
            sp.dma_start(out[0:FULL * P, :].rearrange("(t p) d -> p t d", p=P), xx[:, 0:FULL, :]).then_inc(t_init, 16)
            sp.dma_start(out[FULL * P:N, :], xx[0:LAST, FULL, :]).then_inc(t_init, 16)
            sp.wait_ge(t_gate, 1)
            with nc.allow_non_contiguous_dma(reason="the gates at the end of the rows"):
                sp.dma_start(f_d[0:FULL * P, D:FW].rearrange("(t p) e -> p t e", p=P), gate[:, 0:FULL, :]).then_inc(t_gd, 16)
                sp.dma_start(f_d[FULL * P:N, D:FW], gate[0:LAST, FULL, :]).then_inc(t_gd, 16)

        @block2.gpsimd
        def _(gp):
            nc.gpsimd.iota(rank_i[:], pattern=[[-1, NEXP]], base=NEXP, channel_multiplier=0)
            nc.gpsimd.iota(lane_i[:], pattern=[[1, P]], base=0, channel_multiplier=0)
            nc.gpsimd.iota(tile_i[:], pattern=[[0, 2], [1, NT]], base=1, channel_multiplier=0)
            nc.gpsimd.iota(steps_i[:], pattern=[[UN, UNE]], base=0, channel_multiplier=0)
            nc.gpsimd.iota(order_i[:], pattern=[[1, P]], base=0, channel_multiplier=-1)
            nc.gpsimd.iota(token_i[:], pattern=[[P, NT]], base=1, channel_multiplier=1).then_inc(t_tab, 1)
            gp.wait_ge(t_w, 16 * 4)
            nc.gpsimd.tensor_copy(rw1h[:], rw1s[:]).then_inc(t_rw, 1)
            gp.wait_ge(t_rw, 1)
            nc.gpsimd.tensor_tensor(rw1l[:], rw1s[:], rw1h[:].bitcast(fp32), ALU.subtract).then_inc(t_rw, 1)
            for i in range(2 * NT // MB):
                at = slice(MB * i, MB * i + MB)
                gp.wait_ge(t_eq, i + 1)
                nc.gpsimd.tensor_tensor(slot_hi[:, at, 0, :], slot_eq[:, at, :],
                                        tile_no[:].rearrange("p k t -> p (k t)")[:, at].unsqueeze(2).to_broadcast([P, MB, SC]), ALU.mult).then_inc(t_tile, 1)
            gp.wait_ge(t_slots, 1)
            for X in range(2):
                gp.wait_ge(t_fd[X], 16 * ((GROUPS + 1 - X) // 2))
            gp.wait_ge(t_gd, 32)
            gp.wait_ge(t_init, 32)

            def gather(v, X):
                if after(v, 2):
                    gp.wait_ge(u_T, 2 * v - 2)
                    gp.wait_ge(u_fc, v - 1)
                    gp.sem_inc(t_gp, 1)
                nc.gpsimd.tensor_copy(gidx2[:, X, :], gidx_all[:, bass.ds(UT * v, UT)]).then_inc(u_gix, 1)
                gp.wait_ge(u_gix, v + 1)
                gp.sem_inc(t_gp, 1)
                for j in range(UT):
                    gp.indirect_dma_start(out=frows[:, X, j, :], out_offset=None, in_=f_d[:, :],
                                          in_offset=bass.IndirectOffsetOnAxis(ap=gidx2[:, X, j:j + 1], axis=0)).then_inc(u_g[X], 16)

            def scatter(v, X):
                if after(v, 1):
                    gp.wait_ge(u_sc, 16 * UT * v)
                gp.sem_inc(t_gp, 1)
                nc.gpsimd.tensor_copy(sidx[:], sidx_all[:, bass.ds(UT * v, UT)]).then_inc(u_six, 1)
                gp.wait_ge(u_six, v + 1)
                for j in range(UT):
                    gp.wait_ge(u_y, UT * v + j + 1)
                    gp.sem_inc(t_gp, 1)
                    gp.indirect_dma_start(out=out[:, :], out_offset=bass.IndirectOffsetOnAxis(ap=sidx[:, j:j + 1], axis=0),
                                          in_=ybuf[:, X, j, :], in_offset=None, bounds_check=N - 1, oob_is_err=False,
                                          compute_op=ALU.add).then_inc(u_sc, 16)

            for v in range(4):
                gather(v, v % 2)
            scatter(0, 0)
            gather(4, 0)
            scatter(1, 1)
            gather(5, 1)
            with gp.Fori(3, UMIN // 2) as pair:
                for X in range(2):
                    scatter(2 * pair - 4 + X, X)
                    gather(2 * pair + X, X)
            for v in (UMIN - 1, UMIN):
                scatter(v - 4, v % 2)
                gather(v, v % 2)
            many = gp.value_load(used[0:1, 0:1], min_val=UMIN, max_val=UMAX)
            for v in range(UMIN + 1, UMIN + 4):
                scatter(v - 4, v % 2)
                with gp.If(many > v - 1):
                    gather(v, v % 2)
            gp.wait_ge(u_sc, 16 * UT * UMIN)
            for v in range(UMIN, UMAX):
                with gp.If(many > v):
                    scatter(v, v % 2)
                    if v + 4 < UMAX:
                        with gp.If(many > v + 3):
                            gather(v + 4, v % 2)
                    gp.wait_ge(u_sc, 16 * UT * (v + 1))

        @block2.scalar
        def _(act):
            act.wait_ge(t_bnv, 1)
            nc.scalar.activation(bnr[:], mvb[:, :, 1], ACT.Sqrt, bias=eps1[:]).then_inc(t_bns, 1)
            act.wait_ge(t_bn, 1)

            def width(g):
                return GN if g < NG else TAILN

            def relu_bn(g):
                for m in range(DH):
                    at = agg[:, m * NPAD + GN * g:m * NPAD + GN * g + width(g)]
                    nc.scalar.activation(at, at, ACT.Relu, bias=bnb[:, m:m + 1], scale=bna[:, m:m + 1]).then_inc(t_relu, 1)

            relu_bn(0)
            relu_bn(1)
            for g in range(GROUPS + 3):
                if g + 2 < GROUPS:
                    relu_bn(g + 2)
                if 1 <= g <= GROUPS:
                    q = g - 1
                    act.wait_ge(t_v2, q + 1)
                    if q >= 2:
                        act.wait_ge(t_ft, q - 1)
                        act.wait_ge(t_fd[q % 2], 16 * (q // 2))
                    for j in range(tiles_of(q)):
                        t = 4 * q + j
                        last = nc.scalar.activation(ftok[:, q % 2, j, :], xx[:, t, :], ACT.Identity, bias=nm2[:, t:t + 1], scale=rstd2[:, t:t + 1])
                    last.then_inc(t_f, 1)
                if 2 <= g <= GROUPS + 1:
                    q = g - 2
                    act.wait_ge(t_ft, q + 1)
                    for m in range(DH):
                        nc.scalar.activation(fparts[q % 2][0][:, m, 0:width(q)], bank[3 + m][:, 0:width(q)], ACT.Copy).then_inc(t_fh, 1)
                if g >= 3:
                    q = g - 3
                    act.wait_ge(t_rh, q + 1)
                    if q >= 2:
                        act.wait_ge(t_lg, q - 1)
                    nc.scalar.activation(r1[:, q % 2, 0:width(q)], bank[5 + q % 2][:, 0:width(q)], ACT.Relu, bias=rb1T[:, 0:1]).then_inc(t_rhs, 1)
                if g < GROUPS:
                    ts = slice(4 * g, 4 * g + tiles_of(g))
                    act.wait_ge(t_var2, g + 1)
                    nc.scalar.activation(rstd2[:, ts], mv2[:, ts, 1], ACT.Sqrt, bias=eps1[:]).then_inc(t_s2, 1)
            nc.scalar.activation(warm[:], eps1[:], ACT.Exp)
            act.wait_ge(t_sub, 1)
            nc.scalar.activation(pr[:], lg[:], ACT.Exp).then_inc(t_exp, 1)
            act.wait_ge(t_dm, 1)
            nc.scalar.activation(e2[:], m2[:], ACT.Exp).then_inc(t_e2, 1)
            for i in range(2 * NT // MB):
                at = slice(MB * i, MB * i + MB)
                act.wait_ge(t_eq, i + 1)
                nc.scalar.activation(slot_hi[:, at, 1, :], slot_eq[:, at, :], ACT.Copy, scale=lane_no[:, 0:1]).then_inc(t_lane, 1)

            def first_weights(u, X):
                e = act.value_load(expert_of[0:1, bass.ds(u, 1)], min_val=0, max_val=NEXP - 1)
                if after(u, 2):
                    act.wait_ge(u_r[1], 2 * u - 2)
                act.sem_inc(t_act, 1)
                nc.scalar.activation(b12u[:, X], b12T[:, bass.ds(e, 1)].rearrange("p o l m -> p (o l) m"), ACT.Copy).then_inc(u_w12h, 1)
                nc.scalar.activation(w12h[:, X], wraw12[:, bass.ds(e, 1)].rearrange("p o l k n -> p (o l) k n"), ACT.Copy).then_inc(u_w12h, 1)
                return e

            def last_weights(u, X, e):
                if after(u, 2):
                    act.wait_ge(u_l3, 2 * u - 2)
                act.sem_inc(t_act, 1)
                nc.scalar.activation(w3h[:, X], wraw3[:, bass.ds(e, 1)].rearrange("p o k n -> p (o k) n"), ACT.Copy).then_inc(u_w3h, 1)

            def high_part(u):
                for m in range(DH):
                    act.wait_ge(u_T, 2 * u + m + 1)
                    nc.scalar.activation(fuh[:, m, 0:UN], bank[m][:, 0:UN], ACT.Copy).then_inc(u_fh, 1)

            def relu_parts(u, X, layer):
                for m in range(DH):
                    act.wait_ge(u_l[layer], 2 * u + m + 1)
                    src_, b = bank[2 + 2 * layer + m][:, 0:UN], b12u[:, X, layer, m:m + 1]
                    nc.scalar.activation(rb_[layer][:, m, 0:UN], src_, ACT.Relu, bias=b)
                    nc.scalar.activation(hb[layer][0][:, m, 0:UN], src_, ACT.Relu, bias=b).then_inc(u_r[layer], 1)

            def next_unit(u, X):
                e = first_weights(u, X)
                high_part(u)
                last_weights(u, X, e)

            def act_step(u, X):
                act.wait_ge(u_w12h, 2 * u + 1)
                relu_parts(u, X, 0)
                if not isinstance(u, int) or u < UMAX - 1:
                    next_unit(u + 1, 1 - X)
                relu_parts(u, X, 1)

            act.wait_ge(t_raw, 16 * NRAW)
            act.wait_ge(t_slots, 1)
            next_unit(0, 0)
            units_loop(act, act_step, lambda u, X: None)

        @block2.vector
        def _(dve):
            chain = [0]

            def link(ins):
                chain[0] += 1
                ins.then_inc(t_dve, 1)
                dve.wait_ge(t_dve, chain[0])

            for m in range(DH):
                last = nc.vector.bn_aggr(mvb[:, m, :], stats[:, m, :, :].rearrange("p a b -> p (a b)"))
            last.then_inc(t_bnv, 1)
            dve.wait_ge(t_gb, 32)
            dve.wait_ge(t_bns, 1)
            link(nc.vector.reciprocal(bnr[:], bnr[:]))
            link(nc.vector.tensor_tensor(bna[:], bnr[:], gammaT[:], ALU.mult))
            link(nc.vector.tensor_tensor(bnr[:], mvb[:, :, 0], bna[:], ALU.mult))
            nc.vector.tensor_tensor(bnb[:], betaT[:], bnr[:], ALU.subtract).then_inc(t_bn, 1)
            for g in range(GROUPS + 3):
                if g >= 3:
                    q = g - 3
                    cols = GN if q < NG else TAILN
                    for m in range(DH):
                        dve.wait_ge(t_fh, 2 * q + m + 1)
                        hi, lo = fparts[q % 2]
                        nc.vector.tensor_tensor(lo[:, m, 0:cols], bank[3 + m][:, 0:cols], hi[:, m, 0:cols].bitcast(fp32), ALU.subtract).then_inc(t_fl, 1)
                if 1 <= g <= GROUPS:
                    dve.wait_ge(t_s2, g)
                    ts = slice(4 * (g - 1), 4 * (g - 1) + tiles_of(g - 1))
                    link(nc.vector.reciprocal(rstd2[:, ts], rstd2[:, ts]))
                    nc.vector.scalar_tensor_tensor(nm2[:, ts], mv2[:, ts, 0], -1.0, rstd2[:, ts], ALU.mult, ALU.mult).then_inc(t_v2, 1)
                if g < GROUPS:
                    for j in range(tiles_of(g)):
                        t, r = 4 * g + j, rows_of(4 * g + j)
                        dve.wait_ge(t_tr, min(NT, t - t % 2 + 2))
                        src_ = bank[t // 2 % 3][0:r, D * (t % 2):D * (t % 2) + D]
                        nc.vector.tensor_tensor(xx[0:r, t, :], xx[0:r, t, :], src_, ALU.add).then_inc(t_x1, 1)
                        if j >= 1:
                            dve.wait_ge(t_x1, t)
                            nc.vector.bn_stats(st6b[:, t - 1, :], xx[:, t - 1, :])
                    dve.wait_ge(t_x1, t + 1)
                    link(nc.vector.bn_stats(st6b[:, t, :], xx[:, t, :]))
                    for j in range(tiles_of(g)):
                        last = nc.vector.bn_aggr(mv2[:, 4 * g + j, :], st6b[:, 4 * g + j, :])
                    last.then_inc(t_var2, 1)
            bc = [P, NT, NEXP]
            dve.wait_ge(t_tab, 1)
            nc.vector.tensor_copy(rank[:], rank_i[:])
            nc.vector.tensor_copy(lane[:], lane_i[:])
            nc.vector.tensor_scalar(earlier[:], order_i[:], 0.0, None, ALU.is_gt)
            nc.vector.memset(ones2[:], 1.0)
            for buf in run:
                nc.vector.memset(buf[:, 0:SH, :], 0.0)
            for buf in ends:
                nc.vector.memset(buf[:, 0:4], 0.0)
            nc.vector.tensor_copy(lane_h[:], lane_i[:])
            nc.vector.tensor_copy(steps[:], steps_i[:])
            nc.vector.tensor_copy(tile_no[:], tile_i[:])
            link(nc.vector.tensor_copy(token[:], token_i[:]))
            nc.vector.tensor_scalar(lane_no[:], token[:, 0:1], -1.0, None, ALU.add)
            link(nc.vector.tensor_scalar(here[:], token[:], float(N), None, ALU.is_le))
            link(nc.vector.tensor_scalar(away[:], here[:], 1.0, float(2 * SC), ALU.subtract, ALU.mult))
            dve.wait_ge(t_w, 16 * 4)
            nc.vector.memset(lg[:], 0.0)
            dve.wait_ge(t_lg, GROUPS)
            link(nc.vector.memset(pr[:], 0.0))
            logits = bank[7][:, 0:NT * 8].rearrange("p (t e) -> p t e", e=8)[:, :, 0:NEXP]
            rb = rb2b[:].unsqueeze(1)
            nc.vector.tensor_tensor(lg[:, 0:FULL, :], logits[:, 0:FULL, :], rb.to_broadcast([P, FULL, NEXP]), ALU.add)
            link(nc.vector.tensor_tensor(lg[0:TAILN, FULL:NT, :], logits[0:TAILN, FULL:NT, :], rb[0:TAILN].to_broadcast([TAILN, 1, NEXP]), ALU.add))
            link(nc.vector.reduce_max(m1[:], lg[:], AX.X))
            nc.vector.tensor_tensor(lg[:], lg[:], m1[:].unsqueeze(2).to_broadcast(bc), ALU.subtract).then_inc(t_sub, 1)
            dve.wait_ge(t_exp, 1)
            link(nc.vector.reduce_sum(m2[:], pr[:], AX.X))
            link(nc.vector.reciprocal(m2[:], m2[:]))
            link(nc.vector.tensor_tensor(pr[:], pr[:], m2[:].unsqueeze(2).to_broadcast(bc), ALU.mult))

            def pick(top, chosen):
                link(nc.vector.reduce_max(top[:], pr[:], AX.X))
                link(nc.vector.tensor_tensor(eq[:], pr[:], top[:].unsqueeze(2).to_broadcast(bc), ALU.is_equal))
                link(nc.vector.tensor_tensor(eq[:], eq[:], rank[:].unsqueeze(1).to_broadcast(bc), ALU.mult))
                link(nc.vector.reduce_max(mk[:], eq[:], AX.X))
                link(nc.vector.tensor_tensor(chosen[:], eq[:], mk[:].unsqueeze(2).to_broadcast(bc), ALU.is_equal))

            pick(m1, f1)
            link(nc.vector.scalar_tensor_tensor(pr[:], f1[:], -2.0, pr[:], ALU.mult, ALU.add))
            pick(m2, f2)
            nc.vector.tensor_tensor(m2[:], m2[:], m1[:], ALU.subtract).then_inc(t_dm, 1)
            link(nc.vector.tensor_tensor(chosen[:], f1[:], f2[:], ALU.add))
            link(nc.vector.tensor_tensor(chosen[:], chosen[:], here[:].unsqueeze(2).to_broadcast(bc), ALU.mult))
            src_, shift, turn = chosen[:], 1, 0
            link(nc.vector.tensor_copy(run[1][:, SH:, :], chosen[:]))
            while shift < NT:
                a, b = run[1 - turn], run[turn]
                ins = nc.vector.tensor_tensor(b[:, SH:, :], a[:, SH:, :], a[:, SH - shift:SH - shift + NT, :], ALU.add)
                link(ins)
                shift, turn = 2 * shift, 1 - turn
            total = run[1 - turn]
            nc.vector.tensor_copy(base[:], total[:, SH + NT - 1, :]).then_inc(t_cho, 1)
            link(nc.vector.tensor_tensor(place[:], total[:, SH:, :], chosen[:], ALU.subtract))
            dve.wait_ge(t_pfx, 1)
            link(nc.vector.tensor_copy(tokens_of[:], bank[7][:, 8:8 + NEXP]))
            link(nc.vector.tensor_tensor(exceeded[:], tokens_of[:].unsqueeze(2).to_broadcast([P, NEXP, UNE]), steps[:].unsqueeze(1).to_broadcast([P, NEXP, UNE]), ALU.is_gt))
            link(nc.vector.reduce_sum(units[:], exceeded[:], AX.X))
            link(nc.vector.tensor_copy(ends[0][:, 4:], units[:]))
            for i, shift in enumerate((1, 2, 4)):
                a, b = ends[i % 2], ends[1 - i % 2]
                link(nc.vector.tensor_tensor(b[:, 4:], a[:, 4:], a[:, 4 - shift:4 - shift + NEXP], ALU.add))
            end = ends[1][:, 4:]
            link(nc.vector.tensor_tensor(units[:], end, units[:], ALU.subtract))
            link(nc.vector.scalar_tensor_tensor(base[:], units[:], float(UN), bank[7][:, 0:NEXP], ALU.mult, ALU.add))
            link(nc.vector.tensor_tensor(place[:], place[:], base[:].unsqueeze(1).to_broadcast(bc), ALU.add))
            link(nc.vector.tensor_tensor(eq2[:], f12[:], place[:].unsqueeze(1).to_broadcast([P, 2, NT, NEXP]), ALU.mult))
            link(nc.vector.reduce_sum(pos[:], eq2[:], AX.X))
            link(nc.vector.tensor_copy(pos_i[:], pos[:]))
            nc.vector.tensor_scalar(plo_i[:], pos_i[:], P - 1, None, ALU.bitwise_and)
            link(nc.vector.tensor_scalar(phi_i[:], pos_i[:], 7, None, ALU.logical_shift_right))
            nc.vector.tensor_copy(plo[:], plo_i[:])
            link(nc.vector.tensor_copy(phi[:], phi_i[:]))
            link(nc.vector.tensor_tensor(phi[:], phi[:], away[:].unsqueeze(1).to_broadcast([P, 2, NT]), ALU.add))
            dve.wait_ge(t_init, 32)
            flat = [b[:].rearrange("p k t -> p (k t)") for b in (plo, phi)]
            for i in range(2 * NT // MB):
                at = slice(MB * i, MB * i + MB)
                lo_, hi_ = (f[:, at].unsqueeze(2) for f in flat)
                nc.vector.tensor_tensor(slot_eq[:, at, :], lane_h[:, 0:SC].unsqueeze(1).to_broadcast([P, MB, SC]), hi_.to_broadcast([P, MB, SC]), ALU.is_equal).then_inc(t_eq, 1)
                nc.vector.tensor_tensor(slot_lo[:, at, :], lane_h[:].unsqueeze(1).to_broadcast([P, MB, P]), lo_.to_broadcast([P, MB, P]), ALU.is_equal).then_inc(t_moh, 1)
            dve.wait_ge(t_e2, 1)
            link(nc.vector.tensor_scalar(g1[:], e2[:], 1.0, None, ALU.add))
            link(nc.vector.reciprocal(g1[:], g1[:]))
            link(nc.vector.tensor_tensor(g2[:], e2[:], g1[:], ALU.mult))
            nc.vector.tensor_tensor(g12[:], f1[:], g1[:].unsqueeze(2).to_broadcast(bc), ALU.mult)
            link(nc.vector.tensor_tensor(gate[:], f2[:], g2[:].unsqueeze(2).to_broadcast(bc), ALU.mult))
            nc.vector.tensor_tensor(gate[:], gate[:], g12[:], ALU.add).then_inc(t_gate, 1)
            link(nc.vector.tensor_tensor(past[:], lane[:, 0:UMAX].unsqueeze(2).to_broadcast([P, UMAX, NEXP]),
                                         end.unsqueeze(1).to_broadcast([P, UMAX, NEXP]), ALU.is_ge))
            nc.vector.tensor_copy(used[:], end[:, NEXP - 1:NEXP])
            link(nc.vector.reduce_sum(of_unit[:], past[:], AX.X))
            link(nc.vector.tensor_scalar(expert_of[:], of_unit[:], float(NEXP - 1), None, ALU.min))
            link(nc.vector.tensor_scalar(beyond[:], token[:, 0:1], float(N + P), None, ALU.add))
            dve.wait_ge(t_prod, 1)
            tiles_, lanes_ = bank[6][:, 0:SC], bank[6][:, SC:2 * SC]
            link(nc.vector.tensor_copy(found[:], lanes_))
            link(nc.vector.scalar_tensor_tensor(found[:], tiles_, float(P), found[:], ALU.mult, ALU.add))
            nc.vector.tensor_scalar(gidx_all[:], found[:], -float(P), 0.0, ALU.add, ALU.max)
            link(nc.vector.tensor_scalar(empty[:], tiles_, 0.5, beyond[:, 0:1], ALU.is_lt, ALU.mult))
            nc.vector.scalar_tensor_tensor(sidx_all[:], found[:], -float(P), empty[:], ALU.add, ALU.add).then_inc(t_slots, 1)
            dve.wait_ge(t_slots, 1)
            dve.wait_ge(t_raw, 16 * NRAW)

            def next_unit(u, X):
                e = dve.value_load(expert_of[0:1, bass.ds(u, 1)], min_val=0, max_val=NEXP - 1)
                dve.wait_ge(u_w12h, 2 * u + 2)
                nc.vector.tensor_tensor(w12l[:, X], wraw12[:, bass.ds(e, 1)].rearrange("p o l k n -> p (o l) k n"), w12h[:, X].bitcast(fp32),
                                        ALU.subtract).then_inc(u_w12, 1)
                dve.wait_ge(u_T, 2 * u + 1)
                nc.vector.tensor_copy(sgate[:, bass.ds(UT * u, UT)].unsqueeze(2), frows[:, X, :, bass.ds(D + e, 1)]).then_inc(u_fc, 1)
                for m in range(DH):
                    dve.wait_ge(u_fh, 2 * u + m + 1)
                    nc.vector.tensor_tensor(ful[:, m, 0:UN], bank[m][:, 0:UN], fuh[:, m, 0:UN].bitcast(fp32), ALU.subtract).then_inc(u_fl, 1)
                return e

            def last_weights(u, X, e):
                dve.wait_ge(u_w3h, u + 1)
                nc.vector.tensor_tensor(w3l[:, X], wraw3[:, bass.ds(e, 1)].rearrange("p o k n -> p (o k) n"), w3h[:, X].bitcast(fp32),
                                        ALU.subtract).then_inc(u_w3, 1)

            def low_part(u, X, layer):
                for m in range(DH):
                    dve.wait_ge(u_r[layer], 2 * u + m + 1)
                    nc.vector.tensor_tensor(hb[layer][1][:, m, 0:UN], rb_[layer][:, m, 0:UN], hb[layer][0][:, m, 0:UN].bitcast(fp32),
                                            ALU.subtract).then_inc(u_h[layer], 1)

            def outputs(u, X):
                e = dve.value_load(expert_of[0:1, bass.ds(u, 1)], min_val=0, max_val=NEXP - 1)
                if after(u, 2):
                    dve.wait_ge(u_sc, 16 * UT * (u - 1))
                for h in range(2):
                    dve.wait_ge(u_l3, 2 * u + h + 1)
                    n = min(2, UT - 2 * h)
                    nc.vector.tensor_tensor(ybuf[:, X, 2 * h:2 * h + n, :], bank[6 + h][:, 0:n * D].rearrange("p (j n) -> p j n", j=n),
                                            b3b[:, bass.ds(e, 1), :].to_broadcast([P, n, D]), ALU.add).then_inc(u_ys, 1)
                dve.wait_ge(u_fc, u + 1)
                for j in range(UT):
                    if j % 2 == 0:
                        dve.wait_ge(u_ys, 2 * u + j // 2 + 1)
                    nc.vector.tensor_scalar(ybuf[:, X, j, :], ybuf[:, X, j, :], sgate[:, bass.ds(UT * u + j, 1)], None, ALU.mult).then_inc(u_y, 1)

            def dve_step(u, X):
                low_part(u, X, 0)
                more = not isinstance(u, int) or u < UMAX - 1
                if more:
                    e = next_unit(u + 1, 1 - X)
                if after(u, 1):
                    outputs(u - 1, 1 - X)
                low_part(u, X, 1)
                if more:
                    last_weights(u + 1, 1 - X, e)

            last_weights(0, 0, next_unit(0, 0))
            units_loop(dve, dve_step, outputs)

        @block2.tensor
        def _(pe):
            for g in range(GROUPS + 4):
                if g < GROUPS:
                    pe.wait_ge(t_relu, 2 * g + 2)
                    for j in range(tiles_of(g)):
                        t, r = 4 * g + j, rows_of(4 * g + j)
                        if t % 2 == 0 and t >= 6:
                            pe.wait_ge(t_x1, t - 4)
                        for m in range(DH):
                            last = nc.tensor.transpose(bank[t // 2 % 3][0:r, D * (t % 2) + P * m:D * (t % 2) + P * m + P],
                                                       agg[:, m * NPAD + P * t:m * NPAD + P * t + r], identf[:])
                        last.then_inc(t_tr, 1)
                if 2 <= g <= GROUPS + 1:
                    q = g - 2
                    pe.wait_ge(t_f, q + 1)
                    if q >= 1:
                        pe.wait_ge(t_fl, 2 * q)
                    for m in range(DH):
                        for j in range(tiles_of(q)):
                            r = rows_of(4 * q + j)
                            last = nc.tensor.transpose(bank[3 + m][:, P * j:P * j + r], ftok[0:r, q % 2, j, P * m:P * m + P], identf[0:r, 0:r])
                    last.then_inc(t_ft, 1)
                if 3 <= g <= GROUPS + 2:
                    q, cols = g - 3, GN if g - 3 < NG else TAILN
                    hi, lo = fparts[q % 2]
                    pe.wait_ge(t_fl, 2 * q + 2)
                    if q == 0:
                        pe.wait_ge(t_rw, 2)
                    if q >= 2:
                        pe.wait_ge(t_rhs, q - 1)
                    three(bank[5 + q % 2][:, 0:cols], [((rw1h[:, k, :], rw1l[:, k, :]), (hi[:, k, 0:cols], lo[:, k, 0:cols])) for k in range(DH)]).then_inc(t_rh, 1)
                if g >= 4:
                    q = g - 4
                    pe.wait_ge(t_rhs, q + 1)
                    for j in range(tiles_of(q)):
                        t = 4 * q + j
                        r = rows_of(t)
                        last = nc.tensor.matmul(bank[7][0:r, 8 * t:8 * t + NEXP], r1[:, q % 2, P * j:P * j + r], rw2s[:], start=True, stop=True)
                    last.then_inc(t_lg, 1)
            pe.wait_ge(t_cho, 1)
            nc.tensor.matmul(bank[7][:, 0:NEXP], earlier[:], base[:], start=True, stop=True)
            nc.tensor.matmul(bank[7][:, 8:8 + NEXP], ones2[:], base[:], start=True, stop=True).then_inc(t_pfx, 1)
            for i in range(2 * NT):
                if i % MB == 0:
                    pe.wait_ge(t_moh, i // MB + 1)
                    pe.wait_ge(t_tile, i // MB + 1)
                    pe.wait_ge(t_lane, i // MB + 1)
                last = nc.tensor.matmul(bank[6][:, 0:2 * SC], slot_lo[:, i, :], slot_hi[:, i, :, :].rearrange("p h n -> p (h n)"), start=i == 0, stop=i == 2 * NT - 1)
            last.then_inc(t_prod, 1)

            def rows_unit(u, X, round_):
                pe.wait_ge(u_g[X], 16 * UT * (round_ + 1))
                for m in range(DH):
                    for j in range(UT):
                        last = nc.tensor.transpose(bank[m][:, P * j:P * j + P], frows[:, X, j, P * m:P * m + P], identf[:])
                    last.then_inc(u_T, 1)

            def layer_unit(u, X, layer):
                fhl = (fuh, ful) if layer == 0 else (h1h, h1l)
                for m in range(DH):
                    cs = slice(P * m, P * m + P)
                    three(bank[2 + 2 * layer + m][:, 0:UN], [((w12h[:, X, layer, k, cs], w12l[:, X, layer, k, cs]), (fhl[0][:, k, 0:UN], fhl[1][:, k, 0:UN]))
                                                       for k in range(DH)]).then_inc(u_l[layer], 1)

            def out_unit(u, X):
                pe.wait_ge(u_h[1], 2 * u + 2)
                pe.wait_ge(u_w3, u + 1)
                if after(u, 1):
                    pe.wait_ge(u_ys, 2 * u)
                for h in range(2):
                    for j in range(2 * h, min(2 * h + 2, UT)):
                        last = three(bank[6 + h][:, D * (j % 2):D * (j % 2) + D],
                                     [((h2h[:, k, P * j:P * j + P], h2l[:, k, P * j:P * j + P]), (w3h[:, X, k, :], w3l[:, X, k, :])) for k in range(DH)])
                    last.then_inc(u_l3, 1)

            def pe_step(u, X):
                pe.wait_ge(u_w12, u + 1)
                pe.wait_ge(u_fl, 2 * u + 2)
                layer_unit(u, X, 0)
                if not isinstance(u, int) or u < UMAX - 1:
                    rows_unit(u + 1, 1 - X, (u + 1) // 2)
                if after(u, 1):
                    out_unit(u - 1, 1 - X)
                pe.wait_ge(u_h[0], 2 * u + 2)
                layer_unit(u, X, 1)

            rows_unit(0, 0, 0)
            units_loop(pe, pe_step, out_unit)

        ctx2.close()


_INS = ["x", "src", "dst", "L0_gnn_W", "L0_gnn_bias", "L0_gnn_gamma", "L0_gnn_beta",
        "L0_ffn_router_w1", "L0_ffn_router_b1", "L0_ffn_router_w2", "L0_ffn_router_b2",
        "L0_ffn_expert_w1", "L0_ffn_expert_b1", "L0_ffn_expert_w2", "L0_ffn_expert_b2",
        "L0_ffn_expert_w3", "L0_ffn_expert_b3"]


def kernel(**inputs):
    import numpy as _np
    import concourse.bacc as _bacc
    from concourse import mybir as _mybir
    from concourse.bass_utils import run_bass_kernel_spmd as _run

    nc = _bacc.Bacc("TRN2", target_bir_lowering=False, num_devices=1)
    arrays, args = {}, []
    for name in _INS:
        a = _np.ascontiguousarray(inputs[name])
        arrays[f"in_{name}"] = a
        args.append(nc.dram_tensor(f"in_{name}", a.shape, _mybir.dt.from_np(a.dtype), kind="ExternalInput").ap())
    args.append(nc.dram_tensor("out_0", [N, D], fp32, kind="ExternalOutput").ap())
    build(nc, *args)
    r = _run(nc, [arrays], core_ids=[0])
    return r.results[0]["out_0"]
```
